# Optimizing a Trainium2 kernel written in Bass

```python
import numpy as np
import jax
import jax.numpy as jnp

def _softmax(x, axis=-1):
    return jax.nn.softmax(x, axis=axis)
def _gelu(x):
    return jax.nn.gelu(x, approximate=True)
def _silu(x):
    return jax.nn.silu(x)
def _sigmoid(x):
    return jax.nn.sigmoid(x)
def _layernorm(x, axis=-1, eps=1e-5):
    m = jnp.mean(x, axis=axis, keepdims=True)
    v = jnp.var(x, axis=axis, keepdims=True)
    return (x - m) / jnp.sqrt(v + eps)
def _scatter_add(tgt, idx, src, axis=0):
    return tgt.at[idx].add(src)
def _segment_sum(src, seg, n):
    return jax.ops.segment_sum(src, seg, n)

kernel_name = 'mk_adj_resnorm_d4_adj_256_e5f05c'

def setup_inputs(seed: int = 0):
    np.random.seed(seed)
    _w = jnp.asarray
    def _rec_inputs():
        import jax
        import jax.numpy as jnp
        _gk = jax.random.key(seed)
        x = -0.0003929 + 0.9999 * jax.random.normal(jax.random.fold_in(_gk, 1), (128, 64, 256), jnp.float32)
        _w = (1.0 + jnp.arange(64, dtype=jnp.float32)) ** -0.5
        _w = _w / _w.mean()
        _pij = jnp.clip(0.0625 * _w[:, None] * _w[None, :], 0.0, 1.0)
        _a = jax.random.uniform(jax.random.fold_in(_gk, 2), (64, 64)) < _pij
        _a = jnp.logical_or(_a, jnp.swapaxes(_a, -1, -2))
        _a = jnp.logical_or(_a, jnp.eye(64, dtype=bool))
        _af = _a.astype(jnp.float32)
        _d = jnp.maximum(_af.sum(-1), 1.0) ** -0.5
        _af = _af * _d[..., :, None] * _d[..., None, :]
        adj = _af
        return x, adj
    x, adj = _rec_inputs()
    def _L0_gnn_setup():
        import jax, jax.numpy as jnp
        import numpy as np
        B, N, D_IN, HID, D_OUT = (64, 1024, 256, 128, 256)
        key = jax.random.key(seed)
        kf, ka, kw1, kw2 = jax.random.split(key, 4)
        features = jax.random.normal(kf, (B, N, D_IN), dtype=jnp.float32)
        A = jax.random.uniform(ka, (N, N), dtype=jnp.float32)
        A = 0.5 * (A + A.T)
        lim1 = float(np.sqrt(6.0 / (D_IN + HID)))
        lim2 = float(np.sqrt(6.0 / (HID + D_OUT)))
        W1 = jax.random.uniform(kw1, (D_IN, HID), minval=-lim1, maxval=lim1, dtype=jnp.float32)
        b1 = jnp.zeros((HID,), jnp.float32)
        W2 = jax.random.uniform(kw2, (HID, D_OUT), minval=-lim2, maxval=lim2, dtype=jnp.float32)
        b2 = jnp.zeros((D_OUT,), jnp.float32)
        return {'features': features, 'A': A, 'W1': W1, 'b1': b1, 'W2': W2, 'b2': b2}
    _L0_gnn_all = _L0_gnn_setup()
    _L0_gnn_in = {k: v for k, v in _L0_gnn_all.items() if k in ('W1', 'b1', 'W2', 'b2', )}
    del _L0_gnn_all

    def _L1_gnn_setup():
        import jax, jax.numpy as jnp
        import numpy as np
        EPS = 1e-05

        def _batchnorm(x, gamma, beta):
            mu = jnp.mean(x, axis=0)
            var = jnp.var(x, axis=0)
            return (x - mu) * jax.lax.rsqrt(var + EPS) * gamma + beta
        key = jax.random.key(seed)
        ks = jax.random.split(key, 4)
        b, n, d, h, o = (32, 2048, 256, 512, 256)
        features = jax.random.normal(ks[0], (b, n, d), dtype=jnp.float32)
        A = jax.random.uniform(ks[1], (n, n), dtype=jnp.float32)
        lim1 = float(np.sqrt(6.0 / (d + h)))
        W1 = jax.random.uniform(ks[2], (h, d), minval=-lim1, maxval=lim1, dtype=jnp.float32)
        b1 = jnp.zeros((h,), jnp.float32)
        lim2 = float(np.sqrt(6.0 / (h + o)))
        W2 = jax.random.uniform(ks[3], (o, h), minval=-lim2, maxval=lim2, dtype=jnp.float32)
        b2 = jnp.zeros((o,), jnp.float32)
        g1 = jnp.ones((h,), jnp.float32)
        be1 = jnp.zeros((h,), jnp.float32)
        g2 = jnp.ones((o,), jnp.float32)
        be2 = jnp.zeros((o,), jnp.float32)
        return {'features': features, 'A': A, 'W1': W1, 'b1': b1, 'g1': g1, 'be1': be1, 'W2': W2, 'b2': b2, 'g2': g2, 'be2': be2}
    _L1_gnn_all = _L1_gnn_setup()
    _L1_gnn_in = {k: v for k, v in _L1_gnn_all.items() if k in ('W1', 'b1', 'g1', 'be1', 'W2', 'b2', 'g2', 'be2', )}
    del _L1_gnn_all

    def _L2_gnn_setup():
        import jax, jax.numpy as jnp
        import numpy as np
        BT, N, D, HEADS, E = (1024, 64, 256, 4, 512)
        LRELU_SLOPE = 0.2
        EPS = 1e-08
        key = jax.random.key(seed)
        ks = jax.random.split(key, 8)
        d = D
        return {'H': jax.random.normal(ks[0], (BT, N, d), jnp.float32), 'W_lin': jax.random.normal(ks[1], (d, d), jnp.float32) / np.sqrt(d).astype(np.float32), 'W_val': jax.random.normal(ks[2], (d, d), jnp.float32) / np.sqrt(d).astype(np.float32), 'a': jax.random.normal(ks[3], (HEADS, d // HEADS), jnp.float32), 'W_out': jax.random.normal(ks[4], (d, d), jnp.float32) / np.sqrt(d).astype(np.float32), 'A0': jax.random.uniform(ks[5], (N, N), jnp.float32), 'src': jax.random.randint(ks[6], (E,), 0, N, jnp.int32), 'dst': jax.random.randint(ks[7], (E,), 0, N, jnp.int32)}
    _L2_gnn_all = _L2_gnn_setup()
    _L2_gnn_in = {k: v for k, v in _L2_gnn_all.items() if k in ('W_lin', 'W_val', 'a', 'W_out', 'src', 'dst', )}
    del _L2_gnn_all

    def _L3_gnn_setup():
        import jax, jax.numpy as jnp
        import numpy as np
        B, T, D, H = (64, 2048, 256, 256)
        MAX_SKIP = 4

        def _lstm_last(Wih, Whh, bih, bhh, xs):
            N, _, Hd = xs.shape
            bias = bih + bhh

            def step(carry, x_t):
                h, c = carry
                g = x_t @ Wih.T + h @ Whh.T + bias
                i, f, gg, o = jnp.split(g, 4, axis=-1)
                c = jax.nn.sigmoid(f) * c + jax.nn.sigmoid(i) * jnp.tanh(gg)
                h = jax.nn.sigmoid(o) * jnp.tanh(c)
                return ((h, c), None)
            init = (jnp.zeros((N, Hd), xs.dtype), jnp.zeros((N, Hd), xs.dtype))
            (h_last, _), _ = jax.lax.scan(step, init, jnp.swapaxes(xs, 0, 1))
            return h_last
        key = jax.random.key(seed)
        ks = jax.random.split(key, 8)
        s = 0.05
        x = jax.random.normal(ks[0], (B, T, D), jnp.float32)
        adj = jax.random.uniform(ks[1], (T, T), jnp.float32) / T
        Wg0 = jax.random.normal(ks[2], (D, H), jnp.float32) * s
        bg0 = jnp.zeros((H,), jnp.float32)
        Wg1 = jax.random.normal(ks[3], (H, H), jnp.float32) * s
        bg1 = jnp.zeros((H,), jnp.float32)
        Wih = jax.random.normal(ks[4], (MAX_SKIP, 4 * H, H), jnp.float32) * s
        Whh = jax.random.normal(ks[5], (MAX_SKIP, 4 * H, H), jnp.float32) * s
        bih = jax.random.normal(ks[6], (MAX_SKIP, 4 * H), jnp.float32) * s
        bhh = jax.random.normal(ks[7], (MAX_SKIP, 4 * H), jnp.float32) * s
        return dict(x=x, adj=adj, Wg0=Wg0, bg0=bg0, Wg1=Wg1, bg1=bg1, Wih=Wih, Whh=Whh, bih=bih, bhh=bhh)
    _L3_gnn_all = _L3_gnn_setup()
    _L3_gnn_in = {k: v for k, v in _L3_gnn_all.items() if k in ('Wg0', 'bg0', 'Wg1', 'bg1', 'Wih', 'Whh', 'bih', 'bhh', )}
    del _L3_gnn_all

    return {
        "x": x,
        "adj": adj,
        "L0_gnn_W1": _L0_gnn_in["W1"],
        "L0_gnn_b1": _L0_gnn_in["b1"],
        "L0_gnn_W2": _L0_gnn_in["W2"],
        "L0_gnn_b2": _L0_gnn_in["b2"],
        "L1_gnn_W1": _L1_gnn_in["W1"],
        "L1_gnn_b1": _L1_gnn_in["b1"],
        "L1_gnn_g1": _L1_gnn_in["g1"],
        "L1_gnn_be1": _L1_gnn_in["be1"],
        "L1_gnn_W2": _L1_gnn_in["W2"],
        "L1_gnn_b2": _L1_gnn_in["b2"],
        "L1_gnn_g2": _L1_gnn_in["g2"],
        "L1_gnn_be2": _L1_gnn_in["be2"],
        "L2_gnn_W_lin": _L2_gnn_in["W_lin"],
        "L2_gnn_W_val": _L2_gnn_in["W_val"],
        "L2_gnn_a": _L2_gnn_in["a"],
        "L2_gnn_W_out": _L2_gnn_in["W_out"],
        "L2_gnn_src": _L2_gnn_in["src"],
        "L2_gnn_dst": _L2_gnn_in["dst"],
        "L3_gnn_Wg0": _L3_gnn_in["Wg0"],
        "L3_gnn_bg0": _L3_gnn_in["bg0"],
        "L3_gnn_Wg1": _L3_gnn_in["Wg1"],
        "L3_gnn_bg1": _L3_gnn_in["bg1"],
        "L3_gnn_Wih": _L3_gnn_in["Wih"],
        "L3_gnn_Whh": _L3_gnn_in["Whh"],
        "L3_gnn_bih": _L3_gnn_in["bih"],
        "L3_gnn_bhh": _L3_gnn_in["bhh"],
    }

def reference(x, adj, L0_gnn_W1, L0_gnn_b1, L0_gnn_W2, L0_gnn_b2, L1_gnn_W1, L1_gnn_b1, L1_gnn_g1, L1_gnn_be1, L1_gnn_W2, L1_gnn_b2, L1_gnn_g2, L1_gnn_be2, L2_gnn_W_lin, L2_gnn_W_val, L2_gnn_a, L2_gnn_W_out, L2_gnn_src, L2_gnn_dst, L3_gnn_Wg0, L3_gnn_bg0, L3_gnn_Wg1, L3_gnn_bg1, L3_gnn_Wih, L3_gnn_Whh, L3_gnn_bih, L3_gnn_bhh):
    import jax
    import jax.numpy as jnp
    def _L0_gnn_ref(features, A, W1, b1, W2, b2):
        import jax, jax.numpy as jnp
        import numpy as np
        B, N, D_IN, HID, D_OUT = (64, 1024, 256, 128, 256)
        deg = jnp.sum(A, axis=0) + jnp.sum(A, axis=1) - jnp.diagonal(A)
        d_inv_sqrt = jnp.where(deg > 0, jax.lax.rsqrt(deg), 0.0)
        L = jnp.diag(deg) - A
        L_norm = d_inv_sqrt[:, None] * L * d_inv_sqrt[None, :]
        _, U = jnp.linalg.eigh(L_norm)
        agg = jnp.einsum('mn,bnd->bmd', U.T, features)
        h = jax.nn.relu(agg @ W1 + b1)
        out = h @ W2 + b2
        return jnp.einsum('nm,bmd->bnd', U, out)

    def _L1_gnn_ref(features, A, W1, b1, g1, be1, W2, b2, g2, be2):
        import jax, jax.numpy as jnp
        import numpy as np
        EPS = 1e-05

        def _batchnorm(x, gamma, beta):
            mu = jnp.mean(x, axis=0)
            var = jnp.var(x, axis=0)
            return (x - mu) * jax.lax.rsqrt(var + EPS) * gamma + beta
        b, n, d = features.shape
        A_norm = A + jnp.eye(n, dtype=A.dtype)
        deg = jnp.sum(A_norm, axis=0) + jnp.sum(A_norm, axis=1) - jnp.diagonal(A_norm)
        dinv = jax.lax.rsqrt(deg)
        A_hat = A_norm * dinv[:, None] * dinv[None, :]
        agg = jnp.einsum('nm,bmd->bnd', A_hat, features)
        x = agg.reshape(-1, d)
        h = jax.nn.relu(_batchnorm(x @ W1.T + b1, g1, be1))
        out = h @ W2.T + b2
        out = _batchnorm(out, g2, be2)
        return out.reshape(b, n, -1)

    def _L2_gnn_ref(H, W_lin, W_val, a, W_out, A0, src, dst):
        import jax, jax.numpy as jnp
        import numpy as np
        BT, N, D, HEADS, E = (1024, 64, 256, 4, 512)
        LRELU_SLOPE = 0.2
        EPS = 1e-08
        bt, n, d = H.shape
        h, dh = a.shape
        Xq = (H @ W_lin.T).reshape(bt, n, h, dh)
        Xv = (H @ W_val.T).reshape(bt, n, h, dh)
        Qs = Xq[:, src]
        Kt = Xq[:, dst]
        e = jnp.einsum('behd,hd->beh', jax.nn.leaky_relu(Qs + Kt, LRELU_SLOPE), a)
        e = e + jnp.log(A0[src, dst] + EPS)[None, :, None]
        e_t = e.transpose(1, 0, 2)
        m = jax.ops.segment_max(e_t, src, num_segments=n)
        ex = jnp.exp(e_t - m[src])
        denom = jax.ops.segment_sum(ex, src, num_segments=n)
        attn = ex / denom[src]
        Vt = Xv[:, dst].transpose(1, 0, 2, 3)
        Y = jax.ops.segment_sum(attn[..., None] * Vt, src, num_segments=n)
        Y = Y.transpose(1, 0, 2, 3).reshape(bt, n, d)
        return Y @ W_out.T

    def _L3_gnn_ref(x, adj, Wg0, bg0, Wg1, bg1, Wih, Whh, bih, bhh):
        import jax, jax.numpy as jnp
        import numpy as np
        B, T, D, H = (64, 2048, 256, 256)
        MAX_SKIP = 4

        def _lstm_last(Wih, Whh, bih, bhh, xs):
            N, _, Hd = xs.shape
            bias = bih + bhh

            def step(carry, x_t):
                h, c = carry
                g = x_t @ Wih.T + h @ Whh.T + bias
                i, f, gg, o = jnp.split(g, 4, axis=-1)
                c = jax.nn.sigmoid(f) * c + jax.nn.sigmoid(i) * jnp.tanh(gg)
                h = jax.nn.sigmoid(o) * jnp.tanh(c)
                return ((h, c), None)
            init = (jnp.zeros((N, Hd), xs.dtype), jnp.zeros((N, Hd), xs.dtype))
            (h_last, _), _ = jax.lax.scan(step, init, jnp.swapaxes(xs, 0, 1))
            return h_last
        h = jax.nn.relu(jnp.einsum('ts,bsh->bth', adj, x @ Wg0 + bg0))
        h = jax.nn.relu(jnp.einsum('ts,bsh->bth', adj, h @ Wg1 + bg1))
        Bv, Tv, Hd = h.shape
        for p in range(1, MAX_SKIP + 1):
            nw = Tv // p
            wins = h[:, :nw * p, :].reshape(Bv * nw, p, Hd)
            last = _lstm_last(Wih[p - 1], Whh[p - 1], bih[p - 1], bhh[p - 1], wins)
            idx = jnp.arange(nw) * p + (p - 1)
            h = h.at[:, idx, :].set(last.reshape(Bv, nw, Hd))
        return h

    x = _layernorm(x + _L0_gnn_ref(x, adj, L0_gnn_W1, L0_gnn_b1, L0_gnn_W2, L0_gnn_b2), axis=-1)
    x = _layernorm(x + _L1_gnn_ref(x, adj, L1_gnn_W1, L1_gnn_b1, L1_gnn_g1, L1_gnn_be1, L1_gnn_W2, L1_gnn_b2, L1_gnn_g2, L1_gnn_be2), axis=-1)
    x = _layernorm(x + _L2_gnn_ref(x, L2_gnn_W_lin, L2_gnn_W_val, L2_gnn_a, L2_gnn_W_out, adj, L2_gnn_src, L2_gnn_dst), axis=-1)
    x = _layernorm(x + _L3_gnn_ref(x, adj, L3_gnn_Wg0, L3_gnn_bg0, L3_gnn_Wg1, L3_gnn_bg1, L3_gnn_Wih, L3_gnn_Whh, L3_gnn_bih, L3_gnn_bhh), axis=-1)
    return x


_drawn_inputs = setup_inputs


def setup_inputs(seed=0):
    import zlib

    import numpy as np

    out = dict(_drawn_inputs(seed))
    spreads = {'L0_gnn_b1': (0.0, 0.1),
     'L0_gnn_b2': (0.0, 0.1),
     'L1_gnn_b1': (0.0, 0.8),
     'L1_gnn_g1': (1.0, 0.2),
     'L1_gnn_be1': (0.0, 0.1),
     'L1_gnn_b2': (0.0, 0.8),
     'L1_gnn_g2': (1.0, 0.2),
     'L1_gnn_be2': (0.0, 0.1),
     'L3_gnn_bg0': (0.0, 0.8),
     'L3_gnn_bg1': (0.0, 0.8)}
    factors = {'L3_gnn_Wg0': 7.812,
     'L3_gnn_Wg1': 5.35,
     'L3_gnn_Wih': 3.625,
     'L3_gnn_Whh': 8.0,
     'L3_gnn_bih': 2.841,
     'L3_gnn_bhh': 2.835}
    for name, (base, spread) in spreads.items():
        noise = np.random.default_rng([zlib.crc32(name.encode()), seed]).standard_normal(out[name].shape)
        drawn = base * np.exp(spread * noise) if base else spread * noise
        out[name] = jnp.asarray(drawn.astype(out[name].dtype))
    for name, factor in factors.items():
        out[name] = (out[name] * factor).astype(out[name].dtype)
    return out
```

```python
from contextlib import ExitStack, contextmanager

import concourse.bass as bass
from concourse import mybir

F32 = mybir.dt.float32
BF16 = mybir.dt.bfloat16
I32 = mybir.dt.int32
ALU = mybir.AluOpType
ACT = mybir.ActivationFunctionType
AX = mybir.AxisListType.X

P = 128
N = 64
D = 256
LEVELS = 6
HALVINGS = 40
TIE = 2.0 ** -30
BIG = 1e30
ROOT2 = 2.0 ** 0.5


class Chain:

    def __init__(self, eng, sem, entries):
        self.eng, self.sem, self.entries, self.n, self.turns = eng, sem, entries, 0, 0

    def link(self, ins):
        ins.then_inc(self.sem, 1)
        self.n += 1
        self.eng.wait_ge(self.sem, self.turns + self.n)

    @contextmanager
    def loop(self, count, per_turn, start=0):
        at, outer = self.n, self.turns
        self.eng.sem_inc(self.entries, 1)
        with self.eng.Fori(start, start + count) as i:
            self.turns = outer + (i - start) * per_turn
            yield i
            assert self.n - at == per_turn, (self.n - at, per_turn)
        self.n, self.turns = at + count * per_turn, outer


TABLES = dict(eye=N, below=N, first=N, tie=N, sub=N, sup=N, same=LEVELS * N, last=LEVELS * N, head=LEVELS * N,
              headcol=LEVELS)


def table_slices():
    at, out = 0, {}
    for name, w in TABLES.items():
        out[name] = (at, at + w)
        at += w
    return out, at


def constant_tables():
    import numpy as np
    p = np.arange(N)[:, None]
    c = np.arange(N)[None, :]
    parts = dict(eye=p == c, below=p > c + 1, first=p == c + 1, tie=(c - p) * TIE, sub=c == p - 1, sup=c == p + 1)
    parts["same"] = np.concatenate([p // (2 << l) == c // (2 << l) for l in range(LEVELS)], 1)
    parts["last"] = np.concatenate([(c % (2 << l) == (1 << l) - 1) + 0 * p for l in range(LEVELS)], 1)
    parts["head"] = np.concatenate([(c % (2 << l) == (1 << l)) + 0 * p for l in range(LEVELS)], 1)
    parts["headcol"] = np.concatenate([p % (2 << l) == (1 << l) for l in range(LEVELS)], 1)
    return np.concatenate([parts[k].astype(np.float32) for k in TABLES], 1)


class Mem:

    def __init__(self, nc, ctx):
        self.nc, self.ctx = nc, ctx
        self.ps = ctx.enter_context(nc.psum_tensor("ps", [P, 8 * 512], F32))

    def sb(self, name, shape, dt=F32):
        return self.ctx.enter_context(self.nc.sbuf_tensor(name, shape, dt))

    def sem(self, name):
        return self.ctx.enter_context(self.nc.semaphore(name))


def scope(nc, ctx):
    held = []

    def sb(name, shape, dt=F32):
        return ctx.enter_context(nc.sbuf_tensor(name, shape, dt))

    def sem(name):
        held.append(ctx.enter_context(nc.semaphore(name)))
        return held[-1]

    def clear():
        with nc.Block() as block:
            @block.gpsimd
            def _(pool):
                for s in held:
                    pool.sem_clear(s)

    sem.clear = clear
    return sb, sem


def spectral_basis(nc, m, io):
    with ExitStack() as ctx:
        sb, sem = scope(nc, ctx)
        at, width = table_slices()
        tab = sb("tab", [N, width])
        T = {k: tab[:, a:b] for k, (a, b) in at.items()}
        eye = T["eye"]
        adj2 = sb("adj2", [N, 2, N])
        ones = sb("ones", [N, P])
        mat = sb("mat", [N, 3 * N])
        low = sb("low", [N, 2 * N])
        col = sb("col", [N, 64])
        row = sb("row", [1, 6 * N])
        vt = sb("vt", [N, N])
        sgn_row = sb("sgn_row", [N, N])
        W4 = sb("W4", [N, 4 * N])
        big = [sb(f"big{i}", [N, N]) for i in range(14)]
        dup = sb("dup", [N, 2 * P])
        ps = m.ps
        tables_in = sem("tables_in")
        adj_in = sem("adj_in")
        bd_zero = sem("bd_zero")
        bd_adj_in = sem("bd_adj_in")
        dve_step = sem("eig_dve_step")
        sqrt_in, sqrt_out = sem("sqrt_in"), sem("sqrt_out")
        turn_in, turn_out = sem("turn_in"), sem("turn_out")
        parts_in, sums_out = sem("parts_in"), sem("sums_out")
        v_in, prods_out = sem("v_in"), sem("prods_out")
        rows_in, update_out = sem("rows_in"), sem("update_out")
        sq2_in, sq2_out = sem("sq2_in"), sem("sq2_out")
        pe_turns = sem("pe_turns")
        dve_turns = sem("dve_turns")
        reflectors = N - 2

        def c(i, w=1):
            return col[:, i:i + w]

        with nc.Block() as block:

            @block.sync
            def _(sp):
                sp.dma_start(tab[:, :], io["tables"]).then_inc(tables_in, 16)
                sp.dma_start(adj2[:, 0, :], io["adj"]).then_inc(adj_in, 16)
                sp.dma_start(adj2[:, 1, :], io["adj_t"]).then_inc(adj_in, 16)
                sp.wait_ge(bd_zero, 1)
                for h in range(2):
                    sp.dma_start(m.bd_adj[h * N:(h + 1) * N, h * N:(h + 1) * N], io["adj_t"]).then_inc(bd_adj_in, 16)
                sp.wait_ge(bd_adj_in, 32)

            @block.gpsimd
            def _(pool):
                pool.memset(m.bd_adj[:, :], 0.0).then_inc(bd_zero, 1)
                pool.memset(m.bd_u[:, :], 0.0).then_inc(bd_zero, 1)
                pool.memset(m.bd_ut[:, :], 0.0).then_inc(bd_zero, 1)
                pool.memset(m.bd_hat[:, :], 0.0).then_inc(bd_zero, 1)

            @block.scalar
            def _(act):
                act.wait_ge(sqrt_in, 1)
                act.activation(c(4, 2), c(2, 2), ACT.Sqrt).then_inc(sqrt_out, 1)
                with act.Fori(0, reflectors) as k:
                    act.wait_ge(sqrt_in, k + 2)
                    act.activation(c(7), c(6), ACT.Sqrt).then_inc(sqrt_out, 1)
                with act.Fori(0, LEVELS) as l:
                    act.wait_ge(sq2_in, l * 2 + 1)
                    act.activation(c(41), c(40), ACT.Sqrt).then_inc(sq2_out, 1)
                    act.wait_ge(sq2_in, l * 2 + 2)
                    act.activation(c(43), c(42), ACT.Sqrt).then_inc(sq2_out, 1)

            @block.tensor
            def _(pe):
                pe.wait_ge(tables_in, 16)
                pe.wait_ge(turn_in, 1)
                pe.matmul(ps[:, 0:N], dup[:, 0:P], eye, start=True, stop=True)
                pe.matmul(ps[:, 512:512 + N], dup[:, P:2 * P], eye, start=True, stop=True).then_inc(turn_out, 1)
                with pe.Fori(0, reflectors) as k:
                    pe.wait_ge(parts_in, k + 1)
                    pe.sem_inc(pe_turns, 1)
                    pe.matmul(ps[0:N, 0:2], ones[:, 0:N], c(10, 2), start=True, stop=True).then_inc(sums_out, 1)
                    pe.wait_ge(v_in, k + 1)
                    pe.sem_inc(pe_turns, 1)
                    pe.matmul(ps[0:1, 512:512 + 3 * N], c(12), mat[:, :], start=True, stop=True).then_inc(prods_out, 1)
                    pe.wait_ge(rows_in, k + 1)
                    pe.sem_inc(pe_turns, 1)
                    pe.matmul(ps[0:N, 1024:1024 + 2 * N], row[:, 0:N], row[:, N:3 * N], start=True, stop=False)
                    pe.matmul(ps[0:N, 1024:1024 + N], row[:, N:2 * N], row[:, 0:N], start=False, stop=True)\
                        .then_inc(update_out, 1)
                pe.wait_ge(turn_in, 2)
                pe.matmul(ps[0:N, 0:N], ones[:, 0:N], low[:, 0:N], start=True, stop=True).then_inc(turn_out, 1)
                with pe.Fori(0, LEVELS) as l:
                    pe.wait_ge(turn_in, l * 5 + 3)
                    pe.sem_inc(pe_turns, 1)
                    pe.matmul(ps[0:N, 0:1], big[0][:, :], c(15), start=True, stop=True).then_inc(turn_out, 1)
                    pe.wait_ge(turn_in, l * 5 + 4)
                    pe.sem_inc(pe_turns, 1)
                    pe.matmul(ps[0:N, 512:512 + 2 * N], ones[:, 0:N], W4[:, 0:2 * N], start=True, stop=True)\
                        .then_inc(turn_out, 1)
                    pe.wait_ge(turn_in, l * 5 + 5)
                    pe.sem_inc(pe_turns, 1)
                    pe.matmul(ps[0:N, 1024:1024 + 3 * N], ones[:, 0:N], W4[:, 0:3 * N], start=True, stop=True)\
                        .then_inc(turn_out, 1)
                    pe.wait_ge(turn_in, l * 5 + 6)
                    pe.sem_inc(pe_turns, 1)
                    pe.matmul(ps[0:N, 0:N], big[8][:, :], eye, start=True, stop=True)
                    pe.matmul(ps[0:N, 512:512 + N], big[9][:, :], eye, start=True, stop=True).then_inc(turn_out, 1)
                    pe.wait_ge(turn_in, l * 5 + 7)
                    pe.sem_inc(pe_turns, 1)
                    pe.matmul(ps[0:N, 1024:1024 + N], big[10][:, :], vt[:, :], start=True, stop=True)\
                        .then_inc(turn_out, 1)
                pe.wait_ge(turn_in, 5 * LEVELS + 3)
                pe.matmul(ps[0:N, 0:N], vt[:, :], eye, start=True, stop=True).then_inc(turn_out, 1)
                pe.wait_ge(turn_in, 5 * LEVELS + 4)
                pe.matmul(ps[:, 512:512 + N], dup[:, 0:P], big[0][:, :], start=True, stop=True)
                pe.matmul(ps[:, 1024:1024 + N], dup[:, P:2 * P], mat[:, N:2 * N], start=True, stop=True)\
                    .then_inc(turn_out, 1)

            @block.vector
            def _(dve):
                ch = Chain(dve, dve_step, dve_turns)
                link = ch.link
                tt, ts, stt = dve.tensor_tensor, dve.tensor_scalar, dve.scalar_tensor_tensor
                A = mat[:, 0:N]

                dve.wait_ge(tables_in, 16)
                dve.wait_ge(adj_in, 32)
                link(dve.memset(ones[:, :], 1.0))
                link(dve.memset(col[:, :], 0.0))
                link(dve.tensor_reduce(c(0), adj2[:, :, :], mybir.AxisListType.XY, ALU.add))
                link(tt(big[0][:, :], adj2[:, 0, :], eye, ALU.mult))
                link(dve.tensor_reduce(c(1), big[0][:, :], AX, ALU.add))
                link(tt(c(2), c(0), c(1), ALU.subtract))
                link(ts(c(3), c(2), 1.0, None, ALU.add))
                link(dve.tensor_copy(c(0), c(2)))
                link(ts(c(1), c(2), 0.0, None, ALU.is_gt))
                ts(c(2), c(2), 1e-30, None, ALU.max).then_inc(sqrt_in, 1)
                dve.wait_ge(sqrt_out, 1)
                link(dve.reciprocal(c(4, 2), c(4, 2)))
                link(tt(c(4), c(4), c(1), ALU.mult))
                link(tt(big[1][:, :], adj2[:, 0, :], adj2[:, 1, :], ALU.add))
                link(ts(big[2][:, :], eye, c(0), None, ALU.mult))
                link(stt(big[1][:, :], big[1][:, :], -0.5, big[2][:, :], ALU.mult, ALU.add))
                link(tt(big[3][:, :], adj2[:, 0, :], eye, ALU.add))
                for h in range(2):
                    link(ts(dup[:, h * N:(h + 1) * N], big[1][:, :], c(4), None, ALU.mult))
                link(ts(dup[:, P:P + N], big[3][:, :], c(5), None, ALU.mult))
                dve.tensor_copy(dup[:, P + N:2 * P], dup[:, P:P + N]).then_inc(turn_in, 1)
                dve.wait_ge(turn_out, 1)
                link(ts(A, ps[0:N, 0:N], c(4), None, ALU.mult))
                link(dve.tensor_copy(mat[:, N:2 * N], eye))
                link(dve.tensor_copy(mat[:, 2 * N:3 * N], eye))
                dve.wait_ge(bd_zero, 4)
                link(ts(m.bd_hat[0:N, 0:N], ps[0:N, 512:512 + N], c(5), None, ALU.mult))
                link(dve.tensor_copy(m.root_deg2[0:N, :], c(5)))
                link(dve.tensor_copy(m.root_deg2[N:P, :], c(5)))
                link(ts(m.bd_hat[N:P, N:P], ps[N:P, 512:512 + N], m.root_deg2[N:P, :], None, ALU.mult))

                with ch.loop(reflectors, 22) as k:
                    below, first = T["below"][:, bass.ds(k, 1)], T["first"][:, bass.ds(k, 1)]
                    a_k = A[:, bass.ds(k, 1)]
                    link(tt(c(9), a_k, below, ALU.mult))
                    link(tt(c(11), a_k, first, ALU.mult))
                    tt(c(10), c(9), c(9), ALU.mult).then_inc(parts_in, 1)
                    dve.wait_ge(sums_out, k + 1)
                    link(dve.tensor_copy(c(16, 2), ps[0:N, 0:2]))
                    link(tt(c(18), c(17), c(17), ALU.mult))
                    tt(c(6), c(18), c(16), ALU.add).then_inc(sqrt_in, 1)
                    link(ts(c(19), c(16), 0.0, None, ALU.is_gt))
                    link(ts(c(20), c(17), 0.0, None, ALU.is_ge))
                    link(ts(c(20), c(20), 2.0, -1.0, ALU.mult, ALU.add))
                    link(ts(c(21), c(19), -1.0, 1.0, ALU.mult, ALU.add))
                    dve.wait_ge(sqrt_out, k + 2)
                    link(stt(c(22), c(7), c(20), c(21), ALU.mult, ALU.add))
                    link(tt(c(23), c(22), c(17), ALU.add))
                    link(tt(c(24), c(23), c(21), ALU.add))
                    link(dve.reciprocal(c(25), c(24)))
                    stt(c(12), c(9), c(25), first, ALU.mult, ALU.add).then_inc(v_in, 1)
                    link(dve.reciprocal(c(26), c(22)))
                    link(tt(c(27), c(23), c(26), ALU.mult))
                    link(tt(c(13), c(27), c(19), ALU.mult))
                    dve.wait_ge(prods_out, k + 1)
                    link(dve.tensor_copy(row[:, 0:N], ps[0:1, 512 + 2 * N:512 + 3 * N]))
                    link(ts(row[:, 2 * N:3 * N], ps[0:1, 512 + N:512 + 2 * N], c(13)[0:1, :], None, ALU.mult))
                    link(ts(row[:, 3 * N:4 * N], ps[0:1, 512:512 + N], c(13)[0:1, :], None, ALU.mult))
                    link(tt(row[:, 4 * N:5 * N], row[:, 3 * N:4 * N], row[:, 0:N], ALU.mult))
                    link(dve.tensor_reduce(row[:, 5 * N:5 * N + 1], row[:, 4 * N:5 * N], AX, ALU.add))
                    link(ts(row[:, 5 * N + 1:5 * N + 2], row[:, 5 * N:5 * N + 1], c(13)[0:1, :], -0.5,
                            ALU.mult, ALU.mult))
                    stt(row[:, N:2 * N], row[:, 0:N], row[:, 5 * N + 1:5 * N + 2], row[:, 3 * N:4 * N],
                        ALU.mult, ALU.add).then_inc(rows_in, 1)
                    dve.wait_ge(update_out, k + 1)
                    link(tt(mat[:, 0:2 * N], mat[:, 0:2 * N], ps[0:N, 1024:1024 + 2 * N], ALU.subtract))

                link(tt(big[0][:, :], A, eye, ALU.mult))
                link(tt(big[1][:, :], A, T["sub"], ALU.mult))
                link(tt(big[2][:, :], A, T["sup"], ALU.mult))
                link(dve.tensor_reduce(c(0), big[0][:, :], AX, ALU.add))
                link(dve.tensor_reduce(c(1), big[1][:, :], AX, ALU.add))
                link(dve.tensor_reduce(c(3), big[2][:, :], AX, ALU.add))
                link(stt(c(2), c(1), -1.0, c(1), ALU.mult, ALU.max))
                link(stt(c(3), c(3), -1.0, c(3), ALU.mult, ALU.max))
                link(tt(c(0), c(0), c(2), ALU.subtract))
                link(tt(c(0), c(0), c(3), ALU.subtract))
                link(ts(c(4), c(1), 0.0, None, ALU.is_ge))
                link(ts(c(4), c(4), 2.0, -1.0, ALU.mult, ALU.add))
                ts(low[:, 0:N], eye, c(4), None, ALU.mult).then_inc(turn_in, 1)
                dve.wait_ge(turn_out, 2)
                link(dve.tensor_copy(sgn_row[:, :], ps[0:N, 0:N]))
                link(dve.tensor_copy(vt[:, :], eye))

                d, cut, rho, z, nd, w = c(0), c(15), c(8), c(28), c(29), c(30)
                same, off, part, gt, nxt = big[0], big[1], big[2], big[3], big[4]
                wts, tmp, tmp2, fac, inv, new = big[5], big[6], big[7], big[8], big[9], big[10]
                z_row, origin = big[11], big[12]
                with ch.loop(LEVELS, 98 + 7 * HALVINGS) as l:
                    def lev(name):
                        return T[name][:, bass.ds(l * N, N)]
                    link(tt(tmp[:, :], lev("head"), sgn_row[:, :], ALU.mult))
                    link(tt(tmp[:, :], tmp[:, :], lev("last"), ALU.add))
                    link(tt(tmp[:, :], tmp[:, :], vt[:, :], ALU.mult))
                    link(dve.tensor_reduce(z, tmp[:, :], AX, ALU.add))
                    link(dve.tensor_copy(same[:, :], lev("same")))
                    tt(cut, T["headcol"][:, bass.ds(l, 1)], c(2), ALU.mult).then_inc(turn_in, 1)
                    dve.wait_ge(turn_out, l * 5 + 3)
                    link(dve.tensor_copy(rho, ps[0:N, 0:1]))
                    link(stt(c(31), d, -1.0, d, ALU.mult, ALU.max))
                    link(stt(c(32), z, -1.0, z, ALU.mult, ALU.max))
                    link(stt(c(31), c(32), 1.0 / ROOT2, c(31), ALU.mult, ALU.max))
                    link(ts(W4[:, 0:N], eye, d, None, ALU.mult))
                    ts(W4[:, N:2 * N], eye, c(31), None, ALU.mult).then_inc(turn_in, 1)
                    dve.wait_ge(turn_out, l * 5 + 4)
                    link(tt(tmp[:, :], ps[0:N, 512 + N:512 + 2 * N], same[:, :], ALU.mult))
                    link(dve.tensor_reduce(c(33), tmp[:, :], AX, ALU.max))
                    link(ts(c(33), c(33), 8 * 2.0 ** -24, None, ALU.mult))
                    link(ts(off[:, :], ps[0:N, 512:512 + N], d, None, ALU.subtract))
                    link(tt(c(32), c(32), rho, ALU.mult))
                    link(ts(nd, c(32), ROOT2, c(33), ALU.mult, ALU.is_gt))
                    link(tt(z, z, nd, ALU.mult))
                    link(tt(w, z, z, ALU.mult))
                    link(tt(w, w, rho, ALU.mult))
                    link(ts(W4[:, 0:N], eye, z, None, ALU.mult))
                    link(ts(W4[:, N:2 * N], eye, nd, None, ALU.mult))
                    ts(W4[:, 2 * N:3 * N], eye, w, None, ALU.mult).then_inc(turn_in, 1)
                    dve.wait_ge(turn_out, l * 5 + 5)
                    link(dve.tensor_copy(z_row[:, :], ps[0:N, 1024:1024 + N]))
                    link(tt(part[:, :], ps[0:N, 1024 + N:1024 + 2 * N], same[:, :], ALU.mult))
                    link(tt(wts[:, :], ps[0:N, 1024 + 2 * N:1024 + 3 * N], same[:, :], ALU.mult))
                    link(stt(tmp[:, :], off[:, :], -1.0, off[:, :], ALU.mult, ALU.max))
                    link(tt(tmp2[:, :], T["tie"], off[:, :], ALU.subtract))
                    link(stt(tmp[:, :], tmp[:, :], TIE, tmp2[:, :], ALU.is_lt, ALU.mult))
                    link(tt(off[:, :], off[:, :], tmp[:, :], ALU.add))
                    link(tt(off[:, :], off[:, :], part[:, :], ALU.mult))
                    link(ts(tmp[:, :], part[:, :], -4.0, 4.0, ALU.mult, ALU.add))
                    link(tt(off[:, :], off[:, :], tmp[:, :], ALU.add))
                    link(ts(gt[:, :], off[:, :], 0.0, None, ALU.is_gt))
                    link(tt(gt[:, :], gt[:, :], part[:, :], ALU.mult))
                    link(ts(tmp[:, :], gt[:, :], -BIG, BIG, ALU.mult, ALU.add))
                    link(tt(tmp2[:, :], off[:, :], gt[:, :], ALU.mult))
                    link(tt(nxt[:, :], tmp2[:, :], tmp[:, :], ALU.add))
                    gap, top, hi, ntop = c(34), c(35), c(36), c(39)
                    link(dve.tensor_reduce(gap, nxt[:, :], AX, ALU.min))
                    link(ts(top, gap, BIG / 2, None, ALU.is_gt))
                    link(ts(ntop, top, -1.0, 1.0, ALU.mult, ALU.add))
                    link(dve.tensor_reduce(c(37), wts[:, :], AX, ALU.add))
                    link(tt(c(37), c(37), top, ALU.mult))
                    link(stt(hi, gap, ntop, c(37), ALU.mult, ALU.add))
                    half, neg, right, mu, trial = c(38), c(44), c(45), c(46), c(47)
                    link(ts(half, hi, 0.5, None, ALU.mult))
                    link(ts(tmp[:, :], off[:, :], half, None, ALU.subtract))
                    link(dve.reciprocal(tmp2[:, :], tmp[:, :]))
                    link(tt(tmp[:, :], tmp2[:, :], wts[:, :], ALU.mult))
                    link(dve.tensor_reduce(c(48), tmp[:, :], AX, ALU.add))
                    link(ts(neg, c(48), -1.0, None, ALU.is_lt))
                    link(tt(right, neg, ntop, ALU.mult))
                    link(tt(c(49), right, hi, ALU.mult))
                    link(ts(origin[:, :], off[:, :], c(49), None, ALU.subtract))
                    link(tt(c(50), top, ntop, ALU.subtract))
                    link(tt(c(50), c(50), neg, ALU.mult))
                    link(tt(mu, c(50), half, ALU.mult))
                    with ch.loop(HALVINGS, 7) as _:
                        link(ts(half, half, 0.5, None, ALU.mult))
                        link(tt(trial, mu, half, ALU.add))
                        link(ts(tmp[:, :], origin[:, :], trial, None, ALU.subtract))
                        link(dve.reciprocal(tmp2[:, :], tmp[:, :]))
                        link(stt(tmp[:, :], tmp2[:, :], 1.0, wts[:, :], ALU.mult, ALU.mult, accum_out=c(48)))
                        link(ts(c(48), c(48), -1.0, half, ALU.is_lt, ALU.mult))
                        link(tt(mu, mu, c(48), ALU.add))
                    link(ts(c(51), right, -1.0, 1.0, ALU.mult, ALU.add))
                    link(stt(mu, half, c(51), mu, ALU.mult, ALU.add))
                    link(ts(tmp[:, :], origin[:, :], mu, None, ALU.subtract))
                    link(ts(tmp2[:, :], tmp[:, :], 0.0, 1e-20, ALU.is_equal, ALU.mult))
                    link(tt(tmp[:, :], tmp[:, :], tmp2[:, :], ALU.add))
                    link(dve.reciprocal(inv[:, :], tmp[:, :]))
                    link(ts(part[:, :], part[:, :], nd, None, ALU.mult))
                    link(ts(tmp2[:, :], eye, -1.0, 1.0, ALU.mult, ALU.add))
                    link(tt(tmp2[:, :], tmp2[:, :], off[:, :], ALU.mult))
                    link(tt(tmp2[:, :], tmp2[:, :], eye, ALU.subtract))
                    link(dve.reciprocal(fac[:, :], tmp2[:, :]))
                    link(tt(fac[:, :], fac[:, :], tmp[:, :], ALU.mult))
                    link(tt(fac[:, :], fac[:, :], part[:, :], ALU.mult))
                    link(ts(tmp2[:, :], part[:, :], -1.0, 1.0, ALU.mult, ALU.add))
                    tt(fac[:, :], fac[:, :], tmp2[:, :], ALU.add).then_inc(turn_in, 1)
                    dve.wait_ge(turn_out, l * 5 + 6)
                    link(dve.tensor_reduce(c(40), ps[0:N, 0:N], AX, ALU.mult))
                    link(stt(c(40), c(40), -1.0, c(40), ALU.mult, ALU.max))
                    ts(c(40), c(40), 1e-30, None, ALU.max).then_inc(sq2_in, 1)
                    link(ts(c(52), z, 0.0, None, ALU.is_ge))
                    link(ts(c(52), c(52), 2.0, -1.0, ALU.mult, ALU.add))
                    link(tt(tmp[:, :], ps[0:N, 512:512 + N], part[:, :], ALU.mult))
                    link(ts(c(53), nd, -1.0, 1.0, ALU.mult, ALU.add))
                    link(ts(tmp2[:, :], eye, c(53), None, ALU.mult))
                    dve.wait_ge(sq2_out, l * 2 + 1)
                    link(tt(c(52), c(52), c(41), ALU.mult))
                    stt(new[:, :], tmp[:, :], c(52), tmp2[:, :], ALU.mult, ALU.add).then_inc(turn_in, 1)
                    dve.wait_ge(turn_out, l * 5 + 7)
                    link(dve.tensor_copy(vt[:, :], ps[0:N, 1024:1024 + N]))
                    link(tt(tmp[:, :], vt[:, :], vt[:, :], ALU.mult))
                    dve.tensor_reduce(c(42), tmp[:, :], AX, ALU.add).then_inc(sq2_in, 1)
                    link(ts(tmp2[:, :], off[:, :], gap, None, ALU.is_equal))
                    link(tt(tmp2[:, :], tmp2[:, :], z_row[:, :], ALU.mult))
                    link(dve.tensor_reduce(c(54), tmp2[:, :], AX, ALU.add))
                    link(tt(c(55), c(54), z, ALU.mult))
                    link(ts(c(56), c(55), 0.0, None, ALU.is_gt))
                    link(tt(c(57), c(54), c(54), ALU.mult))
                    link(stt(c(57), z, z, c(57), ALU.mult, ALU.add))
                    link(tt(c(57), c(57), c(33), ALU.mult))
                    link(tt(c(55), c(55), hi, ALU.mult))
                    link(tt(c(55), c(55), c(57), ALU.is_le))
                    link(tt(c(56), c(56), c(55), ALU.mult))
                    link(tt(c(56), c(56), ntop, ALU.mult))
                    link(tt(c(56), c(56), nd, ALU.mult))
                    link(ts(c(56), c(56), -2.0, 1.0, ALU.mult, ALU.add))
                    dve.wait_ge(sq2_out, l * 2 + 2)
                    link(dve.reciprocal(c(58), c(43)))
                    link(tt(c(58), c(58), c(56), ALU.mult))
                    link(ts(vt[:, :], vt[:, :], c(58), None, ALU.mult))
                    link(tt(c(59), c(49), mu, ALU.add))
                    link(tt(c(59), c(59), nd, ALU.mult))
                    link(tt(d, d, c(59), ALU.add))

                dve.tensor_copy(dup[:, 0:N], mat[:, N:2 * N]).then_inc(turn_in, 1)
                dve.wait_ge(turn_out, 5 * LEVELS + 3)
                link(dve.tensor_copy(big[0][:, :], ps[0:N, 0:N]))
                link(dve.tensor_copy(dup[:, N:2 * N], mat[:, N:2 * N]))
                link(dve.tensor_copy(dup[:, P:P + N], big[0][:, :]))
                dve.tensor_copy(dup[:, P + N:2 * P], big[0][:, :]).then_inc(turn_in, 1)
                dve.wait_ge(turn_out, 5 * LEVELS + 4)
                for h in range(2):
                    q = slice(h * N, (h + 1) * N)
                    link(dve.tensor_copy(m.bd_u[q, q], ps[q, 512:512 + N]))
                    link(dve.tensor_copy(m.bd_ut[q, q], ps[q, 1024:1024 + N]))
        sem.clear()


G = 4
GROUPS = 16
TILES = G * GROUPS
ROWS = TILES * P
GR = G * P
EPS = 1e-5


def inverse_root(nc, link, inv, root, square, corr):
    link(nc.vector.reciprocal(inv, root))
    link(nc.vector.tensor_tensor(corr, inv, inv, ALU.mult))
    link(nc.vector.tensor_tensor(corr, corr, square, ALU.mult))
    link(nc.vector.tensor_scalar(corr, corr, -0.5, 1.5, ALU.mult, ALU.add))
    link(nc.vector.tensor_tensor(inv, inv, corr, ALU.mult))


def row_statistics(nc, ch, m, stat, first_tile, tiles):
    ch.eng.sem_inc(ch.entries, 1)
    for t in range(tiles):
        nc.vector.bn_stats(stat[:, t, 0:6], m.X[:, bass.ds(first_tile + t, 1), :]).then_inc(ch.sem, 1)
    ch.n += tiles
    ch.eng.wait_ge(ch.sem, ch.turns + ch.n)
    ch.eng.sem_inc(ch.entries, 1)
    for t in range(tiles):
        nc.vector.bn_aggr(stat[:, t, 6:8], stat[:, t, 0:6]).then_inc(ch.sem, 1)
    ch.n += tiles
    ch.eng.wait_ge(ch.sem, ch.turns + ch.n)
    ch.link(nc.vector.tensor_copy(m.mv[:, bass.ds(first_tile, tiles), :], stat[:, 0:tiles, 6:8]))


def layer_norm(nc, m, tag, out=None):
    with ExitStack() as ctx:
        sb, sem = scope(nc, ctx)
        var, root, inv, corr, shift = (sb(f"{tag}_{k}", [P, TILES]) for k in ("var", "root", "inv", "corr", "shift"))
        step, turns = sem(f"{tag}_step"), sem(f"{tag}_turns")
        var_in, root_out, scales_out = sem(f"{tag}_var_in"), sem(f"{tag}_root_out"), sem(f"{tag}_scales_out")
        even_done, odd_done, stored = sem(f"{tag}_even_done"), sem(f"{tag}_odd_done"), sem(f"{tag}_stored")
        with nc.Block() as block:

            @block.vector
            def _(dve):
                link = Chain(dve, step, turns).link
                nc.vector.tensor_scalar(var[:, :], m.mv[:, :, 1], EPS, None, ALU.add).then_inc(var_in, 1)
                dve.wait_ge(root_out, 1)
                inverse_root(nc, link, inv[:, :], root[:, :], var[:, :], corr[:, :])
                nc.vector.scalar_tensor_tensor(shift[:, :], m.mv[:, :, 0], -1.0, inv[:, :], ALU.mult, ALU.mult)\
                    .then_inc(scales_out, 1)
                with dve.Fori(0, TILES // 2) as i:
                    x = m.X[:, bass.ds(i * 2, 1), :]
                    nc.vector.tensor_scalar(x, x, m.mv[:, bass.ds(i * 2, 1), 0], inv[:, bass.ds(i * 2, 1)],
                                            ALU.subtract, ALU.mult).then_inc(even_done, 1)

            @block.scalar
            def _(act):
                act.wait_ge(var_in, 1)
                nc.scalar.activation(root[:, :], var[:, :], ACT.Sqrt).then_inc(root_out, 1)
                act.wait_ge(scales_out, 1)
                with act.Fori(0, TILES // 2) as i:
                    x = m.X[:, bass.ds(i * 2 + 1, 1), :]
                    nc.scalar.activation(x, x, ACT.Identity, bias=shift[:, bass.ds(i * 2 + 1, 1)],
                                         scale=inv[:, bass.ds(i * 2 + 1, 1)]).then_inc(odd_done, 1)

            if out is not None:
                @block.sync
                def _(sp):
                    view = out.rearrange("(t p) d -> p t d", p=P)
                    with sp.Fori(0, TILES // 8) as i:
                        sp.wait_ge(even_done, i * 4 + 4)
                        sp.wait_ge(odd_done, i * 4 + 4)
                        sp.dma_start(view[:, bass.ds(i * 8, 8), :], m.X[:, bass.ds(i * 8, 8), :]).then_inc(stored, 16)
                    sp.wait_ge(stored, 16 * (TILES // 8))
        sem.clear()


def load_all(nc, m, io):
    m.weights_total = 16 * len(m.weights)
    with nc.Block() as block:

        @block.scalar
        def _(act):
            for k, v in m.weights.items():
                act.dma_start(v, io[k]).then_inc(m.weights_in, 16)

        @block.gpsimd
        def _(pool):
            rows = io["x"].rearrange("(t p) d -> p t d", p=P)
            for q in range(4):
                pool.dma_start(m.X[:, q * 16:(q + 1) * 16, :], rows[:, q * 16:(q + 1) * 16, :]).then_inc(m.x_in, 16)


def two_products(nc, m, tag, first):
    ps, w = m.ps, m.weights
    heads = 1 if first else 2
    mix_a = m.bd_u if first else m.bd_adj
    w1, w2 = (w["l0_w1"], w["l0_w2"]) if first else (w["l3_w0"], w["l3_w1"])
    b2 = w["l0_b2"] if first else w["l3_b1"]
    A_PS, B_PS, C_PS, D_PS = (ps[:, k * 1024:(k + 1) * 1024] for k in range(4))

    def chunked(bank):
        return bank.rearrange("p (c r) -> p c r", c=2)

    with ExitStack() as ctx:
        sb, sem = scope(nc, ctx)
        xs = sb(f"{tag}_xs", [P, G, D])
        agg = sb(f"{tag}_agg", [P, 2, GR])
        pre = sb(f"{tag}_pre", [P, 2, GR])
        hid = sb(f"{tag}_hid", [P, heads, GR])
        mid = sb(f"{tag}_mid", [P, G, D])
        stat = sb(f"{tag}_stat", [P, G, 8])
        sums = sb(f"{tag}_sums", [P, P])
        ones = sb(f"{tag}_ones", [P, P])
        xs_in, a_out, agg_in, b_out, pre_in, hid_in, c_out, mid_in, d_out, d_used = (
            sem(f"{tag}_{k}") for k in ("xs_in", "a_out", "agg_in", "b_out", "pre_in", "hid_in", "c_out", "mid_in",
                                        "d_out", "d_used"))
        ones_in, sums_out, sums_in = sem(f"{tag}_ones_in"), sem(f"{tag}_sums_out"), sem(f"{tag}_sums_in")
        step, turns = sem(f"{tag}_step"), sem(f"{tag}_turns")
        with nc.Block() as block:

            @block.gpsimd
            def _(pool):
                pool.wait_ge(m.x_in, 64)
                pool.tensor_copy(xs[:, :, :], m.X[:, 0:G, :]).then_inc(xs_in, 1)
                with pool.Fori(1, GROUPS) as i:
                    pool.wait_ge(a_out, i)
                    pool.tensor_copy(xs[:, :, :], m.X[:, bass.ds(i * G, G), :]).then_inc(xs_in, 1)

            @block.tensor
            def _(pe):
                pe.wait_ge(m.weights_in, m.weights_total)
                if not first:
                    pe.wait_ge(ones_in, 1)
                    pe.matmul(D_PS[:, 0:P], ones[:, :], m.bd_adj[:, :], start=True, stop=True).then_inc(sums_out, 1)
                    pe.wait_ge(sums_in, 1)

                def mix_in(i):
                    pe.wait_ge(xs_in, i + 1)
                    for c in range(2):
                        for t in range(G):
                            mm = pe.matmul(A_PS[:, c * GR + t * P:c * GR + (t + 1) * P],
                                           xs[:, t, c * P:(c + 1) * P], mix_a[:, :], start=True, stop=True)
                    mm.then_inc(a_out, 1)

                def weights_1(i):
                    pe.wait_ge(agg_in, i + 1)
                    for h in range(heads):
                        for k in range(2):
                            mm = pe.matmul(B_PS[:, h * GR:(h + 1) * GR], w1[:, k, h * P:(h + 1) * P], agg[:, k, :],
                                           start=k == 0, stop=k == 1)
                    mm.then_inc(b_out, 1)

                def weights_2(i):
                    pe.wait_ge(hid_in, i + 1)
                    for t in range(G):
                        for k in range(heads):
                            mm = pe.matmul(C_PS[:, t * D:(t + 1) * D], hid[:, k, t * P:(t + 1) * P], w2[:, k, :],
                                           start=k == 0, stop=k == heads - 1)
                    mm.then_inc(c_out, 1)

                def mix_out(i):
                    pe.wait_ge(mid_in, i + 1)
                    pe.wait_ge(d_used, i + 1)
                    if first:
                        for h in range(2):
                            mm = pe.matmul(D_PS[:, h * GR:(h + 1) * GR], m.bd_ut[:, :], mid[:, 2 * h:2 * h + 2, :],
                                           start=True, stop=True)
                    else:
                        for c in range(2):
                            for t in range(G):
                                mm = pe.matmul(D_PS[:, c * GR + t * P:c * GR + (t + 1) * P],
                                               mid[:, t, c * P:(c + 1) * P], m.bd_adj[:, :], start=True, stop=True)
                    mm.then_inc(d_out, 1)

                mix_in(0)
                weights_1(0)
                with pe.Fori(1, GROUPS) as i:
                    mix_in(i)
                    weights_2(i - 1)
                    weights_1(i)
                    mix_out(i - 1)
                weights_2(GROUPS - 1)
                mix_out(GROUPS - 1)

            @block.scalar
            def _(act):
                act.wait_ge(m.weights_in, m.weights_total)
                if not first:
                    act.sem_inc(d_used, 1)

                def copy_agg(i):
                    act.wait_ge(a_out, i + 1)
                    nc.scalar.copy(agg[:, :, :], chunked(A_PS)).then_inc(agg_in, 1)

                def relu(i):
                    if first:
                        act.wait_ge(b_out, i + 1)
                        nc.scalar.activation(hid[:, 0, :], B_PS[:, 0:GR], ACT.Relu, bias=w["l0_b1"][:, 0:1])\
                            .then_inc(hid_in, 1)
                    else:
                        act.wait_ge(pre_in, i + 1)
                        nc.scalar.activation(hid[:, :, :], pre[:, :, :], ACT.Relu).then_inc(hid_in, 1)

                def result(i):
                    act.wait_ge(d_out, i + 1)
                    nc.scalar.activation(m.T[:, :, bass.ds(i * GR, GR)], chunked(D_PS), ACT.Relu).then_inc(d_used, 1)

                copy_agg(0)
                relu(0)
                with act.Fori(1, GROUPS) as i:
                    copy_agg(i)
                    relu(i)
                    if not first:
                        result(i - 1)
                if not first:
                    result(GROUPS - 1)
                    act.wait_ge(d_used, GROUPS + 1)

            @block.vector
            def _(dve):
                ch = Chain(dve, step, turns)
                if first:
                    dve.sem_inc(d_used, 1)
                else:
                    nc.vector.memset(ones[:, :], 1.0).then_inc(ones_in, 1)
                    dve.wait_ge(sums_out, 1)
                    nc.vector.tensor_copy(sums[:, :], D_PS[:, 0:P]).then_inc(sums_in, 1)
                    dve.wait_ge(sums_in, 1)
                dve.wait_ge(m.weights_in, m.weights_total)

                def bias_1(i):
                    dve.wait_ge(b_out, i + 1)
                    for h in range(2):
                        ins = nc.vector.scalar_tensor_tensor(
                            pre[:, h, :].rearrange("p (t r) -> p t r", t=G), sums[:, None, :].broadcast_to([P, G, P]),
                            w["l3_b0"][:, h:h + 1], B_PS[:, h * GR:(h + 1) * GR].rearrange("p (t r) -> p t r", t=G),
                            ALU.mult, ALU.add)
                    ins.then_inc(pre_in, 1)

                def bias_2(i):
                    dve.wait_ge(c_out, i + 1)
                    nc.vector.tensor_tensor(mid[:, :, :], C_PS.rearrange("p (t d) -> p t d", t=G),
                                            b2[:, None, :].broadcast_to([P, G, D]), ALU.add).then_inc(mid_in, 1)

                def residual(i):
                    dve.wait_ge(d_out, i + 1)
                    x = m.X[:, bass.ds(i * G, G), :]
                    nc.vector.tensor_tensor(x, D_PS.rearrange("p (t d) -> p t d", t=G), x, ALU.add)\
                        .then_inc(d_used, 1)
                    dve.wait_ge(d_used, i + 2)
                    row_statistics(nc, ch, m, stat, i * G, G)

                if not first:
                    bias_1(0)
                with ch.loop(GROUPS - 1, 2 * G + 1 if first else 0, start=1) as i:
                    bias_2(i - 1)
                    if first:
                        residual(i - 1)
                    else:
                        bias_1(i)
                bias_2(GROUPS - 1)
                if first:
                    residual(GROUPS - 1)
        sem.clear()


def batch_normed(nc, m):
    ps, w, T = m.ps, m.weights, m.T
    HC = 4
    A_PS, C_PS = ps[:, 0:1024], ps[:, 0:1024]
    B_PS = ps[:, 1024:1024 + HC * GR]
    O_PS = [ps[:, 0:1024], ps[:, 1024:2048]]
    with ExitStack() as ctx:
        sb, sem = scope(nc, ctx)
        xs = sb("l1_xs", [P, G, D])
        hid = sb("l1_hid", [P, HC, GR])
        nrm = [sb(f"l1_nrm{s}", [P, 2, GR]) for s in range(2)]
        hstat = sb("l1_hstat", [P, HC, GROUPS, 6])
        ostat = sb("l1_ostat", [P, 2, GROUPS, 6])
        stat = sb("l1_stat", [P, G, 8])
        moments = sb("l1_moments", [P, HC + 2, 2])
        var, root, inv, corr, scale, mean, shift = (sb(f"l1_{k}", [P, HC + 2]) for k in
                                                    ("var", "root", "inv", "corr", "scale", "mean", "shift"))
        xs_in, a_out, agg_in, b_out, stats_in = (sem(f"l1_{k}") for k in ("xs_in", "a_out", "agg_in", "b_out",
                                                                          "stats_in"))
        b2_out, hid_in, c_out, out_in = (sem(f"l1_{k}") for k in ("b2_out", "hid_in", "c_out", "out_in"))
        nrm_in, turned, added = (sem(f"l1_{k}") for k in ("nrm_in", "turned", "added"))
        var_in, root_out, scales_in, ostat_in = (sem(f"l1_{k}") for k in ("var_in", "root_out", "scales_in",
                                                                          "ostat_in"))
        step, turns = sem("l1_step"), sem("l1_turns")
        with nc.Block() as block:

            @block.gpsimd
            def _(pool):
                pool.tensor_copy(xs[:, :, :], m.X[:, 0:G, :]).then_inc(xs_in, 1)
                with pool.Fori(1, GROUPS) as i:
                    pool.wait_ge(a_out, i)
                    pool.tensor_copy(xs[:, :, :], m.X[:, bass.ds(i * G, G), :]).then_inc(xs_in, 1)

            @block.tensor
            def _(pe):
                def mix(i):
                    pe.wait_ge(xs_in, i + 1)
                    for c in range(2):
                        for t in range(G):
                            mm = pe.matmul(A_PS[:, c * GR + t * P:c * GR + (t + 1) * P],
                                           xs[:, t, c * P:(c + 1) * P], m.bd_hat[:, :], start=True, stop=True)
                    mm.then_inc(a_out, 1)

                def hidden(i, done):
                    for h in range(HC):
                        if done is b_out:
                            pe.wait_ge(stats_in, i * HC + h + 1)
                        for k in range(2):
                            mm = pe.matmul(B_PS[:, h * GR:(h + 1) * GR], w["l1_w1"][:, k, h * P:(h + 1) * P],
                                           T[:, k, bass.ds(i * GR, GR)], start=k == 0, stop=k == 1)
                        mm.then_inc(done, 1)

                mix(0)
                with pe.Fori(1, GROUPS) as i:
                    pe.wait_ge(agg_in, i)
                    mix(i)
                    hidden(i - 1, b_out)
                pe.wait_ge(agg_in, GROUPS)
                hidden(GROUPS - 1, b_out)

                def output(i):
                    for k in range(HC):
                        if k == 0:
                            pe.wait_ge(out_in, i + 1)
                        for h in range(2):
                            pe.wait_ge(hid_in, i * HC + k + 1)
                            mm = pe.matmul(C_PS[:, h * GR:(h + 1) * GR], w["l1_w2"][:, k, h * P:(h + 1) * P],
                                           hid[:, k, :], start=k == 0, stop=k == HC - 1)
                    mm.then_inc(c_out, 1)

                pe.wait_ge(stats_in, GROUPS * HC + HC)
                hidden(0, b2_out)
                with pe.Fori(1, GROUPS) as i:
                    output(i - 1)
                    hidden(i, b2_out)
                output(GROUPS - 1)

                pe.wait_ge(out_in, GROUPS + 1)
                with pe.Fori(0, GROUPS // 2) as i:
                    for s in range(2):
                        pe.wait_ge(nrm_in, i * 2 + s + 1)
                        pe.wait_ge(added, i * 2 + s + 1)
                        for t in range(G):
                            for c in range(2):
                                mm = pe.transpose(O_PS[s][:, t * D + c * P:t * D + (c + 1) * P],
                                                  nrm[s][:, c, t * P:(t + 1) * P], w["eye"])
                        mm.then_inc(turned, 1)

            @block.scalar
            def _(act):
                with act.Fori(0, GROUPS) as i:
                    act.wait_ge(a_out, i + 1)
                    nc.scalar.copy(T[:, :, bass.ds(i * GR, GR)], A_PS.rearrange("p (c r) -> p c r", c=2))\
                        .then_inc(agg_in, 1)
                act.wait_ge(var_in, 1)
                nc.scalar.activation(root[:, 0:HC], var[:, 0:HC], ACT.Sqrt).then_inc(root_out, 1)
                act.wait_ge(scales_in, 1)
                with act.Fori(0, GROUPS) as i:
                    for h in range(HC):
                        act.wait_ge(b2_out, i * HC + h + 1)
                        nc.scalar.activation(hid[:, h, :], B_PS[:, h * GR:(h + 1) * GR], ACT.Relu,
                                             bias=shift[:, h:h + 1], scale=scale[:, h:h + 1]).then_inc(hid_in, 1)
                act.wait_ge(var_in, 2)
                nc.scalar.activation(root[:, HC:], var[:, HC:], ACT.Sqrt).then_inc(root_out, 1)
                act.wait_ge(scales_in, 2)

                def norm_out(i, s):
                    for c in range(2):
                        ins = nc.scalar.activation(nrm[s][:, c, :], T[:, c, bass.ds(i * GR, GR)], ACT.Identity,
                                                   bias=shift[:, HC + c:HC + c + 1], scale=scale[:, HC + c:HC + c + 1])
                    ins.then_inc(nrm_in, 1)

                norm_out(0, 0)
                norm_out(1, 1)
                with act.Fori(1, GROUPS // 2) as i:
                    for s in range(2):
                        act.wait_ge(turned, i * 2 + s - 1)
                        norm_out(i * 2 + s, s)

            @block.vector
            def _(dve):
                ch = Chain(dve, step, turns)
                link = ch.link
                tt, ts, stt = nc.vector.tensor_tensor, nc.vector.tensor_scalar, nc.vector.scalar_tensor_tensor
                dve.wait_ge(m.weights_in, m.weights_total)
                dve.sem_inc(stats_in, HC)
                with dve.Fori(0, GROUPS) as i:
                    for h in range(HC):
                        dve.wait_ge(b_out, i * HC + h + 1)
                        dve.sem_inc(turns, 1)
                        nc.vector.bn_stats(hstat[:, h, bass.ds(i, 1), :], B_PS[:, h * GR:(h + 1) * GR])\
                            .then_inc(stats_in, 1)
                dve.wait_ge(stats_in, GROUPS * HC + HC)

                def scales(a, b, stats):
                    for h in range(a, b):
                        link(nc.vector.bn_aggr(moments[:, h, :], stats[:, h - a, :, :]))
                    q = slice(a, b)
                    ts(var[:, q], moments[:, q, 1], EPS, None, ALU.add).then_inc(var_in, 1)
                    dve.wait_ge(root_out, 1 if a == 0 else 2)
                    inverse_root(nc, link, inv[:, q], root[:, q], var[:, q], corr[:, q])
                    link(tt(scale[:, q], inv[:, q], w["l1_g"][:, q], ALU.mult))
                    link(tt(mean[:, q], moments[:, q, 0], w["l1_b"][:, q], ALU.add))
                    link(tt(shift[:, q], w["l1_b"][:, q], mean[:, q], ALU.subtract))
                    link(tt(shift[:, q], shift[:, q], scale[:, q], ALU.mult))
                    tt(shift[:, q], shift[:, q], w["l1_be"][:, q], ALU.add).then_inc(scales_in, 1)

                scales(0, HC, hstat)
                dve.sem_inc(out_in, 1)
                with dve.Fori(0, GROUPS) as i:
                    dve.wait_ge(c_out, i + 1)
                    dve.sem_inc(turns, 1)
                    for h in range(2):
                        nc.vector.bn_stats(ostat[:, h, bass.ds(i, 1), :], C_PS[:, h * GR:(h + 1) * GR])\
                            .then_inc(ostat_in, 1)
                    nc.vector.tensor_copy(T[:, :, bass.ds(i * GR, GR)], C_PS.rearrange("p (c r) -> p c r", c=2))\
                        .then_inc(out_in, 1)
                dve.wait_ge(ostat_in, GROUPS * 2)
                scales(HC, HC + 2, ostat)
                dve.sem_inc(added, 2)
                with ch.loop(GROUPS // 2, 2 * (2 * G + 1)) as i:
                    for s in range(2):
                        dve.wait_ge(turned, i * 2 + s + 1)
                        x = m.X[:, bass.ds(i * (2 * G) + s * G, G), :]
                        tt(x, O_PS[s].rearrange("p (t d) -> p t d", t=G), x, ALU.add).then_inc(added, 1)
                        dve.wait_ge(added, i * 2 + s + 3)
                        row_statistics(nc, ch, m, stat, i * (2 * G) + s * G, G)
        sem.clear()


HEADS = 4
EDGES = 512
EC = EDGES // P
BLOCKS = 4
BT = TILES // BLOCKS
NODES = 8
CHUNKS = N // NODES


def graph_attention(nc, m, io):
    ps, w = m.ps, m.weights

    def bank(k, n=1):
        return ps[:, k * 512:(k + n) * 512]

    with ExitStack() as ctx:
        sb, sem = scope(nc, ctx)
        ends_i = sb("ends_i", [P, 2, EC], I32)
        rows_i = sb("rows_i", [P, 2, EDGES], I32)
        ends = sb("ends", [P, 2, EC])
        rows = sb("rows", [P, 2, EDGES])
        at_node = sb("at_node", [P, 2, EC, N])
        pairs = sb("pairs", [P, EC, N * N], BF16)
        gather = sb("gather", [P, EDGES])
        log_a = sb("log_a", [P, N * N])
        ones = sb("l2_ones", [P, P], BF16)
        per_edge = sb("per_edge", [P, EC])
        xs, xt, xq = sb("l2_xs", [P, D]), sb("l2_xt", [P, 2, P]), sb("l2_xq", [P, D])
        leaky = [sb(f"leaky{j}", [P, EDGES]) for j in range(4)]
        value = sb("value", [P, BT, D])
        attn = sb("attn", [P, BT, HEADS, N])
        score, rest = (leaky[j][:, :].rearrange("p (e r) -> p e r", e=EC) for j in range(2))
        times = attn[:, :, :, :].rearrange("p t h n -> p (t h n)")
        part = [sb(f"part{j}", [P, EC, P], BF16) for j in range(3)]
        soft = [sb(f"soft{s}", [P, NODES, N]) for s in range(2)]
        top, den = sb("top", [P, NODES]), sb("den", [P, NODES])
        vs, ws = sb("l2_vs", [P, D]), sb("l2_ws", [P, HEADS, N])
        yt = [sb(f"yt{s}", [P, 2, P]) for s in range(2)]
        stat = sb("l2_stat", [P, 1, 8])
        edges_in, adj_in, log_in, ones_in, pairs_in, count_out, count_in, adj_eps, made = (
            sem(f"l2_{k}") for k in ("edges_in", "adj_in", "log_in", "ones_in", "pairs_in", "count_out", "count_in", "adj_eps",
                                     "made"))
        xs_in, turned, xt_in, q_out, v_out, xq_in, v_in, gather_out, sum_in, leaky_in, score_out = (
            sem(f"l2_{k}") for k in ("xs_in", "turned", "xt_in", "q_out", "v_out", "xq_in", "v_in", "gather_out", "sum_in", "leaky_in",
                                     "score_out"))
        parts_in, dense_out, dense_in, less_max, exp_in, attn_in, turned2, w0_in, w1_in = (
            sem(f"l2_{k}") for k in ("parts_in", "dense_out", "dense_in", "less_max", "exp_in",
                                     "attn_in", "turned2", "w0_in", "w1_in"))
        staged, y_out, yt_in, o_out, added = (sem(f"l2_{k}") for k in ("staged", "y_out", "yt_in", "o_out", "added"))
        w0_in_free, w1_in_free = sem("l2_w0_free"), sem("l2_w1_free")
        step, turns, pe_turns, pool_turns = (sem(f"l2_{k}") for k in ("step", "turns", "pe_turns", "pool_turns"))
        def keep_turned(copy, part_of_two, k, done):
            src = bank(2 + 2 * (k % 2) + part_of_two)[0:N, :].rearrange("m (n t b h) -> m b t h n", t=BT, b=2, h=HEADS)
            n = k * NODES + part_of_two * NODES // 2
            for b in range(2):
                copy(attn[b * N:(b + 1) * N, :, :, n:n + NODES // 2], src[:, b]).then_inc(done, 1)

        with nc.Block() as block:

            @block.sync
            def _(sp):
                sp.dma_start(ends_i[:, :, :], io["edge_ends"]).then_inc(edges_in, 16)
                sp.dma_start(rows_i[:, :, :], io["edge_rows"]).then_inc(edges_in, 16)
                sp.dma_start(log_a[:, :], io["adj_row"].broadcast_to([P, N * N])).then_inc(adj_in, 16)

            @block.gpsimd
            def _(pool):
                with pool.Fori(0, BLOCKS) as q:
                    with pool.Fori(0, BT) as t:
                        pool.wait_ge(turned, q * BT + t + 1)
                        pool.tensor_copy(xs[:, :], m.X[:, bass.ds(q * BT + t, 1), :]).then_inc(xs_in, 1)
                    pool.wait_ge(w0_in, (q + 1) * CHUNKS * 2)
                    pool.wait_ge(w1_in, (q + 1) * CHUNKS * 2)
                    pool.sem_inc(pool_turns, 1)
                    with pool.Fori(0, BT) as t:
                        pool.wait_ge(y_out, q * BT + t + 1)
                        pool.tensor_copy(vs[:, :], value[:, bass.ds(t, 1), :])
                        pool.tensor_copy(ws[:, :, :], attn[:, bass.ds(t, 1), :, :]).then_inc(staged, 1)

            @block.tensor
            def _(pe):
                pe.sem_inc(turned, 1)
                pe.sem_inc(y_out, 1)
                pe.wait_ge(pairs_in, EC)
                pe.wait_ge(ones_in, 1)
                for k in range(CHUNKS):
                    for e in range(EC):
                        mm = pe.matmul(bank(k), ones[:, :], pairs[:, e, k * 512:(k + 1) * 512],
                                       start=e == 0, stop=e == EC - 1)
                mm.then_inc(count_out, 1)
                pe.wait_ge(made, 1)

                with pe.Fori(0, BLOCKS) as q:
                    def turn(t):
                        u = q * BT + t
                        pe.wait_ge(xs_in, u + 1)
                        for c in range(2):
                            mm = pe.transpose(bank(0)[:, c * P:(c + 1) * P], xs[:, c * P:(c + 1) * P], w["eye"])
                        mm.then_inc(turned, 1)

                    def queries_values(t):
                        u = q * BT + t
                        pe.wait_ge(v_in, u + 1)
                        pe.wait_ge(xt_in, u + 1)
                        for j in range(2):
                            for c in range(2):
                                mm = pe.matmul(bank(1 + 6 * j)[:, 0:D], xt[:, c, :], w["l2_wqv"][:, c, j * D:(j + 1) * D],
                                               start=c == 0, stop=c == 1)
                            mm.then_inc(v_out if j else q_out, 1)

                    def gathers(t):
                        pe.wait_ge(xq_in, q * BT + t + 1)
                        pe.sem_inc(pe_turns, 1)
                        for b in range(2):
                            half = slice(b * N, (b + 1) * N)
                            for c in range(2):
                                pe.matmul(bank(2 + 2 * b + c), xq[half, c * P:(c + 1) * P], gather[half, :],
                                          start=True, stop=True).then_inc(gather_out, 1)

                    def scores(t):
                        pe.wait_ge(leaky_in, (q * BT + t + 1) * 4)
                        for b in range(2):
                            for e in range(EC):
                                for c in range(2):
                                    mm = pe.matmul(bank(6)[:, bass.ds(e * P + b * HEADS + t * (2 * HEADS), HEADS)],
                                                   leaky[2 * b + c][:, e * P:(e + 1) * P], w["l2_a"][:, c, :],
                                                   start=c == 0, stop=c == 1)
                        mm.then_inc(score_out, 1)

                    turn(0)
                    queries_values(0)
                    gathers(0)
                    with pe.Fori(1, BT) as t:
                        turn(t)
                        queries_values(t)
                        scores(t - 1)
                        gathers(t)
                    scores(BT - 1)

                    def dense(k):
                        pe.wait_ge(dense_in, q * CHUNKS + k + 1)
                        for j in range(3):
                            for e in range(EC):
                                mm = pe.matmul(bank(k % 2), part[j][:, e, :], pairs[:, e, k * 512:(k + 1) * 512],
                                               start=j + e == 0, stop=j == 2 and e == EC - 1)
                        mm.then_inc(dense_out, 1)

                    def turn_weights(k):
                        v = q * CHUNKS + k
                        pe.wait_ge(w0_in_free, v + 1)
                        pe.wait_ge(w1_in_free, v + 1)
                        pe.wait_ge(attn_in, v + 1)
                        pe.sem_inc(pe_turns, 1)
                        for n in range(NODES):
                            mm = pe.transpose(bank(2 + 2 * (k % 2), 2)[0:N, n * P:(n + 1) * P],
                                              soft[k % 2][:, n, :], w["eye"])
                        mm.then_inc(turned2, 1)

                    pe.wait_ge(v_in, (q + 1) * BT + 1)
                    pe.wait_ge(parts_in, q + 1)
                    dense(0)
                    for k in range(CHUNKS):
                        if k + 1 < CHUNKS:
                            dense(k + 1)
                        turn_weights(k)

                    def sums(t, s):
                        u = q * BT + t
                        pe.wait_ge(yt_in, u + 1)
                        pe.wait_ge(staged, u + 1)
                        pe.sem_inc(pe_turns, 1)
                        for b in range(2):
                            half = slice(b * N, (b + 1) * N)
                            for h in range(HEADS):
                                mm = pe.matmul(bank(3 * s + b)[(h % 2) * N:(h % 2 + 1) * N, h // 2 * N:(h // 2 + 1) * N],
                                               vs[half, h * N:(h + 1) * N], ws[half, h, :], start=True, stop=True)
                        mm.then_inc(y_out, 1)

                    def output(t, s):
                        u = q * BT + t
                        pe.wait_ge(added, u + 1)
                        pe.wait_ge(yt_in, u + 3)
                        for c in range(2):
                            mm = pe.matmul(bank(3 * s + 2)[:, 0:D], yt[s][:, c, :], w["l2_wo"][:, c, :],
                                           start=c == 0, stop=c == 1)
                        mm.then_inc(o_out, 1)

                    sums(0, 0)
                    with pe.Fori(0, BT // 2 - 1) as i:
                        sums(i * 2 + 1, 1)
                        output(i * 2, 0)
                        sums(i * 2 + 2, 0)
                        output(i * 2 + 1, 1)
                    sums(BT - 1, 1)
                    output(BT - 2, 0)
                    output(BT - 1, 1)

            @block.scalar
            def _(act):
                act.sem_inc(v_in, 1)
                act.sem_inc(yt_in, 2)
                act.sem_inc(w1_in_free, 2)
                act.wait_ge(adj_eps, 1)
                nc.scalar.activation(log_a[:, :], log_a[:, :], ACT.Ln)
                act.wait_ge(count_in, 1)
                pair_count = value[:, :, :].rearrange("p t d -> p (t d)")
                nc.scalar.activation(pair_count, pair_count, ACT.Ln).then_inc(log_in, 1)
                with act.Fori(0, BLOCKS) as q:
                    with act.Fori(0, BT) as t:
                        u = q * BT + t
                        act.wait_ge(turned, u + 2)
                        nc.scalar.copy(xt[:, :, :], bank(0)[:, 0:D].rearrange("p (c r) -> p c r", c=2)).then_inc(xt_in, 1)
                        act.wait_ge(v_out, u + 1)
                        nc.scalar.copy(value[:, bass.ds(t, 1), :], bank(7)[:, None, 0:D]).then_inc(v_in, 1)
                        for j in range(4):
                            act.wait_ge(gather_out, u * 4 + j + 1)
                            nc.scalar.copy(leaky[j][:, :], bank(2 + j)).then_inc(sum_in, 1)

                    def exponential(k):
                        act.wait_ge(less_max, q * CHUNKS + k + 1)
                        nc.scalar.activation(soft[k % 2][:, :, :], soft[k % 2][:, :, :], ACT.Exp).then_inc(exp_in, 1)

                    def keep(k):
                        act.wait_ge(turned2, q * CHUNKS + k + 3)
                        keep_turned(nc.scalar.copy, 1, k, w1_in)
                        act.wait_ge(w1_in, (q * CHUNKS + k + 1) * 2)
                        act.sem_inc(w1_in_free, 1)

                    exponential(0)
                    for k in range(CHUNKS):
                        if k + 1 < CHUNKS:
                            exponential(k + 1)
                        keep(k)

                    with act.Fori(0, BT // 2) as i:
                        for s in range(2):
                            act.wait_ge(y_out, q * BT + i * 2 + s + 2)
                            nc.scalar.copy(yt[s][:, :, :].rearrange("p c (b n) -> p b c n", b=2),
                                           bank(3 * s, 2).rearrange("p (b x) -> p b x", b=2)[:, :, 0:P]
                                           .rearrange("p b (c n) -> p b c n", c=2)).then_inc(yt_in, 1)

            @block.vector
            def _(dve):
                ch = Chain(dve, step, turns)
                link = ch.link
                tt, ts, stt = nc.vector.tensor_tensor, nc.vector.tensor_scalar, nc.vector.scalar_tensor_tensor
                dve.sem_inc(dense_in, 2)
                dve.sem_inc(turned2, 2)
                dve.sem_inc(w0_in_free, 2)
                dve.sem_inc(added, 2)
                nc.vector.memset(ones[:, :], 1.0).then_inc(ones_in, 1)
                dve.wait_ge(edges_in, 32)
                link(nc.vector.tensor_copy(ends[:, :, :], ends_i[:, :, :]))
                link(nc.vector.tensor_copy(rows[:, :, :], rows_i[:, :, :]))
                for s in range(2):
                    for e in range(EC):
                        link(ts(at_node[:, s, e, :], w["l2_nodes"], ends[:, s, e:e + 1], None, ALU.is_equal))
                for e in range(EC):
                    tt(pairs[:, e, :].rearrange("p (n m) -> p n m", m=N),
                       at_node[:, 0, e, :, None].broadcast_to([P, N, N]),
                       at_node[:, 1, e, None, :].broadcast_to([P, N, N]), ALU.mult).then_inc(pairs_in, 1)
                link(ts(leaky[0][:, :], rows[:, 0, :], w["l2_node"][:, 0:1], None, ALU.is_equal))
                link(stt(gather[:, :], rows[:, 1, :], w["l2_node"][:, 0:1], leaky[0][:, :], ALU.is_equal, ALU.add))
                for e in range(EC):
                    link(ts(leaky[0][:, :], rows[:, 0, :], ends[:, 0, e:e + 1], None, ALU.is_equal))
                    link(stt(leaky[1][:, :], rows[:, 1, :], ends[:, 1, e:e + 1], leaky[0][:, :],
                             ALU.is_equal, ALU.mult))
                    link(nc.vector.tensor_reduce(per_edge[:, e:e + 1], leaky[1][:, :], AX, ALU.add))
                link(nc.vector.reciprocal(per_edge[:, :], per_edge[:, :]))
                dve.wait_ge(adj_in, 16)
                ts(log_a[:, :], log_a[:, :], 1e-8, None, ALU.add).then_inc(adj_eps, 1)
                dve.wait_ge(count_out, 1)
                pair_count = value[:, :, :].rearrange("p t d -> p (t d)")
                link(nc.vector.tensor_copy(times, ps[:, :]))
                ts(pair_count, times, 1.0, None, ALU.max).then_inc(count_in, 1)
                dve.wait_ge(log_in, 1)
                link(tt(log_a[:, :], log_a[:, :], pair_count, ALU.add))
                link(ts(times, times, 0.0, -BIG, ALU.is_equal, ALU.mult))
                tt(log_a[:, :], log_a[:, :], times, ALU.add).then_inc(made, 1)
                dve.wait_ge(made, 1)

                soften, finish, tile_steps = 2, 3, 3
                with ch.loop(BLOCKS, EC + 4 + CHUNKS * (soften + finish) + BT * tile_steps) as q:
                    with dve.Fori(0, BT) as t:
                        dve.wait_ge(q_out, q * BT + t + 1)
                        nc.vector.tensor_copy(xq[:, :], bank(1)[:, 0:D]).then_inc(xq_in, 1)
                        for j in range(4):
                            dve.wait_ge(sum_in, (q * BT + t) * 4 + j + 1)
                            stt(leaky[j][:, :], leaky[j][:, :], 0.2, leaky[j][:, :], ALU.mult, ALU.max)\
                                .then_inc(leaky_in, 1)

                    dve.wait_ge(score_out, (q + 1) * BT)
                    dve.sem_inc(turns, 1)
                    for e in range(EC):
                        ts(score[:, e, :], bank(6)[:, e * P:(e + 1) * P], per_edge[:, e:e + 1], None, ALU.mult)\
                            .then_inc(step, 1)
                    ch.n += EC
                    dve.wait_ge(step, ch.turns + ch.n)
                    link(nc.vector.tensor_copy(part[0][:, :, :], score[:, :, :]))
                    link(tt(rest[:, :, :], score[:, :, :], part[0][:, :, :], ALU.subtract))
                    link(nc.vector.tensor_copy(part[1][:, :, :], rest[:, :, :]))
                    link(tt(score[:, :, :], rest[:, :, :], part[1][:, :, :], ALU.subtract))
                    nc.vector.tensor_copy(part[2][:, :, :], score[:, :, :]).then_inc(parts_in, 1)

                    def less_maximum(k):
                        v, x = q * CHUNKS + k, soft[k % 2][:, :, :]
                        dve.wait_ge(turned2, v + 1)
                        dve.wait_ge(dense_out, v + 1)
                        tt(x, bank(k % 2).rearrange("p (n m) -> p n m", m=N),
                           log_a[:, k * 512:(k + 1) * 512].rearrange("p (n m) -> p n m", m=N), ALU.add)\
                            .then_inc(dense_in, 1)
                        dve.wait_ge(dense_in, v + 3)
                        link(nc.vector.tensor_reduce(top[:, :], x, AX, ALU.max))
                        link(ts(top[:, :], top[:, :], -BIG / 2, None, ALU.max))
                        tt(x, x, top[:, :, None].broadcast_to([P, NODES, N]), ALU.subtract).then_inc(less_max, 1)
                        dve.wait_ge(less_max, v + 1)

                    def normalise(k):
                        v, x = q * CHUNKS + k, soft[k % 2][:, :, :]
                        dve.wait_ge(exp_in, v + 1)
                        link(nc.vector.tensor_reduce(den[:, :], x, AX, ALU.add))
                        link(ts(den[:, :], den[:, :], 1e-30, None, ALU.max))
                        link(nc.vector.reciprocal(den[:, :], den[:, :]))
                        tt(x, x, den[:, :, None].broadcast_to([P, NODES, N]), ALU.mult).then_inc(attn_in, 1)

                    def keep(k):
                        v = q * CHUNKS + k
                        dve.wait_ge(turned2, v + 3)
                        keep_turned(nc.vector.tensor_copy, 0, k, w0_in)
                        dve.wait_ge(w0_in, (v + 1) * 2)
                        dve.sem_inc(w0_in_free, 1)

                    less_maximum(0)
                    for k in range(CHUNKS):
                        if k + 1 < CHUNKS:
                            less_maximum(k + 1)
                        if k:
                            keep(k - 1)
                        normalise(k)
                    keep(CHUNKS - 1)

                    with ch.loop(BT // 2, 2 * tile_steps) as i:
                        for s in range(2):
                            u = q * BT + i * 2 + s
                            dve.wait_ge(o_out, u + 1)
                            x = m.X[:, bass.ds(u, 1), :]
                            tt(x, bank(3 * s + 2)[:, None, 0:D], x, ALU.add).then_inc(added, 1)
                            dve.wait_ge(added, u + 3)
                            row_statistics(nc, ch, m, stat, u, 1)
        sem.clear()


SKIPS = 4
GATE_ORDER = (0, 2, 1, 3)


def window_batches(p):
    nb = P
    while nb * (N // p) > 512 or P % nb:
        nb -= 1
    return nb


def skip_lstms(nc, m, io):
    ps, T = m.ps, m.T
    with ExitStack() as ctx:
        sb, sem = scope(nc, ctx)
        wx = [sb(f"wx{s}", [P, 2, 4 * D]) for s in range(2)]
        wh = sb("wh", [P, 2, 4 * D])
        bias2 = sb("lstm_bias2", [P, 2, SKIPS * 8])
        bias = sb("lstm_bias", [P, SKIPS * 8])
        gate = [[sb(f"gate{s}{g}", [P, 512]) for g in range(4)] for s in range(2)]
        cell = sb("cell", [P, 2, 512])
        tanh_c = [gate[c][0] for c in range(2)]
        state = [sb(f"state{s}", [P, 2, 512]) for s in range(2)]
        bias_in, bias_sum = sem("lstm_bias_in"), sem("lstm_bias_sum")
        wx_in, wh_in = sem("wx_in"), sem("wh_in")
        gates_out, gates_in, gates_free = sem("lstm_gates_out"), sem("lstm_gates_in"), sem("lstm_gates_free")
        cell_in, tanh_in, state_in, kept = sem("cell_in"), sem("tanh_in"), sem("state_in"), sem("state_kept")
        state_in_primed, pool_turns = sem("state_in_primed"), sem("lstm_pool_turns")
        p_done, step, turns, pe_turns = sem("lstm_p_done"), sem("lstm_step"), sem("lstm_turns"), sem("lstm_pe_turns")

        def shape(p):
            nb = window_batches(p)
            nw = N // p
            return nb, nw, nb * nw, P // nb

        units, gates, groups = [0], [0], [0]
        for p in range(1, SKIPS + 1):
            n = shape(p)[3]
            groups.append(groups[-1] + n)
            units.append(units[-1] + n * 2 * p)
            gates.append(gates[-1] + n * (8 * p - 2))

        def each_unit(p):
            u = g = 0
            for t in range(p):
                for c in range(2):
                    order = [q for q in GATE_ORDER if t or q != 1]
                    yield t, c, order, u, g
                    u += 1
                    g += len(order)

        with nc.Block() as block:

            @block.sync
            def _(sp):
                sp.dma_start(bias2[:, 0, :], io["l3_bih"]).then_inc(bias_in, 16)
                sp.dma_start(bias2[:, 1, :], io["l3_bhh"]).then_inc(bias_in, 16)
                for p in range(1, SKIPS + 1):
                    if p > 2:
                        sp.wait_ge(p_done, p - 2)
                    sp.dma_start(wx[p % 2][:, :, :], io["l3_wih"][p - 1]).then_inc(wx_in, 16)
                    sp.wait_ge(wx_in, 16 * p)
                    if p > 1:
                        if p > 2:
                            sp.wait_ge(p_done, p - 1)
                        sp.dma_start(wh[:, :, :], io["l3_whh"][p - 1]).then_inc(wh_in, 16)

            @block.tensor
            def _(pe):
                for p in range(1, SKIPS + 1):
                    nb, nw, C, n = shape(p)
                    pe.wait_ge(wx_in, 16 * p)
                    if p > 1:
                        pe.wait_ge(kept, groups[p - 1] + 1)
                    with pe.Fori(0, n) as i:
                        rows = T[:, :, :].rearrange("p k (b n) -> p k b n", n=N)
                        for t, c, order, u, g in each_unit(p):
                            pe.wait_ge(gates_free, units[p - 1] + i * (2 * p) + u + 1)
                            for q in order:
                                bank = ps[:, (c * 4 + q) * 512:(c * 4 + q) * 512 + C]
                                col = q * D + c * P
                                for k in range(2):
                                    x = rows[:, k, bass.ds(i * nb, nb), t:t + (nw - 1) * p + 1:p]
                                    mm = pe.matmul(bank.rearrange("p (b w) -> p b w", w=nw), wx[p % 2][:, k, col:col + P],
                                                   x, start=k == 0, stop=k == 1 and t == 0)
                                if t == 0:
                                    mm.then_inc(gates_out, 1)
                            if t == 1:
                                pe.wait_ge(wh_in, 16 * (p - 1))
                            if t:
                                pe.wait_ge(state_in, units[p - 1] + i * (2 * p) + 2 * t)
                                for q in order:
                                    bank = ps[:, (c * 4 + q) * 512:(c * 4 + q) * 512 + C]
                                    col = q * D + c * P
                                    for k in range(2):
                                        mm = pe.matmul(bank, wh[:, k, col:col + P], state[(t - 1) % 2][:, k, 0:C],
                                                       start=False, stop=k == 1)
                                    mm.then_inc(gates_out, 1)
                    pe.wait_ge(state_in, units[p])
                    pe.sem_inc(p_done, 1)

            @block.scalar
            def _(act):
                act.sem_inc(gates_free, 2)
                act.wait_ge(bias_sum, 1)
                for p in range(1, SKIPS + 1):
                    nb, nw, C, n = shape(p)
                    with act.Fori(0, n) as i:
                        for t, c, order, u, g in each_unit(p):
                            unit = units[p - 1] + i * (2 * p) + u
                            act.wait_ge(state_in_primed, unit + 1)
                            for j, q in enumerate(order):
                                act.wait_ge(gates_out, gates[p - 1] + i * (8 * p - 2) + g + j + 1)
                                ins = nc.scalar.activation(
                                    gate[c][q][:, 0:C], ps[:, (c * 4 + q) * 512:(c * 4 + q) * 512 + C],
                                    ACT.Tanh if q == 2 else ACT.Sigmoid,
                                    bias=bias[:, (p - 1) * 8 + q * 2 + c:(p - 1) * 8 + q * 2 + c + 1])
                                ins.then_inc(gates_in, 1)
                            act.wait_ge(gates_in, gates[p - 1] + i * (8 * p - 2) + g + len(order))
                            act.sem_inc(gates_free, 1)
                            act.wait_ge(cell_in, unit + 1)
                            nc.scalar.activation(tanh_c[c][:, 0:C], cell[:, c, 0:C], ACT.Tanh).then_inc(tanh_in, 1)

            @block.vector
            def _(dve):
                tt = nc.vector.tensor_tensor
                dve.wait_ge(bias_in, 32)
                dve.sem_inc(state_in_primed, 2)
                tt(bias[:, :], bias2[:, 0, :], bias2[:, 1, :], ALU.add).then_inc(bias_sum, 1)
                ch = Chain(dve, step, turns)
                for p in range(1, SKIPS + 1):
                    nb, nw, C, n = shape(p)
                    with ch.loop(n, 4 * (p - 1)) as i:
                        for t, c, order, u, g in each_unit(p):
                            gi, gf, gg, go = (gate[c][q][:, 0:C] for q in range(4))
                            unit, at = units[p - 1] + i * (2 * p) + u, gates[p - 1] + i * (8 * p - 2) + g
                            dve.wait_ge(gates_in, at + 2)
                            if t == 0:
                                tt(cell[:, c, 0:C], gi, gg, ALU.mult).then_inc(cell_in, 1)
                            else:
                                tt(gi, gi, gg, ALU.mult).then_inc(step, 1)
                                dve.wait_ge(gates_in, at + 3)
                                tt(gf, gf, cell[:, c, 0:C], ALU.mult).then_inc(step, 1)
                                ch.n += 2
                                dve.wait_ge(step, ch.turns + ch.n)
                                tt(cell[:, c, 0:C], gi, gf, ALU.add).then_inc(cell_in, 1)
                            if t == (p - 1) % 2 and c == 0:
                                dve.wait_ge(kept, groups[p - 1] + i + 1)
                            dve.wait_ge(tanh_in, unit + 1)
                            tt(state[t % 2][:, c, 0:C], go, tanh_c[c][:, 0:C], ALU.mult).then_inc(state_in, 1)
                            dve.wait_ge(state_in, unit + 1)
                            dve.sem_inc(state_in_primed, 1)

            @block.gpsimd
            def _(pool):
                pool.sem_inc(kept, 1)
                for p in range(1, SKIPS + 1):
                    nb, nw, C, n = shape(p)
                    with pool.Fori(0, n) as i:
                        pool.wait_ge(state_in, units[p - 1] + (i + 1) * (2 * p))
                        pool.sem_inc(pool_turns, 1)
                        rows = T[:, :, :].rearrange("p k (b n) -> p k b n", n=N)
                        for k in range(2):
                            ins = pool.tensor_copy(rows[:, k, bass.ds(i * nb, nb), p - 1:p - 1 + (nw - 1) * p + 1:p],
                                                   state[(p - 1) % 2][:, k, 0:C].rearrange("p (b w) -> p b w", w=nw))
                        ins.then_inc(kept, 1)
                pool.wait_ge(kept, groups[SKIPS] + 1)
        sem.clear()


def turn_and_add(nc, m):
    ps, T = m.ps, m.T
    O_PS = [ps[:, 0:1024], ps[:, 1024:2048]]
    with ExitStack() as ctx:
        sb, sem = scope(nc, ctx)
        fixed = [sb(f"turn_fixed{s}", [P, 2, GR]) for s in range(2)]
        stat = sb("turn_stat", [P, G, 8])
        fixed_in, turned, added, step, turns = (sem(f"turn_{k}") for k in ("fixed_in", "turned", "added", "step",
                                                                         "turns"))
        with nc.Block() as block:

            @block.scalar
            def _(act):
                def copy(i, s):
                    nc.scalar.copy(fixed[s][:, :, :], T[:, :, bass.ds(i * GR, GR)]).then_inc(fixed_in, 1)

                copy(0, 0)
                copy(1, 1)
                with act.Fori(1, GROUPS // 2) as i:
                    for s in range(2):
                        act.wait_ge(turned, i * 2 + s - 1)
                        copy(i * 2 + s, s)

            @block.tensor
            def _(pe):
                with pe.Fori(0, GROUPS // 2) as i:
                    for s in range(2):
                        pe.wait_ge(fixed_in, i * 2 + s + 1)
                        pe.wait_ge(added, i * 2 + s + 1)
                        for t in range(G):
                            for c in range(2):
                                mm = pe.transpose(O_PS[s][:, t * D + c * P:t * D + (c + 1) * P],
                                                  fixed[s][:, c, t * P:(t + 1) * P], m.weights["eye"])
                        mm.then_inc(turned, 1)

            @block.vector
            def _(dve):
                ch = Chain(dve, step, turns)
                dve.sem_inc(added, 2)
                with ch.loop(GROUPS // 2, 2 * (2 * G + 1)) as i:
                    for s in range(2):
                        dve.wait_ge(turned, i * 2 + s + 1)
                        x = m.X[:, bass.ds(i * (2 * G) + s * G, G), :]
                        nc.vector.tensor_tensor(x, O_PS[s].rearrange("p (t d) -> p t d", t=G), x, ALU.add)\
                            .then_inc(added, 1)
                        dve.wait_ge(added, i * 2 + s + 3)
                        row_statistics(nc, ch, m, stat, i * (2 * G) + s * G, G)
        sem.clear()


def program(nc, io, out):
    with ExitStack() as ctx:
        m = Mem(nc, ctx)
        m.bd_u, m.bd_ut, m.bd_hat, m.bd_adj = (m.sb(k, [P, P]) for k in ("bd_u", "bd_ut", "bd_hat", "bd_adj"))
        m.root_deg2 = m.sb("root_deg2", [P, 1])
        m.X = m.sb("X", [P, TILES, D])
        m.mv = m.sb("mv", [P, TILES, 2])
        m.weights = {}
        for k, shape in WEIGHTS.items():
            m.weights[k] = m.sb(k, [P] + shape)[(slice(None),) * (1 + len(shape))]
        m.weights_in, m.x_in = m.sem("weights_in"), m.sem("x_in")
        load_all(nc, m, io)
        spectral_basis(nc, m, io)
        two_products(nc, m, "l0", True)
        layer_norm(nc, m, "n0")
        with ExitStack() as inner:
            m.T = inner.enter_context(nc.sbuf_tensor("T1", [P, 2, ROWS], F32))
            batch_normed(nc, m)
        layer_norm(nc, m, "n1")
        graph_attention(nc, m, io)
        layer_norm(nc, m, "n2")
        with ExitStack() as inner:
            m.T = inner.enter_context(nc.sbuf_tensor("T3", [P, 2, ROWS], F32))
            two_products(nc, m, "l3", False)
            skip_lstms(nc, m, io)
            turn_and_add(nc, m)
        layer_norm(nc, m, "n3", out)


WEIGHTS = dict(l0_w1=[2, P], l0_w2=[1, D], l0_b1=[1], l0_b2=[D], eye=[P],
               l1_w1=[2, 512], l1_w2=[4, D], l1_b=[6], l1_g=[6], l1_be=[6],
               l3_w0=[2, D], l3_w1=[2, D], l3_b0=[2], l3_b1=[D],
               l2_wqv=[2, 2 * D], l2_wo=[2, D], l2_a=[2, HEADS], l2_nodes=[N], l2_node=[1])


def kernel(**inputs):
    import numpy as np
    import concourse.bacc as bacc
    from concourse.bass_utils import run_bass_kernel_spmd

    a = {k: np.asarray(v) for k, v in inputs.items()}

    def chunks(w):
        return w.reshape(-1, P, w.shape[-1]).transpose(1, 0, 2)

    def column(b):
        return b.reshape(-1, P).T

    def everywhere(b):
        return np.broadcast_to(b, (P,) + b.shape)

    head_vectors = np.zeros((D, HEADS), np.float32)
    for h in range(HEADS):
        head_vectors[h * N:(h + 1) * N, h] = a["L2_gnn_a"][h]
    head_vectors = chunks(head_vectors)

    given = dict(
        adj=a["adj"], adj_t=a["adj"].T, tables=constant_tables(), x=a["x"].reshape(ROWS, D),
        l0_w1=chunks(a["L0_gnn_W1"]), l0_w2=chunks(a["L0_gnn_W2"]), l0_b1=column(a["L0_gnn_b1"]),
        l0_b2=everywhere(a["L0_gnn_b2"]), eye=np.eye(P, dtype=np.float32),
        l1_w1=chunks(a["L1_gnn_W1"].T), l1_w2=chunks(a["L1_gnn_W2"].T),
        l3_w0=chunks(a["L3_gnn_Wg0"]), l3_w1=chunks(a["L3_gnn_Wg1"]), l3_b0=column(a["L3_gnn_bg0"]),
        l3_b1=everywhere(a["L3_gnn_bg1"]), l3_bih=column(a["L3_gnn_bih"]), l3_bhh=column(a["L3_gnn_bhh"]),
        l3_wih=a["L3_gnn_Wih"].reshape(4, 4 * D, 2, P).transpose(0, 3, 2, 1),
        l3_whh=a["L3_gnn_Whh"].reshape(4, 4 * D, 2, P).transpose(0, 3, 2, 1),
        l2_wqv=np.concatenate([chunks(a["L2_gnn_W_lin"].T), chunks(a["L2_gnn_W_val"].T)], 2),
        l2_wo=chunks(a["L2_gnn_W_out"].T), l2_a=head_vectors, adj_row=a["adj"].reshape(1, N * N),
        l2_nodes=everywhere(np.arange(N, dtype=np.float32)),
        l2_node=(np.arange(P) % N).astype(np.float32)[:, None],
        edge_ends=np.stack([a[k].reshape(EC, P).T for k in ("L2_gnn_src", "L2_gnn_dst")], 1),
        edge_rows=everywhere(np.stack([a["L2_gnn_src"], a["L2_gnn_dst"]])),
        l1_b=column(np.concatenate([a["L1_gnn_b1"], a["L1_gnn_b2"]])),
        l1_g=column(np.concatenate([a["L1_gnn_g1"], a["L1_gnn_g2"]])),
        l1_be=column(np.concatenate([a["L1_gnn_be1"], a["L1_gnn_be2"]])),
    )
    nc = bacc.Bacc("TRN2", target_bir_lowering=False, num_devices=1)
    io, arrays = {}, {}
    for name, v in given.items():
        v = np.ascontiguousarray(v)
        arrays[f"in_{name}"] = v
        io[name] = nc.dram_tensor(f"in_{name}", v.shape, mybir.dt.from_np(v.dtype), kind="ExternalInput").ap()
    out = nc.dram_tensor("out", (ROWS, D), F32, kind="ExternalOutput").ap()
    program(nc, io, out)
    r = run_bass_kernel_spmd(nc, [arrays], core_ids=[0])
    return r.results[0]["out"].reshape(a["x"].shape)
```

```python
from contextlib import ExitStack, contextmanager

import concourse.bass as bass
from concourse import mybir

F32 = mybir.dt.float32
BF16 = mybir.dt.bfloat16
I32 = mybir.dt.int32
ALU = mybir.AluOpType
ACT = mybir.ActivationFunctionType
AX = mybir.AxisListType.X

P = 128
N = 64
D = 256
LEVELS = 6
LEVEL_STEPS = 87
NEWTON = 14
TIE = 2.0 ** -30
BIG = 1e30
ROOT2 = 2.0 ** 0.5


class Chain:

    def __init__(self, eng, sem, entries):
        self.eng, self.sem, self.entries, self.n, self.turns = eng, sem, entries, 0, 0

    def go(self, ins):
        ins.then_inc(self.sem, 1)
        self.n += 1

    def link(self, ins):
        self.go(ins)
        self.eng.wait_ge(self.sem, self.turns + self.n)

    @contextmanager
    def loop(self, count, per_turn, start=0):
        at, outer = self.n, self.turns
        self.eng.sem_inc(self.entries, 1)
        with self.eng.Fori(start, start + count) as i:
            self.turns = outer + (i - start) * per_turn
            yield i
            assert self.n - at == per_turn, (self.n - at, per_turn)
        self.n, self.turns = at + count * per_turn, outer


TABLES = dict(eye=N, not_eye=N, below=N, first=N, from_first=N, tie=N, sub=N, sup=N, same=LEVELS * N, last=LEVELS * N, head=LEVELS * N,
              headcol=LEVELS)


def table_slices():
    at, out = 0, {}
    for name, w in TABLES.items():
        out[name] = (at, at + w)
        at += w
    return out, at


def constant_tables():
    import numpy as np
    p = np.arange(N)[:, None]
    c = np.arange(N)[None, :]
    parts = dict(eye=p == c, not_eye=p != c, below=p > c + 1, first=p == c + 1, from_first=p > c, tie=(c - p) * TIE, sub=c == p - 1, sup=c == p + 1)
    parts["same"] = np.concatenate([p // (2 << l) == c // (2 << l) for l in range(LEVELS)], 1)
    parts["last"] = np.concatenate([(c % (2 << l) == (1 << l) - 1) + 0 * p for l in range(LEVELS)], 1)
    parts["head"] = np.concatenate([(c % (2 << l) == (1 << l)) + 0 * p for l in range(LEVELS)], 1)
    parts["headcol"] = np.concatenate([p % (2 << l) == (1 << l) for l in range(LEVELS)], 1)
    return np.concatenate([parts[k].astype(np.float32) for k in TABLES], 1)


class Mem:

    def __init__(self, nc, ctx):
        self.nc, self.ctx = nc, ctx
        self.ps = ctx.enter_context(nc.psum_tensor("ps", [P, 8 * 512], F32))

    def sb(self, name, shape, dt=F32):
        return self.ctx.enter_context(self.nc.sbuf_tensor(name, shape, dt))

    def sem(self, name):
        return self.ctx.enter_context(self.nc.semaphore(name))


def scope(nc, ctx):
    held = []

    def sb(name, shape, dt=F32):
        return ctx.enter_context(nc.sbuf_tensor(name, shape, dt))

    def sem(name):
        held.append(ctx.enter_context(nc.semaphore(name)))
        return held[-1]

    def clear():
        with nc.Block() as block:
            @block.gpsimd
            def _(pool):
                for s in held:
                    pool.sem_clear(s)

    sem.clear = clear
    return sb, sem


def spectral_basis(nc, m, io):
    with ExitStack() as ctx:
        sb, sem = scope(nc, ctx)
        at, width = table_slices()
        tab = sb("tab", [N, width])
        T = {k: tab[:, a:b] for k, (a, b) in at.items()}
        eye = T["eye"]
        adj2 = sb("adj2", [N, 2, N])
        ones = sb("ones", [N, P])
        mat = sb("mat", [N, 3 * N])
        low = sb("low", [N, 2 * N])
        col = sb("col", [N, 64])
        row = sb("row", [1, 6 * N])
        vt = sb("vt", [N, N])
        sgn_row = sb("sgn_row", [N, N])
        W4 = sb("W4", [N, 4 * N])
        heads, rhos, pick = sb("heads", [N, LEVELS]), sb("rhos", [N, LEVELS]), sb("pick", [N, LEVELS, N])
        big = [sb(f"big{i}", [N, N]) for i in range(14)]
        dup = sb("dup", [N, 2 * P])
        ps = m.ps
        tables_in = sem("tables_in")
        adj_in = sem("adj_in")
        bd_zero = sem("bd_zero")
        bd_adj_in = sem("bd_adj_in")
        dve_step = sem("eig_dve_step")
        sqrt_in, sqrt_out = sem("sqrt_in"), sem("sqrt_out")
        turn_in, turn_out = sem("turn_in"), sem("turn_out")
        parts_in, square_out, sums_out = sem("parts_in"), sem("square_out"), sem("sums_out")
        v_in, prods_out = sem("v_in"), sem("prods_out")
        rows_in, update_out = sem("rows_in"), sem("update_out")
        sq2_in, sq2_out = sem("sq2_in"), sem("sq2_out")
        pe_turns = sem("pe_turns")
        dve_turns = sem("dve_turns")
        reflectors = N - 2

        def c(i, w=1):
            return col[:, i:i + w]

        with nc.Block() as block:

            @block.sync
            def _(sp):
                sp.dma_start(tab[:, :], io["tables"]).then_inc(tables_in, 16)
                sp.dma_start(adj2[:, 0, :], io["adj"]).then_inc(adj_in, 16)
                sp.dma_start(adj2[:, 1, :], io["adj_t"]).then_inc(adj_in, 16)
                sp.wait_ge(bd_zero, 1)
                for h in range(2):
                    sp.dma_start(m.bd_adj[h * N:(h + 1) * N, h * N:(h + 1) * N], io["adj_t"]).then_inc(bd_adj_in, 16)
                sp.wait_ge(bd_adj_in, 32)

            @block.gpsimd
            def _(pool):
                pool.memset(m.bd_adj[:, :], 0.0).then_inc(bd_zero, 1)
                pool.memset(m.bd_u[:, :], 0.0).then_inc(bd_zero, 1)
                pool.memset(m.bd_ut[:, :], 0.0).then_inc(bd_zero, 1)
                pool.memset(m.bd_hat[:, :], 0.0).then_inc(bd_zero, 1)

            @block.scalar
            def _(act):
                act.wait_ge(sqrt_in, 1)
                act.activation(c(4, 2), c(2, 2), ACT.Sqrt).then_inc(sqrt_out, 1)
                with act.Fori(0, reflectors) as k:
                    act.wait_ge(square_out, k + 1)
                    act.activation(c(7), ps[0:N, 1536:1537], ACT.Sqrt).then_inc(sqrt_out, 1)
                with act.Fori(0, LEVELS) as l:
                    act.wait_ge(sq2_in, l * 2 + 1)
                    act.activation(c(59), c(58), ACT.Sqrt).then_inc(sq2_out, 1)
                    act.wait_ge(sq2_in, l * 2 + 2)
                    act.activation(c(59), c(58), ACT.Sqrt).then_inc(sq2_out, 1)

            @block.tensor
            def _(pe):
                pe.wait_ge(tables_in, 16)
                pe.wait_ge(turn_in, 1)
                pe.matmul(ps[:, 0:N], dup[:, 0:P], eye, start=True, stop=True)
                pe.matmul(ps[:, 512:512 + N], dup[:, P:2 * P], eye, start=True, stop=True).then_inc(turn_out, 1)
                with pe.Fori(0, reflectors) as k:
                    pe.wait_ge(parts_in, k + 1)
                    pe.matmul(ps[:, 1536:1537], ones[:, :], c(10), start=True, stop=True).then_inc(square_out, 1)
                    pe.matmul(ps[:, 0:2], ones[:, :], c(11, 2), start=True, stop=True).then_inc(sums_out, 1)
                    pe.wait_ge(v_in, k + 1)
                    pe.sem_inc(pe_turns, 1)
                    pe.matmul(ps[0:1, 512:512 + 3 * N], c(13), mat[:, :], start=True, stop=True).then_inc(prods_out, 1)
                    pe.wait_ge(rows_in, k + 1)
                    pe.sem_inc(pe_turns, 1)
                    pe.matmul(ps[0:N, 1024:1024 + 2 * N], row[:, 0:N], row[:, N:3 * N], start=True, stop=False)
                    pe.matmul(ps[0:N, 1024:1024 + N], row[:, N:2 * N], row[:, 0:N], start=False, stop=True)\
                        .then_inc(update_out, 1)
                pe.wait_ge(turn_in, 2)
                pe.matmul(ps[0:N, 0:N], ones[:, 0:N], low[:, 0:N], start=True, stop=True)
                for l in range(LEVELS):
                    mm = pe.matmul(ps[0:N, 512 + l:513 + l], T["same"][:, l * N:(l + 1) * N], heads[:, l:l + 1],
                                   start=True, stop=True)
                mm.then_inc(turn_out, 1)
                with pe.Fori(0, LEVELS) as l:
                    pe.wait_ge(turn_in, l * 4 + 3)
                    pe.matmul(ps[:, 512:512 + 2 * N], ones[:, :], W4[:, 0:2 * N], start=True, stop=True)\
                        .then_inc(turn_out, 1)
                    pe.wait_ge(turn_in, l * 4 + 4)
                    pe.matmul(ps[:, 1024:1024 + 3 * N], ones[:, :], W4[:, N:4 * N], start=True, stop=True)\
                        .then_inc(turn_out, 1)
                    pe.wait_ge(turn_in, l * 4 + 5)
                    pe.sem_inc(pe_turns, 1)
                    pe.matmul(ps[0:N, 0:N], big[8][:, :], eye, start=True, stop=True)
                    pe.matmul(ps[0:N, 512:512 + N], big[9][:, :], eye, start=True, stop=True).then_inc(turn_out, 1)
                    pe.wait_ge(turn_in, l * 4 + 6)
                    pe.sem_inc(pe_turns, 1)
                    pe.matmul(ps[0:N, 1024:1024 + N], big[10][:, :], vt[:, :], start=True, stop=True)\
                        .then_inc(turn_out, 1)
                pe.wait_ge(turn_in, 4 * LEVELS + 3)
                pe.matmul(ps[0:N, 0:N], vt[:, :], eye, start=True, stop=True).then_inc(turn_out, 1)
                pe.wait_ge(turn_in, 4 * LEVELS + 4)
                pe.matmul(ps[:, 512:512 + N], dup[:, 0:P], big[0][:, :], start=True, stop=True)
                pe.matmul(ps[:, 1024:1024 + N], dup[:, P:2 * P], mat[:, N:2 * N], start=True, stop=True)\
                    .then_inc(turn_out, 1)

            @block.vector
            def _(dve):
                ch = Chain(dve, dve_step, dve_turns)
                link, go = ch.link, ch.go
                tt, ts, stt = dve.tensor_tensor, dve.tensor_scalar, dve.scalar_tensor_tensor
                A = mat[:, 0:N]

                dve.wait_ge(tables_in, 16)
                dve.wait_ge(adj_in, 32)
                link(dve.memset(ones[:, :], 1.0))
                link(dve.memset(col[:, :], 0.0))
                link(dve.tensor_reduce(c(0), adj2[:, :, :], mybir.AxisListType.XY, ALU.add))
                link(tt(big[0][:, :], adj2[:, 0, :], eye, ALU.mult))
                link(dve.tensor_reduce(c(1), big[0][:, :], AX, ALU.add))
                link(tt(c(2), c(0), c(1), ALU.subtract))
                link(ts(c(3), c(2), 1.0, None, ALU.add))
                link(dve.tensor_copy(c(0), c(2)))
                link(ts(c(1), c(2), 0.0, None, ALU.is_gt))
                ts(c(2), c(2), 1e-30, None, ALU.max).then_inc(sqrt_in, 1)
                dve.wait_ge(sqrt_out, 1)
                link(dve.reciprocal(c(4, 2), c(4, 2)))
                link(tt(c(4), c(4), c(1), ALU.mult))
                link(tt(big[1][:, :], adj2[:, 0, :], adj2[:, 1, :], ALU.add))
                link(ts(big[2][:, :], eye, c(0), None, ALU.mult))
                link(stt(big[1][:, :], big[1][:, :], -0.5, big[2][:, :], ALU.mult, ALU.add))
                link(tt(big[3][:, :], adj2[:, 0, :], eye, ALU.add))
                for h in range(2):
                    link(ts(dup[:, h * N:(h + 1) * N], big[1][:, :], c(4), None, ALU.mult))
                link(ts(dup[:, P:P + N], big[3][:, :], c(5), None, ALU.mult))
                dve.tensor_copy(dup[:, P + N:2 * P], dup[:, P:P + N]).then_inc(turn_in, 1)
                dve.wait_ge(turn_out, 1)
                link(ts(A, ps[0:N, 0:N], c(4), None, ALU.mult))
                link(dve.tensor_copy(mat[:, N:2 * N], eye))
                link(dve.tensor_copy(mat[:, 2 * N:3 * N], eye))
                dve.wait_ge(bd_zero, 4)
                link(ts(m.bd_hat[0:N, 0:N], ps[0:N, 512:512 + N], c(5), None, ALU.mult))
                link(dve.tensor_copy(m.root_deg2[0:N, :], c(5)))
                link(dve.tensor_copy(m.root_deg2[N:P, :], c(5)))
                link(ts(m.bd_hat[N:P, N:P], ps[N:P, 512:512 + N], m.root_deg2[N:P, :], None, ALU.mult))

                alpha, below_sq = ps[0:N, 0:1], ps[0:N, 1:2]
                x, v, tau, some, none, sign = c(9), c(13), c(14), c(16), c(17), c(18)
                size, length, diff, inv_diff, inv_beta, factor = c(19), c(20), c(21), c(22), c(23), c(24)
                row_v, row_w, row_q, row_p = (row[:, i * N:(i + 1) * N] for i in range(4))
                with ch.loop(reflectors, 19) as k:
                    below, first = T["below"][:, bass.ds(k, 1)], T["first"][:, bass.ds(k, 1)]
                    from_first = T["from_first"][:, bass.ds(k, 1)]
                    a_k = A[:, bass.ds(k, 1)]
                    stt(c(10), a_k, from_first, a_k, ALU.mult, ALU.mult)
                    tt(c(11), a_k, first, ALU.mult)
                    stt(c(12), a_k, below, a_k, ALU.mult, ALU.mult).then_inc(parts_in, 1)
                    go(tt(x, a_k, below, ALU.mult))
                    dve.wait_ge(sums_out, k + 1)
                    go(ts(some, below_sq, 0.0, None, ALU.is_gt))
                    go(ts(none, below_sq, 0.0, None, ALU.is_le))
                    go(ts(sign, alpha, 0.0, 2.0, ALU.is_ge, ALU.mult))
                    link(ts(size, alpha, -1.0, None, ALU.mult))
                    go(ts(sign, sign, -1.0, None, ALU.add))
                    go(tt(size, size, alpha, ALU.max))
                    dve.wait_ge(sqrt_out, k + 2)
                    link(tt(length, c(7), none, ALU.add))
                    link(stt(diff, length, size, sign, ALU.add, ALU.mult))
                    link(nc.vector.reciprocal(inv_diff, diff))
                    stt(v, x, inv_diff, first, ALU.mult, ALU.add).then_inc(v_in, 1)
                    link(nc.vector.reciprocal(inv_beta, length))
                    link(stt(tau, inv_beta, sign, diff, ALU.mult, ALU.mult))
                    link(tt(tau, tau, some, ALU.mult))
                    link(ts(factor, tau, tau, -0.5, ALU.mult, ALU.mult))
                    dve.wait_ge(prods_out, k + 1)
                    link(dve.tensor_copy(row_v, ps[0:1, 512 + 2 * N:512 + 3 * N]))
                    go(ts(row_p, ps[0:1, 512:512 + N], tau[0:1, :], None, ALU.mult))
                    go(ts(row_q, ps[0:1, 512 + N:512 + 2 * N], tau[0:1, :], None, ALU.mult))
                    link(dve.tensor_tensor_reduce(row[:, 4 * N:5 * N], ps[0:1, 512:512 + N], row_v, factor[0:1, :],
                                                  0.0, ALU.mult, ALU.add, row[:, 5 * N:5 * N + 1]))
                    stt(row_w, row_v, row[:, 5 * N:5 * N + 1], row_p, ALU.mult, ALU.add).then_inc(rows_in, 1)
                    dve.wait_ge(update_out, k + 1)
                    link(tt(mat[:, 0:2 * N], mat[:, 0:2 * N], ps[0:N, 1024:1024 + 2 * N], ALU.subtract))

                link(tt(big[0][:, :], A, eye, ALU.mult))
                link(tt(big[1][:, :], A, T["sub"], ALU.mult))
                link(tt(big[2][:, :], A, T["sup"], ALU.mult))
                link(dve.tensor_reduce(c(0), big[0][:, :], AX, ALU.add))
                link(dve.tensor_reduce(c(1), big[1][:, :], AX, ALU.add))
                link(dve.tensor_reduce(c(3), big[2][:, :], AX, ALU.add))
                link(stt(c(2), c(1), -1.0, c(1), ALU.mult, ALU.max))
                link(stt(c(3), c(3), -1.0, c(3), ALU.mult, ALU.max))
                link(tt(c(0), c(0), c(2), ALU.subtract))
                link(tt(c(0), c(0), c(3), ALU.subtract))
                link(ts(c(4), c(1), 0.0, None, ALU.is_ge))
                link(ts(c(4), c(4), 2.0, -1.0, ALU.mult, ALU.add))
                link(tt(heads[:, :], T["headcol"], c(2).broadcast_to([N, LEVELS]), ALU.mult))
                ts(low[:, 0:N], eye, c(4), None, ALU.mult).then_inc(turn_in, 1)
                dve.wait_ge(turn_out, 2)
                link(dve.tensor_copy(sgn_row[:, :], ps[0:N, 0:N]))
                link(dve.tensor_copy(rhos[:, :], ps[0:N, 512:512 + LEVELS]))
                link(tt(pick[:, :, :], T["head"].rearrange("p (l n) -> p l n", n=N),
                        sgn_row[:, None, :].broadcast_to([N, LEVELS, N]), ALU.mult))
                link(tt(pick[:, :, :], T["last"].rearrange("p (l n) -> p l n", n=N), pick[:, :, :], ALU.add))
                link(dve.tensor_copy(vt[:, :], eye))

                d, rho, z, abs_z, abs_d, nd, w, zr, mass = (c(i) for i in (0, 8, 28, 29, 30, 31, 32, 33, 34))
                largest, tol, gap, top, ntop, total, hi, half, value = (c(i) for i in range(35, 44))
                neg, right, start, both, shift, mu, own, s0, s1 = (c(i) for i in range(44, 53))
                num, den, z_next, close, keep, square, root, sq2, len2 = (c(i) for i in range(53, 62))
                same, off, part, off1, pad, wts, rest, tmp, fac, inv, new, z_row, origin, tmp2 = (
                    b[:, :] for b in big[0:14])
                with ch.loop(LEVELS, LEVEL_STEPS + 9 * NEWTON) as l:
                    go(tt(W4[:, 0:N], eye, d.broadcast_to([N, N]), ALU.mult))
                    go(stt(abs_d, d, -1.0, d, ALU.mult, ALU.max))
                    go(dve.tensor_copy(rho, rhos[:, bass.ds(l, 1)]))
                    go(dve.tensor_copy(same, T["same"][:, bass.ds(l * N, N)]))
                    link(tt(tmp, pick[:, bass.ds(l, 1), :], vt[:, :], ALU.mult))
                    link(dve.tensor_reduce(z, tmp, AX, ALU.add))
                    link(stt(abs_z, z, -1.0, z, ALU.mult, ALU.max))
                    link(stt(mass, abs_z, 1.0 / ROOT2, abs_d, ALU.mult, ALU.max))
                    ts(W4[:, N:2 * N], eye, mass, None, ALU.mult).then_inc(turn_in, 1)
                    go(tt(zr, abs_z, rho, ALU.mult))
                    link(tt(w, z, z, ALU.mult))
                    link(tt(w, w, rho, ALU.mult))
                    dve.wait_ge(turn_out, l * 4 + 3)
                    go(ts(off, ps[0:N, 512:512 + N], d, None, ALU.subtract))
                    link(dve.tensor_tensor_reduce(tmp2, ps[0:N, 512 + N:512 + 2 * N], same, 1.0, 0.0,
                                                  ALU.mult, ALU.max, largest))
                    link(ts(nd, zr, ROOT2 * 2.0 ** 21, largest, ALU.mult, ALU.is_gt))
                    go(ts(W4[:, N:2 * N], eye, z, nd, ALU.mult, ALU.mult))
                    go(ts(W4[:, 2 * N:3 * N], eye, nd, None, ALU.mult))
                    link(ts(W4[:, 3 * N:4 * N], eye, w, nd, ALU.mult, ALU.mult))
                    tt(z, z, nd, ALU.mult).then_inc(turn_in, 1)
                    go(stt(tmp, off, -1.0, off, ALU.mult, ALU.max))
                    link(tt(tmp2, T["tie"], off, ALU.subtract))
                    link(stt(tmp, tmp, TIE, tmp2, ALU.is_lt, ALU.mult))
                    link(tt(off, off, tmp, ALU.add))
                    dve.wait_ge(turn_out, l * 4 + 4)
                    link(tt(part, ps[0:N, 1024 + N:1024 + 2 * N], same, ALU.mult))
                    go(dve.tensor_tensor_reduce(wts, ps[0:N, 1024 + 2 * N:1024 + 3 * N], same, 1.0, 0.0,
                                                ALU.mult, ALU.add, total))
                    go(ts(pad, part, -4.0, 4.0, ALU.mult, ALU.add))
                    go(dve.tensor_copy(z_row, ps[0:N, 1024:1024 + N]))
                    link(tt(off1, off, part, ALU.mult))
                    go(tt(off, off1, pad, ALU.add))
                    link(ts(tmp, off1, 0.0, BIG, ALU.is_le, ALU.mult))
                    go(ts(tol, largest, 8 * 2.0 ** -24, None, ALU.mult))
                    link(dve.tensor_tensor_reduce(tmp2, off1, tmp, 1.0, BIG, ALU.add, ALU.min, gap))
                    go(ts(ntop, gap, BIG / 2, None, ALU.is_le))
                    link(ts(top, gap, BIG / 2, None, ALU.is_gt))
                    link(tt(total, total, top, ALU.mult))
                    link(stt(hi, gap, ntop, total, ALU.mult, ALU.add))
                    link(ts(half, hi, 0.5, None, ALU.mult))
                    link(ts(tmp, off, half, None, ALU.subtract))
                    link(dve.reciprocal(tmp2, tmp))
                    link(dve.tensor_tensor_reduce(tmp, tmp2, wts, 1.0, 0.0, ALU.mult, ALU.add, value))
                    link(ts(neg, value, -1.0, None, ALU.is_lt))
                    go(tt(both, neg, top, ALU.mult))
                    link(tt(right, neg, ntop, ALU.mult))
                    go(tt(shift, right, hi, ALU.mult))
                    link(stt(start, right, -2.0, both, ALU.mult, ALU.add))
                    go(stt(mu, start, 1.0, half, ALU.add, ALU.mult))
                    link(ts(origin, off, shift, None, ALU.subtract))
                    link(stt(tmp, origin, 0.0, part, ALU.is_equal, ALU.mult))
                    link(dve.tensor_tensor_reduce(tmp2, wts, tmp, 1.0, 0.0, ALU.mult, ALU.add, own))
                    link(tt(rest, wts, tmp2, ALU.subtract))
                    with ch.loop(NEWTON, 9) as _:
                        link(ts(tmp, origin, mu, None, ALU.subtract))
                        link(dve.reciprocal(tmp2, tmp))
                        link(stt(fac, tmp2, 1.0, rest, ALU.mult, ALU.mult, accum_out=s0))
                        link(stt(tmp, fac, 1.0, tmp2, ALU.mult, ALU.mult, accum_out=s1))
                        link(tt(s1, s1, mu, ALU.mult))
                        go(stt(num, s1, mu, own, ALU.mult, ALU.add))
                        link(stt(den, s0, 1.0, s1, ALU.add, ALU.add))
                        link(dve.reciprocal(den, den))
                        link(tt(mu, num, den, ALU.mult))
                    link(ts(mu, mu, -BIG, BIG, ALU.max, ALU.min))
                    link(ts(tmp, origin, mu, None, ALU.subtract))
                    go(tt(rest, T["not_eye"], off, ALU.mult))
                    link(ts(tmp2, tmp, 0.0, 1e-20, ALU.is_equal, ALU.mult))
                    go(ts(part, part, nd, None, ALU.mult))
                    link(tt(rest, rest, eye, ALU.subtract))
                    link(tt(tmp, tmp, tmp2, ALU.add))
                    go(dve.reciprocal(inv, tmp))
                    go(ts(tmp2, part, -1.0, 1.0, ALU.mult, ALU.add))
                    link(dve.reciprocal(wts, rest))
                    link(tt(fac, wts, tmp, ALU.mult))
                    link(tt(fac, fac, part, ALU.mult))
                    tt(fac, fac, tmp2, ALU.add).then_inc(turn_in, 1)
                    go(ts(keep, nd, -1.0, 1.0, ALU.mult, ALU.add))
                    link(ts(wts, off, gap, None, ALU.is_equal))
                    go(ts(rest, eye, keep, None, ALU.mult))
                    link(dve.tensor_tensor_reduce(off1, wts, z_row, 1.0, 0.0, ALU.mult, ALU.add, z_next))
                    go(tt(close, z_next, z, ALU.mult))
                    link(tt(s0, z_next, z_next, ALU.mult))
                    go(ts(keep, close, 0.0, -2.0, ALU.is_gt, ALU.mult))
                    go(tt(close, close, hi, ALU.mult))
                    link(stt(s0, z, z, s0, ALU.mult, ALU.add))
                    go(tt(keep, keep, ntop, ALU.mult))
                    link(tt(s0, s0, tol, ALU.mult))
                    link(tt(close, close, s0, ALU.is_le))
                    go(tt(keep, keep, nd, ALU.mult))
                    go(ts(sq2, z, 0.0, 2.0, ALU.is_ge, ALU.mult))
                    link(tt(s1, shift, mu, ALU.add))
                    go(ts(sq2, sq2, -1.0, None, ALU.add))
                    go(tt(s1, s1, nd, ALU.mult))
                    link(tt(keep, keep, close, ALU.mult))
                    go(tt(d, d, s1, ALU.add))
                    link(ts(keep, keep, 1.0, None, ALU.add))
                    dve.wait_ge(turn_out, l * 4 + 5)
                    link(dve.tensor_reduce(square, ps[0:N, 0:N], AX, ALU.mult))
                    link(stt(square, square, -1.0, square, ALU.mult, ALU.max))
                    ts(square, square, 1e-30, None, ALU.max).then_inc(sq2_in, 1)
                    link(tt(tmp, ps[0:N, 512:512 + N], part, ALU.mult))
                    dve.wait_ge(sq2_out, l * 2 + 1)
                    link(tt(sq2, sq2, root, ALU.mult))
                    stt(new, tmp, sq2, rest, ALU.mult, ALU.add).then_inc(turn_in, 1)
                    dve.wait_ge(turn_out, l * 4 + 6)
                    link(dve.tensor_copy(vt[:, :], ps[0:N, 1024:1024 + N]))
                    dve.tensor_tensor_reduce(tmp, vt[:, :], vt[:, :], 1.0, 0.0, ALU.mult, ALU.add, square)\
                        .then_inc(sq2_in, 1)
                    dve.wait_ge(sq2_out, l * 2 + 2)
                    link(dve.reciprocal(len2, root))
                    link(ts(vt[:, :], vt[:, :], len2, keep, ALU.mult, ALU.mult))

                dve.tensor_copy(dup[:, 0:N], mat[:, N:2 * N]).then_inc(turn_in, 1)
                dve.wait_ge(turn_out, 4 * LEVELS + 3)
                link(dve.tensor_copy(big[0][:, :], ps[0:N, 0:N]))
                link(dve.tensor_copy(dup[:, N:2 * N], mat[:, N:2 * N]))
                link(dve.tensor_copy(dup[:, P:P + N], big[0][:, :]))
                dve.tensor_copy(dup[:, P + N:2 * P], big[0][:, :]).then_inc(turn_in, 1)
                dve.wait_ge(turn_out, 4 * LEVELS + 4)
                for h in range(2):
                    q = slice(h * N, (h + 1) * N)
                    link(dve.tensor_copy(m.bd_u[q, q], ps[q, 512:512 + N]))
                    link(dve.tensor_copy(m.bd_ut[q, q], ps[q, 1024:1024 + N]))
        sem.clear()


G = 4
GROUPS = 16
TILES = G * GROUPS
ROWS = TILES * P
GR = G * P
EPS = 1e-5


def inverse_root(nc, link, inv, root, square, corr):
    link(nc.vector.reciprocal(inv, root))
    link(nc.vector.tensor_tensor(corr, inv, inv, ALU.mult))
    link(nc.vector.tensor_tensor(corr, corr, square, ALU.mult))
    link(nc.vector.tensor_scalar(corr, corr, -0.5, 1.5, ALU.mult, ALU.add))
    link(nc.vector.tensor_tensor(inv, inv, corr, ALU.mult))


def row_statistics(nc, ch, m, stat, first_tile, tiles):
    ch.eng.sem_inc(ch.entries, 1)
    for t in range(tiles):
        nc.vector.bn_stats(stat[:, t, 0:6], m.X[:, bass.ds(first_tile + t, 1), :]).then_inc(ch.sem, 1)
    ch.n += tiles
    ch.eng.wait_ge(ch.sem, ch.turns + ch.n)
    ch.eng.sem_inc(ch.entries, 1)
    for t in range(tiles):
        nc.vector.bn_aggr(stat[:, t, 6:8], stat[:, t, 0:6]).then_inc(ch.sem, 1)
    ch.n += tiles
    ch.eng.wait_ge(ch.sem, ch.turns + ch.n)
    ch.link(nc.vector.tensor_copy(m.mv[:, bass.ds(first_tile, tiles), :], stat[:, 0:tiles, 6:8]))


def layer_norm(nc, m, tag, out=None):
    with ExitStack() as ctx:
        sb, sem = scope(nc, ctx)
        var, root, inv, corr, shift = (sb(f"{tag}_{k}", [P, TILES]) for k in ("var", "root", "inv", "corr", "shift"))
        step, turns = sem(f"{tag}_step"), sem(f"{tag}_turns")
        var_in, root_out, scales_out = sem(f"{tag}_var_in"), sem(f"{tag}_root_out"), sem(f"{tag}_scales_out")
        even_done, odd_done, stored = sem(f"{tag}_even_done"), sem(f"{tag}_odd_done"), sem(f"{tag}_stored")
        with nc.Block() as block:

            @block.vector
            def _(dve):
                link = Chain(dve, step, turns).link
                nc.vector.tensor_scalar(var[:, :], m.mv[:, :, 1], EPS, None, ALU.add).then_inc(var_in, 1)
                dve.wait_ge(root_out, 1)
                inverse_root(nc, link, inv[:, :], root[:, :], var[:, :], corr[:, :])
                nc.vector.scalar_tensor_tensor(shift[:, :], m.mv[:, :, 0], -1.0, inv[:, :], ALU.mult, ALU.mult)\
                    .then_inc(scales_out, 1)
                with dve.Fori(0, TILES // 2) as i:
                    x = m.X[:, bass.ds(i * 2, 1), :]
                    nc.vector.tensor_scalar(x, x, m.mv[:, bass.ds(i * 2, 1), 0], inv[:, bass.ds(i * 2, 1)],
                                            ALU.subtract, ALU.mult).then_inc(even_done, 1)

            @block.scalar
            def _(act):
                act.wait_ge(var_in, 1)
                nc.scalar.activation(root[:, :], var[:, :], ACT.Sqrt).then_inc(root_out, 1)
                act.wait_ge(scales_out, 1)
                with act.Fori(0, TILES // 2) as i:
                    x = m.X[:, bass.ds(i * 2 + 1, 1), :]
                    nc.scalar.activation(x, x, ACT.Identity, bias=shift[:, bass.ds(i * 2 + 1, 1)],
                                         scale=inv[:, bass.ds(i * 2 + 1, 1)]).then_inc(odd_done, 1)

            if out is not None:
                @block.sync
                def _(sp):
                    view = out.rearrange("(t p) d -> p t d", p=P)
                    with sp.Fori(0, TILES // 8) as i:
                        sp.wait_ge(even_done, i * 4 + 4)
                        sp.wait_ge(odd_done, i * 4 + 4)
                        sp.dma_start(view[:, bass.ds(i * 8, 8), :], m.X[:, bass.ds(i * 8, 8), :]).then_inc(stored, 16)
                    sp.wait_ge(stored, 16 * (TILES // 8))
        sem.clear()


def load_all(nc, m, io):
    m.weights_total = 16 * len(m.weights)
    with nc.Block() as block:

        @block.scalar
        def _(act):
            for k, v in m.weights.items():
                act.dma_start(v, io[k]).then_inc(m.weights_in, 16)

        @block.gpsimd
        def _(pool):
            rows = io["x"].rearrange("(t p) d -> p t d", p=P)
            for q in range(4):
                pool.dma_start(m.X[:, q * 16:(q + 1) * 16, :], rows[:, q * 16:(q + 1) * 16, :]).then_inc(m.x_in, 16)


def two_products(nc, m, tag, first):
    ps, w = m.ps, m.weights
    heads = 1 if first else 2
    mix_a = m.bd_u if first else m.bd_adj
    w1, w2 = (w["l0_w1"], w["l0_w2"]) if first else (w["l3_w0"], w["l3_w1"])
    b2 = w["l0_b2"] if first else w["l3_b1"]
    A_PS, B_PS, C_PS, D_PS = (ps[:, k * 1024:(k + 1) * 1024] for k in range(4))

    def chunked(bank):
        return bank.rearrange("p (c r) -> p c r", c=2)

    with ExitStack() as ctx:
        sb, sem = scope(nc, ctx)
        xs = sb(f"{tag}_xs", [P, G, D])
        agg = sb(f"{tag}_agg", [P, 2, GR])
        pre = sb(f"{tag}_pre", [P, 2, GR])
        hid = sb(f"{tag}_hid", [P, heads, GR])
        mid = sb(f"{tag}_mid", [P, G, D])
        stat = sb(f"{tag}_stat", [P, G, 8])
        sums = sb(f"{tag}_sums", [P, P])
        ones = sb(f"{tag}_ones", [P, P])
        xs_in, a_out, agg_in, b_out, pre_in, hid_in, c_out, mid_in, d_out, d_used = (
            sem(f"{tag}_{k}") for k in ("xs_in", "a_out", "agg_in", "b_out", "pre_in", "hid_in", "c_out", "mid_in",
                                        "d_out", "d_used"))
        ones_in, sums_out, sums_in = sem(f"{tag}_ones_in"), sem(f"{tag}_sums_out"), sem(f"{tag}_sums_in")
        step, turns = sem(f"{tag}_step"), sem(f"{tag}_turns")
        with nc.Block() as block:

            @block.gpsimd
            def _(pool):
                pool.wait_ge(m.x_in, 64)
                pool.tensor_copy(xs[:, :, :], m.X[:, 0:G, :]).then_inc(xs_in, 1)
                with pool.Fori(1, GROUPS) as i:
                    pool.wait_ge(a_out, i)
                    pool.tensor_copy(xs[:, :, :], m.X[:, bass.ds(i * G, G), :]).then_inc(xs_in, 1)

            @block.tensor
            def _(pe):
                pe.wait_ge(m.weights_in, m.weights_total)
                if not first:
                    pe.wait_ge(ones_in, 1)
                    pe.matmul(D_PS[:, 0:P], ones[:, :], m.bd_adj[:, :], start=True, stop=True).then_inc(sums_out, 1)
                    pe.wait_ge(sums_in, 1)

                def mix_in(i):
                    pe.wait_ge(xs_in, i + 1)
                    for c in range(2):
                        for t in range(G):
                            mm = pe.matmul(A_PS[:, c * GR + t * P:c * GR + (t + 1) * P],
                                           xs[:, t, c * P:(c + 1) * P], mix_a[:, :], start=True, stop=True)
                    mm.then_inc(a_out, 1)

                def weights_1(i):
                    pe.wait_ge(agg_in, i + 1)
                    for h in range(heads):
                        for k in range(2):
                            mm = pe.matmul(B_PS[:, h * GR:(h + 1) * GR], w1[:, k, h * P:(h + 1) * P], agg[:, k, :],
                                           start=k == 0, stop=k == 1)
                    mm.then_inc(b_out, 1)

                def weights_2(i):
                    pe.wait_ge(hid_in, i + 1)
                    for t in range(G):
                        for k in range(heads):
                            mm = pe.matmul(C_PS[:, t * D:(t + 1) * D], hid[:, k, t * P:(t + 1) * P], w2[:, k, :],
                                           start=k == 0, stop=k == heads - 1)
                    mm.then_inc(c_out, 1)

                def mix_out(i):
                    pe.wait_ge(mid_in, i + 1)
                    pe.wait_ge(d_used, i + 1)
                    if first:
                        for h in range(2):
                            mm = pe.matmul(D_PS[:, h * GR:(h + 1) * GR], m.bd_ut[:, :], mid[:, 2 * h:2 * h + 2, :],
                                           start=True, stop=True)
                    else:
                        for c in range(2):
                            for t in range(G):
                                mm = pe.matmul(D_PS[:, c * GR + t * P:c * GR + (t + 1) * P],
                                               mid[:, t, c * P:(c + 1) * P], m.bd_adj[:, :], start=True, stop=True)
                    mm.then_inc(d_out, 1)

                mix_in(0)
                weights_1(0)
                with pe.Fori(1, GROUPS) as i:
                    mix_in(i)
                    weights_2(i - 1)
                    weights_1(i)
                    mix_out(i - 1)
                weights_2(GROUPS - 1)
                mix_out(GROUPS - 1)

            @block.scalar
            def _(act):
                act.wait_ge(m.weights_in, m.weights_total)
                if not first:
                    act.sem_inc(d_used, 1)

                def copy_agg(i):
                    act.wait_ge(a_out, i + 1)
                    nc.scalar.copy(agg[:, :, :], chunked(A_PS)).then_inc(agg_in, 1)

                def relu(i):
                    if first:
                        act.wait_ge(b_out, i + 1)
                        nc.scalar.activation(hid[:, 0, :], B_PS[:, 0:GR], ACT.Relu, bias=w["l0_b1"][:, 0:1])\
                            .then_inc(hid_in, 1)
                    else:
                        act.wait_ge(pre_in, i + 1)
                        nc.scalar.activation(hid[:, :, :], pre[:, :, :], ACT.Relu).then_inc(hid_in, 1)

                def result(i):
                    act.wait_ge(d_out, i + 1)
                    nc.scalar.activation(m.T[:, :, bass.ds(i * GR, GR)], chunked(D_PS), ACT.Relu).then_inc(d_used, 1)

                copy_agg(0)
                relu(0)
                with act.Fori(1, GROUPS) as i:
                    copy_agg(i)
                    relu(i)
                    if not first:
                        result(i - 1)
                if not first:
                    result(GROUPS - 1)
                    act.wait_ge(d_used, GROUPS + 1)

            @block.vector
            def _(dve):
                ch = Chain(dve, step, turns)
                if first:
                    dve.sem_inc(d_used, 1)
                else:
                    nc.vector.memset(ones[:, :], 1.0).then_inc(ones_in, 1)
                    dve.wait_ge(sums_out, 1)
                    nc.vector.tensor_copy(sums[:, :], D_PS[:, 0:P]).then_inc(sums_in, 1)
                    dve.wait_ge(sums_in, 1)
                dve.wait_ge(m.weights_in, m.weights_total)

                def bias_1(i):
                    dve.wait_ge(b_out, i + 1)
                    for h in range(2):
                        ins = nc.vector.scalar_tensor_tensor(
                            pre[:, h, :].rearrange("p (t r) -> p t r", t=G), sums[:, None, :].broadcast_to([P, G, P]),
                            w["l3_b0"][:, h:h + 1], B_PS[:, h * GR:(h + 1) * GR].rearrange("p (t r) -> p t r", t=G),
                            ALU.mult, ALU.add)
                    ins.then_inc(pre_in, 1)

                def bias_2(i):
                    dve.wait_ge(c_out, i + 1)
                    nc.vector.tensor_tensor(mid[:, :, :], C_PS.rearrange("p (t d) -> p t d", t=G),
                                            b2[:, None, :].broadcast_to([P, G, D]), ALU.add).then_inc(mid_in, 1)

                def residual(i):
                    dve.wait_ge(d_out, i + 1)
                    x = m.X[:, bass.ds(i * G, G), :]
                    nc.vector.tensor_tensor(x, D_PS.rearrange("p (t d) -> p t d", t=G), x, ALU.add)\
                        .then_inc(d_used, 1)
                    dve.wait_ge(d_used, i + 2)
                    row_statistics(nc, ch, m, stat, i * G, G)

                if not first:
                    bias_1(0)
                with ch.loop(GROUPS - 1, 2 * G + 1 if first else 0, start=1) as i:
                    bias_2(i - 1)
                    if first:
                        residual(i - 1)
                    else:
                        bias_1(i)
                bias_2(GROUPS - 1)
                if first:
                    residual(GROUPS - 1)
        sem.clear()


def batch_normed(nc, m):
    ps, w, T = m.ps, m.weights, m.T
    HC = 4
    A_PS, C_PS = ps[:, 0:1024], ps[:, 0:1024]
    B_PS = ps[:, 1024:1024 + HC * GR]
    O_PS = [ps[:, 0:1024], ps[:, 1024:2048]]
    with ExitStack() as ctx:
        sb, sem = scope(nc, ctx)
        xs = sb("l1_xs", [P, G, D])
        hid = sb("l1_hid", [P, HC, GR])
        nrm = [sb(f"l1_nrm{s}", [P, 2, GR]) for s in range(2)]
        hstat = sb("l1_hstat", [P, HC, GROUPS, 6])
        ostat = sb("l1_ostat", [P, 2, GROUPS, 6])
        stat = sb("l1_stat", [P, G, 8])
        moments = sb("l1_moments", [P, HC + 2, 2])
        var, root, inv, corr, scale, mean, shift = (sb(f"l1_{k}", [P, HC + 2]) for k in
                                                    ("var", "root", "inv", "corr", "scale", "mean", "shift"))
        xs_in, a_out, agg_in, b_out, stats_in = (sem(f"l1_{k}") for k in ("xs_in", "a_out", "agg_in", "b_out",
                                                                          "stats_in"))
        b2_out, hid_in, c_out, out_in = (sem(f"l1_{k}") for k in ("b2_out", "hid_in", "c_out", "out_in"))
        nrm_in, turned, added = (sem(f"l1_{k}") for k in ("nrm_in", "turned", "added"))
        var_in, root_out, scales_in, ostat_in = (sem(f"l1_{k}") for k in ("var_in", "root_out", "scales_in",
                                                                          "ostat_in"))
        step, turns = sem("l1_step"), sem("l1_turns")
        with nc.Block() as block:

            @block.gpsimd
            def _(pool):
                pool.tensor_copy(xs[:, :, :], m.X[:, 0:G, :]).then_inc(xs_in, 1)
                with pool.Fori(1, GROUPS) as i:
                    pool.wait_ge(a_out, i)
                    pool.tensor_copy(xs[:, :, :], m.X[:, bass.ds(i * G, G), :]).then_inc(xs_in, 1)

            @block.tensor
            def _(pe):
                def mix(i):
                    pe.wait_ge(xs_in, i + 1)
                    for c in range(2):
                        for t in range(G):
                            mm = pe.matmul(A_PS[:, c * GR + t * P:c * GR + (t + 1) * P],
                                           xs[:, t, c * P:(c + 1) * P], m.bd_hat[:, :], start=True, stop=True)
                    mm.then_inc(a_out, 1)

                def hidden(i, done):
                    for h in range(HC):
                        if done is b_out:
                            pe.wait_ge(stats_in, i * HC + h + 1)
                        for k in range(2):
                            mm = pe.matmul(B_PS[:, h * GR:(h + 1) * GR], w["l1_w1"][:, k, h * P:(h + 1) * P],
                                           T[:, k, bass.ds(i * GR, GR)], start=k == 0, stop=k == 1)
                        mm.then_inc(done, 1)

                mix(0)
                with pe.Fori(1, GROUPS) as i:
                    pe.wait_ge(agg_in, i)
                    mix(i)
                    hidden(i - 1, b_out)
                pe.wait_ge(agg_in, GROUPS)
                hidden(GROUPS - 1, b_out)

                def output(i):
                    for k in range(HC):
                        if k == 0:
                            pe.wait_ge(out_in, i + 1)
                        for h in range(2):
                            pe.wait_ge(hid_in, i * HC + k + 1)
                            mm = pe.matmul(C_PS[:, h * GR:(h + 1) * GR], w["l1_w2"][:, k, h * P:(h + 1) * P],
                                           hid[:, k, :], start=k == 0, stop=k == HC - 1)
                    mm.then_inc(c_out, 1)

                pe.wait_ge(stats_in, GROUPS * HC + HC)
                hidden(0, b2_out)
                with pe.Fori(1, GROUPS) as i:
                    output(i - 1)
                    hidden(i, b2_out)
                output(GROUPS - 1)

                pe.wait_ge(out_in, GROUPS + 1)
                with pe.Fori(0, GROUPS // 2) as i:
                    for s in range(2):
                        pe.wait_ge(nrm_in, i * 2 + s + 1)
                        pe.wait_ge(added, i * 2 + s + 1)
                        for t in range(G):
                            for c in range(2):
                                mm = pe.transpose(O_PS[s][:, t * D + c * P:t * D + (c + 1) * P],
                                                  nrm[s][:, c, t * P:(t + 1) * P], w["eye"])
                        mm.then_inc(turned, 1)

            @block.scalar
            def _(act):
                with act.Fori(0, GROUPS) as i:
                    act.wait_ge(a_out, i + 1)
                    nc.scalar.copy(T[:, :, bass.ds(i * GR, GR)], A_PS.rearrange("p (c r) -> p c r", c=2))\
                        .then_inc(agg_in, 1)
                act.wait_ge(var_in, 1)
                nc.scalar.activation(root[:, 0:HC], var[:, 0:HC], ACT.Sqrt).then_inc(root_out, 1)
                act.wait_ge(scales_in, 1)
                with act.Fori(0, GROUPS) as i:
                    for h in range(HC):
                        act.wait_ge(b2_out, i * HC + h + 1)
                        nc.scalar.activation(hid[:, h, :], B_PS[:, h * GR:(h + 1) * GR], ACT.Relu,
                                             bias=shift[:, h:h + 1], scale=scale[:, h:h + 1]).then_inc(hid_in, 1)
                act.wait_ge(var_in, 2)
                nc.scalar.activation(root[:, HC:], var[:, HC:], ACT.Sqrt).then_inc(root_out, 1)
                act.wait_ge(scales_in, 2)

                def norm_out(i, s):
                    for c in range(2):
                        ins = nc.scalar.activation(nrm[s][:, c, :], T[:, c, bass.ds(i * GR, GR)], ACT.Identity,
                                                   bias=shift[:, HC + c:HC + c + 1], scale=scale[:, HC + c:HC + c + 1])
                    ins.then_inc(nrm_in, 1)

                norm_out(0, 0)
                norm_out(1, 1)
                with act.Fori(1, GROUPS // 2) as i:
                    for s in range(2):
                        act.wait_ge(turned, i * 2 + s - 1)
                        norm_out(i * 2 + s, s)

            @block.vector
            def _(dve):
                ch = Chain(dve, step, turns)
                link = ch.link
                tt, ts, stt = nc.vector.tensor_tensor, nc.vector.tensor_scalar, nc.vector.scalar_tensor_tensor
                dve.wait_ge(m.weights_in, m.weights_total)
                dve.sem_inc(stats_in, HC)
                with dve.Fori(0, GROUPS) as i:
                    for h in range(HC):
                        dve.wait_ge(b_out, i * HC + h + 1)
                        dve.sem_inc(turns, 1)
                        nc.vector.bn_stats(hstat[:, h, bass.ds(i, 1), :], B_PS[:, h * GR:(h + 1) * GR])\
                            .then_inc(stats_in, 1)
                dve.wait_ge(stats_in, GROUPS * HC + HC)

                def scales(a, b, stats):
                    for h in range(a, b):
                        link(nc.vector.bn_aggr(moments[:, h, :], stats[:, h - a, :, :]))
                    q = slice(a, b)
                    ts(var[:, q], moments[:, q, 1], EPS, None, ALU.add).then_inc(var_in, 1)
                    dve.wait_ge(root_out, 1 if a == 0 else 2)
                    inverse_root(nc, link, inv[:, q], root[:, q], var[:, q], corr[:, q])
                    link(tt(scale[:, q], inv[:, q], w["l1_g"][:, q], ALU.mult))
                    link(tt(mean[:, q], moments[:, q, 0], w["l1_b"][:, q], ALU.add))
                    link(tt(shift[:, q], w["l1_b"][:, q], mean[:, q], ALU.subtract))
                    link(tt(shift[:, q], shift[:, q], scale[:, q], ALU.mult))
                    tt(shift[:, q], shift[:, q], w["l1_be"][:, q], ALU.add).then_inc(scales_in, 1)

                scales(0, HC, hstat)
                dve.sem_inc(out_in, 1)
                with dve.Fori(0, GROUPS) as i:
                    dve.wait_ge(c_out, i + 1)
                    dve.sem_inc(turns, 1)
                    for h in range(2):
                        nc.vector.bn_stats(ostat[:, h, bass.ds(i, 1), :], C_PS[:, h * GR:(h + 1) * GR])\
                            .then_inc(ostat_in, 1)
                    nc.vector.tensor_copy(T[:, :, bass.ds(i * GR, GR)], C_PS.rearrange("p (c r) -> p c r", c=2))\
                        .then_inc(out_in, 1)
                dve.wait_ge(ostat_in, GROUPS * 2)
                scales(HC, HC + 2, ostat)
                dve.sem_inc(added, 2)
                with ch.loop(GROUPS // 2, 2 * (2 * G + 1)) as i:
                    for s in range(2):
                        dve.wait_ge(turned, i * 2 + s + 1)
                        x = m.X[:, bass.ds(i * (2 * G) + s * G, G), :]
                        tt(x, O_PS[s].rearrange("p (t d) -> p t d", t=G), x, ALU.add).then_inc(added, 1)
                        dve.wait_ge(added, i * 2 + s + 3)
                        row_statistics(nc, ch, m, stat, i * (2 * G) + s * G, G)
        sem.clear()


HEADS = 4
EDGES = 512
EC = EDGES // P
BLOCKS = 4
BT = TILES // BLOCKS
NODES = 8
CHUNKS = N // NODES


def graph_attention(nc, m, io):
    ps, w = m.ps, m.weights

    def bank(k, n=1):
        return ps[:, k * 512:(k + n) * 512]

    with ExitStack() as ctx:
        sb, sem = scope(nc, ctx)
        ends_i = sb("ends_i", [P, 2, EC], I32)
        rows_i = sb("rows_i", [P, 2, EDGES], I32)
        ends = sb("ends", [P, 2, EC])
        rows = sb("rows", [P, 2, EDGES])
        at_node = sb("at_node", [P, 2, EC, N])
        pairs = sb("pairs", [P, EC, N * N], BF16)
        gather = sb("gather", [P, 2, EDGES], BF16)
        log_a = sb("log_a", [P, N * N])
        ones = sb("l2_ones", [P, P], BF16)
        per_edge = sb("per_edge", [P, EC])
        xs, xt = sb("l2_xs", [P, D]), sb("l2_xt", [P, 2, P])
        xq, xq_rest = sb("l2_xq", [P, 3, D], BF16), sb("l2_xq_rest", [P, D])
        leaky = [sb(f"leaky{j}", [P, EDGES]) for j in range(4)]
        value = sb("value", [P, BT, D])
        attn = sb("attn", [P, BT, HEADS, N])
        score, rest = (leaky[j][:, :].rearrange("p (e r) -> p e r", e=EC) for j in range(2))
        times = attn[:, :, :, :].rearrange("p t h n -> p (t h n)")
        part = [sb(f"part{j}", [P, EC, P], BF16) for j in range(3)]
        soft = [sb(f"soft{s}", [P, NODES, N]) for s in range(2)]
        top, den = sb("top", [P, NODES]), sb("den", [P, NODES])
        vs, ws = sb("l2_vs", [P, D]), sb("l2_ws", [P, HEADS, N])
        yt = [sb(f"yt{s}", [P, 2, P]) for s in range(2)]
        stat = sb("l2_stat", [P, 1, 8])
        edges_in, adj_in, log_in, ones_in, pairs_in, count_out, count_in, adj_eps, made = (
            sem(f"l2_{k}") for k in ("edges_in", "adj_in", "log_in", "ones_in", "pairs_in", "count_out", "count_in", "adj_eps",
                                     "made"))
        xs_in, turned, xt_in, q_out, v_out, xq_in, v_in, gather_out, sum_in, leaky_in, score_out = (
            sem(f"l2_{k}") for k in ("xs_in", "turned", "xt_in", "q_out", "v_out", "xq_in", "v_in", "gather_out", "sum_in", "leaky_in",
                                     "score_out"))
        parts_in, dense_out, dense_in, less_max, exp_in, attn_in, turned2, w0_in, w1_in = (
            sem(f"l2_{k}") for k in ("parts_in", "dense_out", "dense_in", "less_max", "exp_in",
                                     "attn_in", "turned2", "w0_in", "w1_in"))
        staged, y_out, yt_in, o_out, added = (sem(f"l2_{k}") for k in ("staged", "y_out", "yt_in", "o_out", "added"))
        w0_in_free, w1_in_free = sem("l2_w0_free"), sem("l2_w1_free")
        step, turns, pe_turns, pool_turns = (sem(f"l2_{k}") for k in ("step", "turns", "pe_turns", "pool_turns"))
        def keep_turned(copy, part_of_two, k, done):
            src = bank(2 + 2 * (k % 2) + part_of_two)[0:N, :].rearrange("m (n t b h) -> m b t h n", t=BT, b=2, h=HEADS)
            n = k * NODES + part_of_two * NODES // 2
            for b in range(2):
                copy(attn[b * N:(b + 1) * N, :, :, n:n + NODES // 2], src[:, b]).then_inc(done, 1)

        with nc.Block() as block:

            @block.sync
            def _(sp):
                sp.dma_start(ends_i[:, :, :], io["edge_ends"]).then_inc(edges_in, 16)
                sp.dma_start(rows_i[:, :, :], io["edge_rows"]).then_inc(edges_in, 16)
                sp.dma_start(log_a[:, :], io["adj_row"].broadcast_to([P, N * N])).then_inc(adj_in, 16)

            @block.gpsimd
            def _(pool):
                with pool.Fori(0, BLOCKS) as q:
                    with pool.Fori(0, BT) as t:
                        pool.wait_ge(turned, q * BT + t + 1)
                        pool.tensor_copy(xs[:, :], m.X[:, bass.ds(q * BT + t, 1), :]).then_inc(xs_in, 1)
                    pool.wait_ge(w0_in, (q + 1) * CHUNKS * 2)
                    pool.wait_ge(w1_in, (q + 1) * CHUNKS * 2)
                    pool.sem_inc(pool_turns, 1)
                    with pool.Fori(0, BT) as t:
                        pool.wait_ge(y_out, q * BT + t + 1)
                        pool.tensor_copy(vs[:, :], value[:, bass.ds(t, 1), :])
                        pool.tensor_copy(ws[:, :, :], attn[:, bass.ds(t, 1), :, :]).then_inc(staged, 1)

            @block.tensor
            def _(pe):
                pe.sem_inc(turned, 1)
                pe.sem_inc(y_out, 1)
                pe.wait_ge(pairs_in, EC)
                pe.wait_ge(ones_in, 1)
                for k in range(CHUNKS):
                    for e in range(EC):
                        mm = pe.matmul(bank(k), ones[:, :], pairs[:, e, k * 512:(k + 1) * 512],
                                       start=e == 0, stop=e == EC - 1)
                mm.then_inc(count_out, 1)
                pe.wait_ge(made, 1)

                with pe.Fori(0, BLOCKS) as q:
                    def turn(t):
                        u = q * BT + t
                        pe.wait_ge(xs_in, u + 1)
                        pe.wait_ge(v_in, u + 1)
                        for c in range(2):
                            mm = pe.transpose(bank(0)[:, c * P:(c + 1) * P], xs[:, c * P:(c + 1) * P], w["eye"])
                        mm.then_inc(turned, 1)

                    def queries_values(t):
                        pe.wait_ge(xt_in, q * BT + t + 1)
                        for j in range(2):
                            for c in range(2):
                                mm = pe.matmul(bank(1 - j)[:, j * D:(j + 1) * D], xt[:, c, :],
                                               w["l2_wqv"][:, c, j * D:(j + 1) * D], start=c == 0, stop=c == 1)
                            mm.then_inc(v_out if j else q_out, 1)

                    def gathers(t):
                        pe.wait_ge(xq_in, q * BT + t + 1)
                        for b in range(2):
                            for c in range(2):
                                for j in range(3):
                                    mm = pe.matmul(bank(2 + 2 * b + c), xq[:, j, c * P:(c + 1) * P], gather[:, b, :],
                                                   start=j == 0, stop=j == 2)
                                mm.then_inc(gather_out, 1)

                    def scores(t):
                        pe.wait_ge(leaky_in, (q * BT + t + 1) * 4)
                        for b in range(2):
                            for c in range(2):
                                for e in range(EC):
                                    at = t * (2 * HEADS) + e * 2 * P + b * HEADS + c * 2
                                    mm = pe.matmul(bank(6, 2)[:, bass.ds(at, P)], leaky[2 * b + c][:, e * P:(e + 1) * P],
                                                   w["l2_a"][:, c, :], start=True, stop=True)
                        mm.then_inc(score_out, 1)

                    turn(0)
                    queries_values(0)
                    turn(1)
                    gathers(0)
                    with pe.Fori(1, BT - 1) as t:
                        queries_values(t)
                        scores(t - 1)
                        turn(t + 1)
                        gathers(t)
                    queries_values(BT - 1)
                    scores(BT - 2)
                    gathers(BT - 1)
                    scores(BT - 1)

                    def dense(k):
                        pe.wait_ge(dense_in, q * CHUNKS + k + 1)
                        for j in range(3):
                            for e in range(EC):
                                mm = pe.matmul(bank(k % 2), part[j][:, e, :], pairs[:, e, k * 512:(k + 1) * 512],
                                               start=j + e == 0, stop=j == 2 and e == EC - 1)
                        mm.then_inc(dense_out, 1)

                    def turn_weights(k):
                        v = q * CHUNKS + k
                        pe.wait_ge(w0_in_free, v + 1)
                        pe.wait_ge(w1_in_free, v + 1)
                        pe.wait_ge(attn_in, v + 1)
                        pe.sem_inc(pe_turns, 1)
                        for n in range(NODES):
                            mm = pe.transpose(bank(2 + 2 * (k % 2), 2)[0:N, n * P:(n + 1) * P],
                                              soft[k % 2][:, n, :], w["eye"])
                        mm.then_inc(turned2, 1)

                    pe.wait_ge(v_in, (q + 1) * BT + 1)
                    pe.wait_ge(parts_in, q + 1)
                    dense(0)
                    for k in range(CHUNKS):
                        if k + 1 < CHUNKS:
                            dense(k + 1)
                        turn_weights(k)

                    def sums(t, s):
                        u = q * BT + t
                        pe.wait_ge(yt_in, u + 1)
                        pe.wait_ge(staged, u + 1)
                        pe.sem_inc(pe_turns, 1)
                        for b in range(2):
                            half = slice(b * N, (b + 1) * N)
                            for h in range(HEADS):
                                mm = pe.matmul(bank(3 * s + b)[(h % 2) * N:(h % 2 + 1) * N, h // 2 * N:(h // 2 + 1) * N],
                                               vs[half, h * N:(h + 1) * N], ws[half, h, :], start=True, stop=True)
                        mm.then_inc(y_out, 1)

                    def output(t, s):
                        u = q * BT + t
                        pe.wait_ge(added, u + 1)
                        pe.wait_ge(yt_in, u + 3)
                        for c in range(2):
                            mm = pe.matmul(bank(3 * s + 2)[:, 0:D], yt[s][:, c, :], w["l2_wo"][:, c, :],
                                           start=c == 0, stop=c == 1)
                        mm.then_inc(o_out, 1)

                    sums(0, 0)
                    with pe.Fori(0, BT // 2 - 1) as i:
                        sums(i * 2 + 1, 1)
                        output(i * 2, 0)
                        sums(i * 2 + 2, 0)
                        output(i * 2 + 1, 1)
                    sums(BT - 1, 1)
                    output(BT - 2, 0)
                    output(BT - 1, 1)

            @block.scalar
            def _(act):
                act.sem_inc(v_in, 1)
                act.sem_inc(yt_in, 2)
                act.sem_inc(w1_in_free, 2)
                act.wait_ge(adj_eps, 1)
                nc.scalar.activation(log_a[:, :], log_a[:, :], ACT.Ln)
                act.wait_ge(count_in, 1)
                pair_count = value[:, :, :].rearrange("p t d -> p (t d)")
                nc.scalar.activation(pair_count, pair_count, ACT.Ln).then_inc(log_in, 1)
                with act.Fori(0, BLOCKS) as q:
                    def keep_turned_x(t):
                        act.wait_ge(turned, q * BT + t + 2)
                        nc.scalar.copy(xt[:, :, :], bank(0)[:, 0:D].rearrange("p (c r) -> p c r", c=2)).then_inc(xt_in, 1)

                    def keep_values(t):
                        act.wait_ge(v_out, q * BT + t + 1)
                        nc.scalar.copy(value[:, bass.ds(t, 1), :], bank(0)[:, None, D:2 * D]).then_inc(v_in, 1)

                    def keep_sums(t):
                        for j in range(4):
                            act.wait_ge(gather_out, (q * BT + t) * 4 + j + 1)
                            nc.scalar.copy(leaky[j][:, :], bank(2 + j)).then_inc(sum_in, 1)

                    keep_turned_x(0)
                    with act.Fori(0, BT - 1) as t:
                        keep_values(t)
                        keep_turned_x(t + 1)
                        keep_sums(t)
                    keep_values(BT - 1)
                    keep_sums(BT - 1)

                    def exponential(k):
                        act.wait_ge(less_max, q * CHUNKS + k + 1)
                        nc.scalar.activation(soft[k % 2][:, :, :], soft[k % 2][:, :, :], ACT.Exp).then_inc(exp_in, 1)

                    def keep(k):
                        act.wait_ge(turned2, q * CHUNKS + k + 3)
                        keep_turned(nc.scalar.copy, 1, k, w1_in)
                        act.wait_ge(w1_in, (q * CHUNKS + k + 1) * 2)
                        act.sem_inc(w1_in_free, 1)

                    exponential(0)
                    for k in range(CHUNKS):
                        if k + 1 < CHUNKS:
                            exponential(k + 1)
                        keep(k)

                    with act.Fori(0, BT // 2) as i:
                        for s in range(2):
                            act.wait_ge(y_out, q * BT + i * 2 + s + 2)
                            nc.scalar.copy(yt[s][:, :, :].rearrange("p c (b n) -> p b c n", b=2),
                                           bank(3 * s, 2).rearrange("p (b x) -> p b x", b=2)[:, :, 0:P]
                                           .rearrange("p b (c n) -> p b c n", c=2)).then_inc(yt_in, 1)

            @block.vector
            def _(dve):
                ch = Chain(dve, step, turns)
                link = ch.link
                tt, ts, stt = nc.vector.tensor_tensor, nc.vector.tensor_scalar, nc.vector.scalar_tensor_tensor
                dve.sem_inc(dense_in, 2)
                dve.sem_inc(turned2, 2)
                dve.sem_inc(w0_in_free, 2)
                dve.sem_inc(added, 2)
                nc.vector.memset(ones[:, :], 1.0).then_inc(ones_in, 1)
                dve.wait_ge(edges_in, 32)
                link(nc.vector.tensor_copy(ends[:, :, :], ends_i[:, :, :]))
                link(nc.vector.tensor_copy(rows[:, :, :], rows_i[:, :, :]))
                for s in range(2):
                    for e in range(EC):
                        link(ts(at_node[:, s, e, :], w["l2_nodes"], ends[:, s, e:e + 1], None, ALU.is_equal))
                for e in range(EC):
                    tt(pairs[:, e, :].rearrange("p (n m) -> p n m", m=N),
                       at_node[:, 0, e, :, None].broadcast_to([P, N, N]),
                       at_node[:, 1, e, None, :].broadcast_to([P, N, N]), ALU.mult).then_inc(pairs_in, 1)
                for b in range(2):
                    node = w["l2_node"][:, b:b + 1]
                    link(ts(leaky[0][:, :], rows[:, 0, :], node, None, ALU.is_equal))
                    link(stt(gather[:, b, :], rows[:, 1, :], node, leaky[0][:, :], ALU.is_equal, ALU.add))
                for e in range(EC):
                    link(ts(leaky[0][:, :], rows[:, 0, :], ends[:, 0, e:e + 1], None, ALU.is_equal))
                    link(stt(leaky[1][:, :], rows[:, 1, :], ends[:, 1, e:e + 1], leaky[0][:, :],
                             ALU.is_equal, ALU.mult))
                    link(nc.vector.tensor_reduce(per_edge[:, e:e + 1], leaky[1][:, :], AX, ALU.add))
                link(nc.vector.reciprocal(per_edge[:, :], per_edge[:, :]))
                dve.wait_ge(adj_in, 16)
                ts(log_a[:, :], log_a[:, :], 1e-8, None, ALU.add).then_inc(adj_eps, 1)
                dve.wait_ge(count_out, 1)
                pair_count = value[:, :, :].rearrange("p t d -> p (t d)")
                link(nc.vector.tensor_copy(times, ps[:, :]))
                ts(pair_count, times, 1.0, None, ALU.max).then_inc(count_in, 1)
                dve.wait_ge(log_in, 1)
                link(tt(log_a[:, :], log_a[:, :], pair_count, ALU.add))
                link(ts(times, times, 0.0, -BIG, ALU.is_equal, ALU.mult))
                tt(log_a[:, :], log_a[:, :], times, ALU.add).then_inc(made, 1)
                dve.wait_ge(made, 1)

                soften, finish, tile_steps = 2, 3, 3
                query_steps = 4
                with ch.loop(BLOCKS, EC + 4 + CHUNKS * (soften + finish) + BT * (tile_steps + query_steps)) as q:
                    with ch.loop(BT, query_steps) as t:
                        dve.wait_ge(q_out, q * BT + t + 1)
                        link(nc.vector.tensor_copy(xq[:, 0, :], bank(1)[:, 0:D]))
                        link(tt(xq_rest[:, :], bank(1)[:, 0:D], xq[:, 0, :], ALU.subtract))
                        link(nc.vector.tensor_copy(xq[:, 1, :], xq_rest[:, :]))
                        link(tt(xq_rest[:, :], xq_rest[:, :], xq[:, 1, :], ALU.subtract))
                        nc.vector.tensor_copy(xq[:, 2, :], xq_rest[:, :]).then_inc(xq_in, 1)
                        for j in range(4):
                            dve.wait_ge(sum_in, (q * BT + t) * 4 + j + 1)
                            stt(leaky[j][:, :], leaky[j][:, :], 0.2, leaky[j][:, :], ALU.mult, ALU.max)\
                                .then_inc(leaky_in, 1)

                    dve.wait_ge(score_out, (q + 1) * BT)
                    dve.sem_inc(turns, 1)
                    for e in range(EC):
                        ts(score[:, e, :], bank(6, 2)[:, e * 2 * P:e * 2 * P + P], per_edge[:, e:e + 1], None, ALU.mult)\
                            .then_inc(step, 1)
                    ch.n += EC
                    dve.wait_ge(step, ch.turns + ch.n)
                    link(nc.vector.tensor_copy(part[0][:, :, :], score[:, :, :]))
                    link(tt(rest[:, :, :], score[:, :, :], part[0][:, :, :], ALU.subtract))
                    link(nc.vector.tensor_copy(part[1][:, :, :], rest[:, :, :]))
                    link(tt(score[:, :, :], rest[:, :, :], part[1][:, :, :], ALU.subtract))
                    nc.vector.tensor_copy(part[2][:, :, :], score[:, :, :]).then_inc(parts_in, 1)

                    def less_maximum(k):
                        v, x = q * CHUNKS + k, soft[k % 2][:, :, :]
                        dve.wait_ge(turned2, v + 1)
                        dve.wait_ge(dense_out, v + 1)
                        tt(x, bank(k % 2).rearrange("p (n m) -> p n m", m=N),
                           log_a[:, k * 512:(k + 1) * 512].rearrange("p (n m) -> p n m", m=N), ALU.add)\
                            .then_inc(dense_in, 1)
                        dve.wait_ge(dense_in, v + 3)
                        link(nc.vector.tensor_reduce(top[:, :], x, AX, ALU.max))
                        link(ts(top[:, :], top[:, :], -BIG / 2, None, ALU.max))
                        tt(x, x, top[:, :, None].broadcast_to([P, NODES, N]), ALU.subtract).then_inc(less_max, 1)
                        dve.wait_ge(less_max, v + 1)

                    def normalise(k):
                        v, x = q * CHUNKS + k, soft[k % 2][:, :, :]
                        dve.wait_ge(exp_in, v + 1)
                        link(nc.vector.tensor_reduce(den[:, :], x, AX, ALU.add))
                        link(ts(den[:, :], den[:, :], 1e-30, None, ALU.max))
                        link(nc.vector.reciprocal(den[:, :], den[:, :]))
                        tt(x, x, den[:, :, None].broadcast_to([P, NODES, N]), ALU.mult).then_inc(attn_in, 1)

                    def keep(k):
                        v = q * CHUNKS + k
                        dve.wait_ge(turned2, v + 3)
                        keep_turned(nc.vector.tensor_copy, 0, k, w0_in)
                        dve.wait_ge(w0_in, (v + 1) * 2)
                        dve.sem_inc(w0_in_free, 1)

                    less_maximum(0)
                    for k in range(CHUNKS):
                        if k + 1 < CHUNKS:
                            less_maximum(k + 1)
                        if k:
                            keep(k - 1)
                        normalise(k)
                    keep(CHUNKS - 1)

                    with ch.loop(BT // 2, 2 * tile_steps) as i:
                        for s in range(2):
                            u = q * BT + i * 2 + s
                            dve.wait_ge(o_out, u + 1)
                            x = m.X[:, bass.ds(u, 1), :]
                            tt(x, bank(3 * s + 2)[:, None, 0:D], x, ALU.add).then_inc(added, 1)
                            dve.wait_ge(added, u + 3)
                            row_statistics(nc, ch, m, stat, u, 1)
        sem.clear()


SKIPS = 4
GATE_ORDER = (0, 2, 1, 3)


def window_batches(p):
    nb = P
    while nb * (N // p) > 512 or P % nb:
        nb -= 1
    return nb


def skip_lstms(nc, m, io):
    ps, T = m.ps, m.T
    with ExitStack() as ctx:
        sb, sem = scope(nc, ctx)
        wx = [sb(f"wx{s}", [P, 2, 4 * D]) for s in range(2)]
        wh = sb("wh", [P, 2, 4 * D])
        bias2 = sb("lstm_bias2", [P, 2, SKIPS * 8])
        bias = sb("lstm_bias", [P, SKIPS * 8])
        gate = [[sb(f"gate{s}{g}", [P, 512]) for g in range(4)] for s in range(2)]
        cell = sb("cell", [P, 2, 512])
        tanh_c = [gate[c][0] for c in range(2)]
        state = [sb(f"state{s}", [P, 2, 512]) for s in range(2)]
        bias_in, bias_sum = sem("lstm_bias_in"), sem("lstm_bias_sum")
        wx_in, wh_in = sem("wx_in"), sem("wh_in")
        gates_out, gates_in, gates_free = sem("lstm_gates_out"), sem("lstm_gates_in"), sem("lstm_gates_free")
        cell_in, tanh_in, state_in, kept = sem("cell_in"), sem("tanh_in"), sem("state_in"), sem("state_kept")
        state_in_primed, pool_turns = sem("state_in_primed"), sem("lstm_pool_turns")
        p_done, step, turns, pe_turns = sem("lstm_p_done"), sem("lstm_step"), sem("lstm_turns"), sem("lstm_pe_turns")

        def shape(p):
            nb = window_batches(p)
            nw = N // p
            return nb, nw, nb * nw, P // nb

        units, gates, groups = [0], [0], [0]
        for p in range(1, SKIPS + 1):
            n = shape(p)[3]
            groups.append(groups[-1] + n)
            units.append(units[-1] + n * 2 * p)
            gates.append(gates[-1] + n * (8 * p - 2))

        def each_unit(p):
            u = g = 0
            for t in range(p):
                for c in range(2):
                    order = [q for q in GATE_ORDER if t or q != 1]
                    yield t, c, order, u, g
                    u += 1
                    g += len(order)

        with nc.Block() as block:

            @block.sync
            def _(sp):
                sp.dma_start(bias2[:, 0, :], io["l3_bih"]).then_inc(bias_in, 16)
                sp.dma_start(bias2[:, 1, :], io["l3_bhh"]).then_inc(bias_in, 16)
                for p in range(1, SKIPS + 1):
                    if p > 2:
                        sp.wait_ge(p_done, p - 2)
                    sp.dma_start(wx[p % 2][:, :, :], io["l3_wih"][p - 1]).then_inc(wx_in, 16)
                    sp.wait_ge(wx_in, 16 * p)
                    if p > 1:
                        if p > 2:
                            sp.wait_ge(p_done, p - 1)
                        sp.dma_start(wh[:, :, :], io["l3_whh"][p - 1]).then_inc(wh_in, 16)

            @block.tensor
            def _(pe):
                for p in range(1, SKIPS + 1):
                    nb, nw, C, n = shape(p)
                    pe.wait_ge(wx_in, 16 * p)
                    if p > 1:
                        pe.wait_ge(kept, groups[p - 1] + 1)
                    with pe.Fori(0, n) as i:
                        rows = T[:, :, :].rearrange("p k (b n) -> p k b n", n=N)
                        for t, c, order, u, g in each_unit(p):
                            pe.wait_ge(gates_free, units[p - 1] + i * (2 * p) + u + 1)
                            for q in order:
                                bank = ps[:, (c * 4 + q) * 512:(c * 4 + q) * 512 + C]
                                col = q * D + c * P
                                for k in range(2):
                                    x = rows[:, k, bass.ds(i * nb, nb), t:t + (nw - 1) * p + 1:p]
                                    mm = pe.matmul(bank.rearrange("p (b w) -> p b w", w=nw), wx[p % 2][:, k, col:col + P],
                                                   x, start=k == 0, stop=k == 1 and t == 0)
                                if t == 0:
                                    mm.then_inc(gates_out, 1)
                            if t == 1:
                                pe.wait_ge(wh_in, 16 * (p - 1))
                            if t:
                                pe.wait_ge(state_in, units[p - 1] + i * (2 * p) + 2 * t)
                                for q in order:
                                    bank = ps[:, (c * 4 + q) * 512:(c * 4 + q) * 512 + C]
                                    col = q * D + c * P
                                    for k in range(2):
                                        mm = pe.matmul(bank, wh[:, k, col:col + P], state[(t - 1) % 2][:, k, 0:C],
                                                       start=False, stop=k == 1)
                                    mm.then_inc(gates_out, 1)
                    pe.wait_ge(state_in, units[p])
                    pe.sem_inc(p_done, 1)

            @block.scalar
            def _(act):
                act.sem_inc(gates_free, 2)
                act.wait_ge(bias_sum, 1)
                for p in range(1, SKIPS + 1):
                    nb, nw, C, n = shape(p)
                    with act.Fori(0, n) as i:
                        for t, c, order, u, g in each_unit(p):
                            unit = units[p - 1] + i * (2 * p) + u
                            act.wait_ge(state_in_primed, unit + 1)
                            for j, q in enumerate(order):
                                act.wait_ge(gates_out, gates[p - 1] + i * (8 * p - 2) + g + j + 1)
                                ins = nc.scalar.activation(
                                    gate[c][q][:, 0:C], ps[:, (c * 4 + q) * 512:(c * 4 + q) * 512 + C],
                                    ACT.Tanh if q == 2 else ACT.Sigmoid,
                                    bias=bias[:, (p - 1) * 8 + q * 2 + c:(p - 1) * 8 + q * 2 + c + 1])
                                ins.then_inc(gates_in, 1)
                            act.wait_ge(gates_in, gates[p - 1] + i * (8 * p - 2) + g + len(order))
                            act.sem_inc(gates_free, 1)
                            act.wait_ge(cell_in, unit + 1)
                            nc.scalar.activation(tanh_c[c][:, 0:C], cell[:, c, 0:C], ACT.Tanh).then_inc(tanh_in, 1)

            @block.vector
            def _(dve):
                tt = nc.vector.tensor_tensor
                dve.wait_ge(bias_in, 32)
                dve.sem_inc(state_in_primed, 2)
                tt(bias[:, :], bias2[:, 0, :], bias2[:, 1, :], ALU.add).then_inc(bias_sum, 1)
                ch = Chain(dve, step, turns)
                for p in range(1, SKIPS + 1):
                    nb, nw, C, n = shape(p)
                    with ch.loop(n, 4 * (p - 1)) as i:
                        for t, c, order, u, g in each_unit(p):
                            gi, gf, gg, go = (gate[c][q][:, 0:C] for q in range(4))
                            unit, at = units[p - 1] + i * (2 * p) + u, gates[p - 1] + i * (8 * p - 2) + g
                            dve.wait_ge(gates_in, at + 2)
                            if t == 0:
                                tt(cell[:, c, 0:C], gi, gg, ALU.mult).then_inc(cell_in, 1)
                            else:
                                tt(gi, gi, gg, ALU.mult).then_inc(step, 1)
                                dve.wait_ge(gates_in, at + 3)
                                tt(gf, gf, cell[:, c, 0:C], ALU.mult).then_inc(step, 1)
                                ch.n += 2
                                dve.wait_ge(step, ch.turns + ch.n)
                                tt(cell[:, c, 0:C], gi, gf, ALU.add).then_inc(cell_in, 1)
                            if t == (p - 1) % 2 and c == 0:
                                dve.wait_ge(kept, groups[p - 1] + i + 1)
                            dve.wait_ge(tanh_in, unit + 1)
                            tt(state[t % 2][:, c, 0:C], go, tanh_c[c][:, 0:C], ALU.mult).then_inc(state_in, 1)
                            dve.wait_ge(state_in, unit + 1)
                            dve.sem_inc(state_in_primed, 1)

            @block.gpsimd
            def _(pool):
                pool.sem_inc(kept, 1)
                for p in range(1, SKIPS + 1):
                    nb, nw, C, n = shape(p)
                    with pool.Fori(0, n) as i:
                        pool.wait_ge(state_in, units[p - 1] + (i + 1) * (2 * p))
                        pool.sem_inc(pool_turns, 1)
                        rows = T[:, :, :].rearrange("p k (b n) -> p k b n", n=N)
                        for k in range(2):
                            ins = pool.tensor_copy(rows[:, k, bass.ds(i * nb, nb), p - 1:p - 1 + (nw - 1) * p + 1:p],
                                                   state[(p - 1) % 2][:, k, 0:C].rearrange("p (b w) -> p b w", w=nw))
                        ins.then_inc(kept, 1)
                pool.wait_ge(kept, groups[SKIPS] + 1)
        sem.clear()


def turn_and_add(nc, m):
    ps, T = m.ps, m.T
    O_PS = [ps[:, 0:1024], ps[:, 1024:2048]]
    with ExitStack() as ctx:
        sb, sem = scope(nc, ctx)
        fixed = [sb(f"turn_fixed{s}", [P, 2, GR]) for s in range(2)]
        stat = sb("turn_stat", [P, G, 8])
        fixed_in, turned, added, step, turns = (sem(f"turn_{k}") for k in ("fixed_in", "turned", "added", "step",
                                                                         "turns"))
        with nc.Block() as block:

            @block.scalar
            def _(act):
                def copy(i, s):
                    nc.scalar.copy(fixed[s][:, :, :], T[:, :, bass.ds(i * GR, GR)]).then_inc(fixed_in, 1)

                copy(0, 0)
                copy(1, 1)
                with act.Fori(1, GROUPS // 2) as i:
                    for s in range(2):
                        act.wait_ge(turned, i * 2 + s - 1)
                        copy(i * 2 + s, s)

            @block.tensor
            def _(pe):
                with pe.Fori(0, GROUPS // 2) as i:
                    for s in range(2):
                        pe.wait_ge(fixed_in, i * 2 + s + 1)
                        pe.wait_ge(added, i * 2 + s + 1)
                        for t in range(G):
                            for c in range(2):
                                mm = pe.transpose(O_PS[s][:, t * D + c * P:t * D + (c + 1) * P],
                                                  fixed[s][:, c, t * P:(t + 1) * P], m.weights["eye"])
                        mm.then_inc(turned, 1)

            @block.vector
            def _(dve):
                ch = Chain(dve, step, turns)
                dve.sem_inc(added, 2)
                with ch.loop(GROUPS // 2, 2 * (2 * G + 1)) as i:
                    for s in range(2):
                        dve.wait_ge(turned, i * 2 + s + 1)
                        x = m.X[:, bass.ds(i * (2 * G) + s * G, G), :]
                        nc.vector.tensor_tensor(x, O_PS[s].rearrange("p (t d) -> p t d", t=G), x, ALU.add)\
                            .then_inc(added, 1)
                        dve.wait_ge(added, i * 2 + s + 3)
                        row_statistics(nc, ch, m, stat, i * (2 * G) + s * G, G)
        sem.clear()


def program(nc, io, out):
    with ExitStack() as ctx:
        m = Mem(nc, ctx)
        m.bd_u, m.bd_ut, m.bd_hat, m.bd_adj = (m.sb(k, [P, P]) for k in ("bd_u", "bd_ut", "bd_hat", "bd_adj"))
        m.root_deg2 = m.sb("root_deg2", [P, 1])
        m.X = m.sb("X", [P, TILES, D])
        m.mv = m.sb("mv", [P, TILES, 2])
        m.weights = {}
        for k, shape in WEIGHTS.items():
            m.weights[k] = m.sb(k, [P] + shape)[(slice(None),) * (1 + len(shape))]
        m.weights_in, m.x_in = m.sem("weights_in"), m.sem("x_in")
        load_all(nc, m, io)
        spectral_basis(nc, m, io)
        two_products(nc, m, "l0", True)
        layer_norm(nc, m, "n0")
        with ExitStack() as inner:
            m.T = inner.enter_context(nc.sbuf_tensor("T1", [P, 2, ROWS], F32))
            batch_normed(nc, m)
        layer_norm(nc, m, "n1")
        graph_attention(nc, m, io)
        layer_norm(nc, m, "n2")
        with ExitStack() as inner:
            m.T = inner.enter_context(nc.sbuf_tensor("T3", [P, 2, ROWS], F32))
            two_products(nc, m, "l3", False)
            skip_lstms(nc, m, io)
            turn_and_add(nc, m)
        layer_norm(nc, m, "n3", out)


WEIGHTS = dict(l0_w1=[2, P], l0_w2=[1, D], l0_b1=[1], l0_b2=[D], eye=[P],
               l1_w1=[2, 512], l1_w2=[4, D], l1_b=[6], l1_g=[6], l1_be=[6],
               l3_w0=[2, D], l3_w1=[2, D], l3_b0=[2], l3_b1=[D],
               l2_wqv=[2, 2 * D], l2_wo=[2, D], l2_a=[2, P], l2_nodes=[N], l2_node=[2])


def kernel(**inputs):
    import numpy as np
    import concourse.bacc as bacc
    from concourse.bass_utils import run_bass_kernel_spmd

    a = {k: np.asarray(v) for k, v in inputs.items()}

    def chunks(w):
        return w.reshape(-1, P, w.shape[-1]).transpose(1, 0, 2)

    def column(b):
        return b.reshape(-1, P).T

    def everywhere(b):
        return np.broadcast_to(b, (P,) + b.shape)

    head_vectors = np.zeros((P, 2, P), np.float32)
    for h in range(HEADS):
        head_vectors[h % 2 * N:(h % 2 + 1) * N, h // 2, h % 2] = a["L2_gnn_a"][h]

    given = dict(
        adj=a["adj"], adj_t=a["adj"].T, tables=constant_tables(), x=a["x"].reshape(ROWS, D),
        l0_w1=chunks(a["L0_gnn_W1"]), l0_w2=chunks(a["L0_gnn_W2"]), l0_b1=column(a["L0_gnn_b1"]),
        l0_b2=everywhere(a["L0_gnn_b2"]), eye=np.eye(P, dtype=np.float32),
        l1_w1=chunks(a["L1_gnn_W1"].T), l1_w2=chunks(a["L1_gnn_W2"].T),
        l3_w0=chunks(a["L3_gnn_Wg0"]), l3_w1=chunks(a["L3_gnn_Wg1"]), l3_b0=column(a["L3_gnn_bg0"]),
        l3_b1=everywhere(a["L3_gnn_bg1"]), l3_bih=column(a["L3_gnn_bih"]), l3_bhh=column(a["L3_gnn_bhh"]),
        l3_wih=a["L3_gnn_Wih"].reshape(4, 4 * D, 2, P).transpose(0, 3, 2, 1),
        l3_whh=a["L3_gnn_Whh"].reshape(4, 4 * D, 2, P).transpose(0, 3, 2, 1),
        l2_wqv=np.concatenate([chunks(a["L2_gnn_W_lin"].T), chunks(a["L2_gnn_W_val"].T)], 2),
        l2_wo=chunks(a["L2_gnn_W_out"].T), l2_a=head_vectors, adj_row=a["adj"].reshape(1, N * N),
        l2_nodes=everywhere(np.arange(N, dtype=np.float32)),
        l2_node=np.stack([np.where(np.arange(P) // N == b, np.arange(P) % N, -1) for b in range(2)], 1)
        .astype(np.float32),
        edge_ends=np.stack([a[k].reshape(EC, P).T for k in ("L2_gnn_src", "L2_gnn_dst")], 1),
        edge_rows=everywhere(np.stack([a["L2_gnn_src"], a["L2_gnn_dst"]])),
        l1_b=column(np.concatenate([a["L1_gnn_b1"], a["L1_gnn_b2"]])),
        l1_g=column(np.concatenate([a["L1_gnn_g1"], a["L1_gnn_g2"]])),
        l1_be=column(np.concatenate([a["L1_gnn_be1"], a["L1_gnn_be2"]])),
    )
    nc = bacc.Bacc("TRN2", target_bir_lowering=False, num_devices=1)
    io, arrays = {}, {}
    for name, v in given.items():
        v = np.ascontiguousarray(v)
        arrays[f"in_{name}"] = v
        io[name] = nc.dram_tensor(f"in_{name}", v.shape, mybir.dt.from_np(v.dtype), kind="ExternalInput").ap()
    out = nc.dram_tensor("out", (ROWS, D), F32, kind="ExternalOutput").ap()
    program(nc, io, out)
    r = run_bass_kernel_spmd(nc, [arrays], core_ids=[0])
    return r.results[0]["out"].reshape(a["x"].shape)
```

```python
from contextlib import ExitStack, contextmanager

import concourse.bass as bass
from concourse import mybir

F32 = mybir.dt.float32
BF16 = mybir.dt.bfloat16
F16 = mybir.dt.float16
I32 = mybir.dt.int32
ALU = mybir.AluOpType
ACT = mybir.ActivationFunctionType
AX = mybir.AxisListType.X

P = 128
N = 64
D = 256
LEVELS = 6
LEVEL_STEPS = 87
NEWTON = 14
TIE = 2.0 ** -30
BIG = 1e30
ROOT2 = 2.0 ** 0.5


class Chain:

    def __init__(self, eng, sem, entries):
        self.eng, self.sem, self.entries, self.n, self.turns = eng, sem, entries, 0, 0

    def go(self, ins):
        ins.then_inc(self.sem, 1)
        self.n += 1

    def link(self, ins):
        self.go(ins)
        self.eng.wait_ge(self.sem, self.turns + self.n)

    @contextmanager
    def loop(self, count, per_turn, start=0):
        at, outer = self.n, self.turns
        self.eng.sem_inc(self.entries, 1)
        with self.eng.Fori(start, start + count) as i:
            self.turns = outer + (i - start) * per_turn
            yield i
            assert self.n - at == per_turn, (self.n - at, per_turn)
        self.n, self.turns = at + count * per_turn, outer


TABLES = dict(eye=N, not_eye=N, below=N, first=N, from_first=N, tie=N, sub=N, sup=N, same=LEVELS * N, last=LEVELS * N, head=LEVELS * N,
              headcol=LEVELS)


def table_slices():
    at, out = 0, {}
    for name, w in TABLES.items():
        out[name] = (at, at + w)
        at += w
    return out, at


def constant_tables():
    import numpy as np
    p = np.arange(N)[:, None]
    c = np.arange(N)[None, :]
    parts = dict(eye=p == c, not_eye=p != c, below=p > c + 1, first=p == c + 1, from_first=p > c, tie=(c - p) * TIE, sub=c == p - 1, sup=c == p + 1)
    parts["same"] = np.concatenate([p // (2 << l) == c // (2 << l) for l in range(LEVELS)], 1)
    parts["last"] = np.concatenate([(c % (2 << l) == (1 << l) - 1) + 0 * p for l in range(LEVELS)], 1)
    parts["head"] = np.concatenate([(c % (2 << l) == (1 << l)) + 0 * p for l in range(LEVELS)], 1)
    parts["headcol"] = np.concatenate([p % (2 << l) == (1 << l) for l in range(LEVELS)], 1)
    return np.concatenate([parts[k].astype(np.float32) for k in TABLES], 1)


class Mem:

    def __init__(self, nc, ctx):
        self.nc, self.ctx = nc, ctx
        self.ps = ctx.enter_context(nc.psum_tensor("ps", [P, 8 * 512], F32))

    def sb(self, name, shape, dt=F32):
        return self.ctx.enter_context(self.nc.sbuf_tensor(name, shape, dt))

    def sem(self, name):
        return self.ctx.enter_context(self.nc.semaphore(name))


def scope(nc, ctx):
    held = []

    def sb(name, shape, dt=F32):
        return ctx.enter_context(nc.sbuf_tensor(name, shape, dt))

    def sem(name):
        held.append(ctx.enter_context(nc.semaphore(name)))
        return held[-1]

    def clear():
        with nc.Block() as block:
            @block.gpsimd
            def _(pool):
                for s in held:
                    pool.sem_clear(s)

    sem.clear = clear
    return sb, sem


def spectral_basis(nc, m, io):
    with ExitStack() as ctx:
        sb, sem = scope(nc, ctx)
        at, width = table_slices()
        tab = sb("tab", [N, width])
        T = {k: tab[:, a:b] for k, (a, b) in at.items()}
        eye = T["eye"]
        adj2 = sb("adj2", [N, 2, N])
        ones = sb("ones", [N, P])
        mat = sb("mat", [N, 3 * N])
        low = sb("low", [N, 2 * N])
        col = sb("col", [N, 64])
        row = sb("row", [1, 6 * N])
        vt = sb("vt", [N, N])
        sgn_row = sb("sgn_row", [N, N])
        W4 = sb("W4", [N, 4 * N])
        heads, rhos, pick = sb("heads", [N, LEVELS]), sb("rhos", [N, LEVELS]), sb("pick", [N, LEVELS, N])
        big = [sb(f"big{i}", [N, N]) for i in range(14)]
        dup = sb("dup", [N, 2 * P])
        ps = m.ps
        tables_in = sem("tables_in")
        adj_in = sem("adj_in")
        bd_zero = sem("bd_zero")
        bd_adj_in = sem("bd_adj_in")
        dve_step = sem("eig_dve_step")
        sqrt_in, sqrt_out = sem("sqrt_in"), sem("sqrt_out")
        turn_in, turn_out = sem("turn_in"), sem("turn_out")
        parts_in, square_out, sums_out = sem("parts_in"), sem("square_out"), sem("sums_out")
        v_in, prods_out = sem("v_in"), sem("prods_out")
        rows_in, update_out = sem("rows_in"), sem("update_out")
        sq2_in, sq2_out = sem("sq2_in"), sem("sq2_out")
        pe_turns = sem("pe_turns")
        dve_turns = sem("dve_turns")
        reflectors = N - 2

        def c(i, w=1):
            return col[:, i:i + w]

        with nc.Block() as block:

            @block.sync
            def _(sp):
                sp.dma_start(tab[:, :], io["tables"]).then_inc(tables_in, 16)
                sp.dma_start(adj2[:, 0, :], io["adj"]).then_inc(adj_in, 16)
                sp.dma_start(adj2[:, 1, :], io["adj_t"]).then_inc(adj_in, 16)
                sp.wait_ge(tables_in, 16)
                sp.wait_ge(adj_in, 32)
                load_weights(m, io, sp)
                sp.wait_ge(bd_zero, 1)
                for h in range(2):
                    sp.dma_start(m.bd_adj[h * N:(h + 1) * N, h * N:(h + 1) * N], io["adj_t"]).then_inc(bd_adj_in, 16)
                sp.wait_ge(bd_adj_in, 32)

            @block.gpsimd
            def _(pool):
                pool.memset(m.bd_adj[:, :], 0.0).then_inc(bd_zero, 1)
                pool.wait_ge(tables_in, 16)
                pool.wait_ge(adj_in, 32)
                load_rows(m, io, pool)
                pool.memset(m.bd_u[:, :], 0.0).then_inc(bd_zero, 1)
                pool.memset(m.bd_ut[:, :], 0.0).then_inc(bd_zero, 1)
                pool.memset(m.bd_hat[:, :], 0.0).then_inc(bd_zero, 1)

            @block.scalar
            def _(act):
                act.wait_ge(sqrt_in, 1)
                act.activation(c(4, 2), c(2, 2), ACT.Sqrt).then_inc(sqrt_out, 1)
                with act.Fori(0, reflectors) as k:
                    act.wait_ge(square_out, k + 1)
                    act.activation(c(7), ps[0:N, 1536:1537], ACT.Sqrt).then_inc(sqrt_out, 1)
                with act.Fori(0, LEVELS) as l:
                    act.wait_ge(sq2_in, l * 2 + 1)
                    act.activation(c(59), c(58), ACT.Sqrt).then_inc(sq2_out, 1)
                    act.wait_ge(sq2_in, l * 2 + 2)
                    act.activation(c(59), c(58), ACT.Sqrt).then_inc(sq2_out, 1)

            @block.tensor
            def _(pe):
                pe.wait_ge(tables_in, 16)
                pe.wait_ge(turn_in, 1)
                pe.matmul(ps[:, 0:N], dup[:, 0:P], eye, start=True, stop=True)
                pe.matmul(ps[:, 512:512 + N], dup[:, P:2 * P], eye, start=True, stop=True).then_inc(turn_out, 1)
                with pe.Fori(0, reflectors) as k:
                    pe.wait_ge(parts_in, k + 1)
                    pe.matmul(ps[:, 1536:1537], ones[:, :], c(10), start=True, stop=True).then_inc(square_out, 1)
                    pe.matmul(ps[:, 0:2], ones[:, :], c(11, 2), start=True, stop=True).then_inc(sums_out, 1)
                    pe.wait_ge(v_in, k + 1)
                    pe.sem_inc(pe_turns, 1)
                    pe.matmul(ps[0:1, 512:512 + 3 * N], c(13), mat[:, :], start=True, stop=True).then_inc(prods_out, 1)
                    pe.wait_ge(rows_in, k + 1)
                    pe.sem_inc(pe_turns, 1)
                    pe.matmul(ps[0:N, 1024:1024 + 2 * N], row[:, 0:N], row[:, N:3 * N], start=True, stop=False)
                    pe.matmul(ps[0:N, 1024:1024 + N], row[:, N:2 * N], row[:, 0:N], start=False, stop=True)\
                        .then_inc(update_out, 1)
                pe.wait_ge(turn_in, 2)
                pe.matmul(ps[0:N, 0:N], ones[:, 0:N], low[:, 0:N], start=True, stop=True)
                for l in range(LEVELS):
                    mm = pe.matmul(ps[0:N, 512 + l:513 + l], T["same"][:, l * N:(l + 1) * N], heads[:, l:l + 1],
                                   start=True, stop=True)
                mm.then_inc(turn_out, 1)
                with pe.Fori(0, LEVELS) as l:
                    pe.wait_ge(turn_in, l * 4 + 3)
                    pe.matmul(ps[:, 512:512 + 2 * N], ones[:, :], W4[:, 0:2 * N], start=True, stop=True)\
                        .then_inc(turn_out, 1)
                    pe.wait_ge(turn_in, l * 4 + 4)
                    pe.matmul(ps[:, 1024:1024 + 3 * N], ones[:, :], W4[:, N:4 * N], start=True, stop=True)\
                        .then_inc(turn_out, 1)
                    pe.wait_ge(turn_in, l * 4 + 5)
                    pe.sem_inc(pe_turns, 1)
                    pe.matmul(ps[0:N, 0:N], big[8][:, :], eye, start=True, stop=True)
                    pe.matmul(ps[0:N, 512:512 + N], big[9][:, :], eye, start=True, stop=True).then_inc(turn_out, 1)
                    pe.wait_ge(turn_in, l * 4 + 6)
                    pe.sem_inc(pe_turns, 1)
                    pe.matmul(ps[0:N, 1024:1024 + N], big[10][:, :], vt[:, :], start=True, stop=True)\
                        .then_inc(turn_out, 1)
                pe.wait_ge(turn_in, 4 * LEVELS + 3)
                pe.matmul(ps[0:N, 0:N], vt[:, :], eye, start=True, stop=True).then_inc(turn_out, 1)
                pe.wait_ge(turn_in, 4 * LEVELS + 4)
                pe.matmul(ps[:, 512:512 + N], dup[:, 0:P], big[0][:, :], start=True, stop=True)
                pe.matmul(ps[:, 1024:1024 + N], dup[:, P:2 * P], mat[:, N:2 * N], start=True, stop=True)\
                    .then_inc(turn_out, 1)

            @block.vector
            def _(dve):
                ch = Chain(dve, dve_step, dve_turns)
                link, go = ch.link, ch.go
                tt, ts, stt = dve.tensor_tensor, dve.tensor_scalar, dve.scalar_tensor_tensor
                A = mat[:, 0:N]

                dve.wait_ge(tables_in, 16)
                dve.wait_ge(adj_in, 32)
                link(dve.memset(ones[:, :], 1.0))
                link(dve.memset(col[:, :], 0.0))
                link(dve.tensor_reduce(c(0), adj2[:, :, :], mybir.AxisListType.XY, ALU.add))
                link(tt(big[0][:, :], adj2[:, 0, :], eye, ALU.mult))
                link(dve.tensor_reduce(c(1), big[0][:, :], AX, ALU.add))
                link(tt(c(2), c(0), c(1), ALU.subtract))
                link(ts(c(3), c(2), 1.0, None, ALU.add))
                link(dve.tensor_copy(c(0), c(2)))
                link(ts(c(1), c(2), 0.0, None, ALU.is_gt))
                ts(c(2), c(2), 1e-30, None, ALU.max).then_inc(sqrt_in, 1)
                dve.wait_ge(sqrt_out, 1)
                link(dve.reciprocal(c(4, 2), c(4, 2)))
                link(tt(c(4), c(4), c(1), ALU.mult))
                link(tt(big[1][:, :], adj2[:, 0, :], adj2[:, 1, :], ALU.add))
                link(ts(big[2][:, :], eye, c(0), None, ALU.mult))
                link(stt(big[1][:, :], big[1][:, :], -0.5, big[2][:, :], ALU.mult, ALU.add))
                link(tt(big[3][:, :], adj2[:, 0, :], eye, ALU.add))
                for h in range(2):
                    link(ts(dup[:, h * N:(h + 1) * N], big[1][:, :], c(4), None, ALU.mult))
                link(ts(dup[:, P:P + N], big[3][:, :], c(5), None, ALU.mult))
                dve.tensor_copy(dup[:, P + N:2 * P], dup[:, P:P + N]).then_inc(turn_in, 1)
                dve.wait_ge(turn_out, 1)
                link(ts(A, ps[0:N, 0:N], c(4), None, ALU.mult))
                link(dve.tensor_copy(mat[:, N:2 * N], eye))
                link(dve.tensor_copy(mat[:, 2 * N:3 * N], eye))
                dve.wait_ge(bd_zero, 4)
                link(ts(m.bd_hat[0:N, 0:N], ps[0:N, 512:512 + N], c(5), None, ALU.mult))
                link(dve.tensor_copy(m.root_deg2[0:N, :], c(5)))
                link(dve.tensor_copy(m.root_deg2[N:P, :], c(5)))
                link(ts(m.bd_hat[N:P, N:P], ps[N:P, 512:512 + N], m.root_deg2[N:P, :], None, ALU.mult))

                alpha, below_sq = ps[0:N, 0:1], ps[0:N, 1:2]
                x, v, tau, some, none, sign = c(9), c(13), c(14), c(16), c(17), c(18)
                size, length, diff, inv_diff, inv_beta, factor = c(19), c(20), c(21), c(22), c(23), c(24)
                row_v, row_w, row_q, row_p = (row[:, i * N:(i + 1) * N] for i in range(4))
                with ch.loop(reflectors, 19) as k:
                    below, first = T["below"][:, bass.ds(k, 1)], T["first"][:, bass.ds(k, 1)]
                    from_first = T["from_first"][:, bass.ds(k, 1)]
                    a_k = A[:, bass.ds(k, 1)]
                    stt(c(10), a_k, from_first, a_k, ALU.mult, ALU.mult)
                    tt(c(11), a_k, first, ALU.mult)
                    stt(c(12), a_k, below, a_k, ALU.mult, ALU.mult).then_inc(parts_in, 1)
                    go(tt(x, a_k, below, ALU.mult))
                    dve.wait_ge(sums_out, k + 1)
                    go(ts(some, below_sq, 0.0, None, ALU.is_gt))
                    go(ts(none, below_sq, 0.0, None, ALU.is_le))
                    go(ts(sign, alpha, 0.0, 2.0, ALU.is_ge, ALU.mult))
                    link(ts(size, alpha, -1.0, None, ALU.mult))
                    go(ts(sign, sign, -1.0, None, ALU.add))
                    go(tt(size, size, alpha, ALU.max))
                    dve.wait_ge(sqrt_out, k + 2)
                    link(tt(length, c(7), none, ALU.add))
                    link(stt(diff, length, size, sign, ALU.add, ALU.mult))
                    link(nc.vector.reciprocal(inv_diff, diff))
                    stt(v, x, inv_diff, first, ALU.mult, ALU.add).then_inc(v_in, 1)
                    link(nc.vector.reciprocal(inv_beta, length))
                    link(stt(tau, inv_beta, sign, diff, ALU.mult, ALU.mult))
                    link(tt(tau, tau, some, ALU.mult))
                    link(ts(factor, tau, tau, -0.5, ALU.mult, ALU.mult))
                    dve.wait_ge(prods_out, k + 1)
                    link(dve.tensor_copy(row_v, ps[0:1, 512 + 2 * N:512 + 3 * N]))
                    go(ts(row_p, ps[0:1, 512:512 + N], tau[0:1, :], None, ALU.mult))
                    go(ts(row_q, ps[0:1, 512 + N:512 + 2 * N], tau[0:1, :], None, ALU.mult))
                    link(dve.tensor_tensor_reduce(row[:, 4 * N:5 * N], ps[0:1, 512:512 + N], row_v, factor[0:1, :],
                                                  0.0, ALU.mult, ALU.add, row[:, 5 * N:5 * N + 1]))
                    stt(row_w, row_v, row[:, 5 * N:5 * N + 1], row_p, ALU.mult, ALU.add).then_inc(rows_in, 1)
                    dve.wait_ge(update_out, k + 1)
                    link(tt(mat[:, 0:2 * N], mat[:, 0:2 * N], ps[0:N, 1024:1024 + 2 * N], ALU.subtract))

                link(tt(big[0][:, :], A, eye, ALU.mult))
                link(tt(big[1][:, :], A, T["sub"], ALU.mult))
                link(tt(big[2][:, :], A, T["sup"], ALU.mult))
                link(dve.tensor_reduce(c(0), big[0][:, :], AX, ALU.add))
                link(dve.tensor_reduce(c(1), big[1][:, :], AX, ALU.add))
                link(dve.tensor_reduce(c(3), big[2][:, :], AX, ALU.add))
                link(stt(c(2), c(1), -1.0, c(1), ALU.mult, ALU.max))
                link(stt(c(3), c(3), -1.0, c(3), ALU.mult, ALU.max))
                link(tt(c(0), c(0), c(2), ALU.subtract))
                link(tt(c(0), c(0), c(3), ALU.subtract))
                link(ts(c(4), c(1), 0.0, None, ALU.is_ge))
                link(ts(c(4), c(4), 2.0, -1.0, ALU.mult, ALU.add))
                link(tt(heads[:, :], T["headcol"], c(2).broadcast_to([N, LEVELS]), ALU.mult))
                ts(low[:, 0:N], eye, c(4), None, ALU.mult).then_inc(turn_in, 1)
                dve.wait_ge(turn_out, 2)
                link(dve.tensor_copy(sgn_row[:, :], ps[0:N, 0:N]))
                link(dve.tensor_copy(rhos[:, :], ps[0:N, 512:512 + LEVELS]))
                link(tt(pick[:, :, :], T["head"].rearrange("p (l n) -> p l n", n=N),
                        sgn_row[:, None, :].broadcast_to([N, LEVELS, N]), ALU.mult))
                link(tt(pick[:, :, :], T["last"].rearrange("p (l n) -> p l n", n=N), pick[:, :, :], ALU.add))
                link(dve.tensor_copy(vt[:, :], eye))

                d, rho, z, abs_z, abs_d, nd, w, zr, mass = (c(i) for i in (0, 8, 28, 29, 30, 31, 32, 33, 34))
                largest, tol, gap, top, ntop, total, hi, half, value = (c(i) for i in range(35, 44))
                neg, right, start, both, shift, mu, own, s0, s1 = (c(i) for i in range(44, 53))
                num, den, z_next, close, keep, square, root, sq2, len2 = (c(i) for i in range(53, 62))
                same, off, part, off1, pad, wts, rest, tmp, fac, inv, new, z_row, origin, tmp2 = (
                    b[:, :] for b in big[0:14])
                with ch.loop(LEVELS, LEVEL_STEPS + 9 * NEWTON) as l:
                    go(tt(W4[:, 0:N], eye, d.broadcast_to([N, N]), ALU.mult))
                    go(stt(abs_d, d, -1.0, d, ALU.mult, ALU.max))
                    go(dve.tensor_copy(rho, rhos[:, bass.ds(l, 1)]))
                    go(dve.tensor_copy(same, T["same"][:, bass.ds(l * N, N)]))
                    link(tt(tmp, pick[:, bass.ds(l, 1), :], vt[:, :], ALU.mult))
                    link(dve.tensor_reduce(z, tmp, AX, ALU.add))
                    link(stt(abs_z, z, -1.0, z, ALU.mult, ALU.max))
                    link(stt(mass, abs_z, 1.0 / ROOT2, abs_d, ALU.mult, ALU.max))
                    ts(W4[:, N:2 * N], eye, mass, None, ALU.mult).then_inc(turn_in, 1)
                    go(tt(zr, abs_z, rho, ALU.mult))
                    link(tt(w, z, z, ALU.mult))
                    link(tt(w, w, rho, ALU.mult))
                    dve.wait_ge(turn_out, l * 4 + 3)
                    go(ts(off, ps[0:N, 512:512 + N], d, None, ALU.subtract))
                    link(dve.tensor_tensor_reduce(tmp2, ps[0:N, 512 + N:512 + 2 * N], same, 1.0, 0.0,
                                                  ALU.mult, ALU.max, largest))
                    link(ts(nd, zr, ROOT2 * 2.0 ** 21, largest, ALU.mult, ALU.is_gt))
                    go(ts(W4[:, N:2 * N], eye, z, nd, ALU.mult, ALU.mult))
                    go(ts(W4[:, 2 * N:3 * N], eye, nd, None, ALU.mult))
                    link(ts(W4[:, 3 * N:4 * N], eye, w, nd, ALU.mult, ALU.mult))
                    tt(z, z, nd, ALU.mult).then_inc(turn_in, 1)
                    go(stt(tmp, off, -1.0, off, ALU.mult, ALU.max))
                    link(tt(tmp2, T["tie"], off, ALU.subtract))
                    link(stt(tmp, tmp, TIE, tmp2, ALU.is_lt, ALU.mult))
                    link(tt(off, off, tmp, ALU.add))
                    dve.wait_ge(turn_out, l * 4 + 4)
                    link(tt(part, ps[0:N, 1024 + N:1024 + 2 * N], same, ALU.mult))
                    go(dve.tensor_tensor_reduce(wts, ps[0:N, 1024 + 2 * N:1024 + 3 * N], same, 1.0, 0.0,
                                                ALU.mult, ALU.add, total))
                    go(ts(pad, part, -4.0, 4.0, ALU.mult, ALU.add))
                    go(dve.tensor_copy(z_row, ps[0:N, 1024:1024 + N]))
                    link(tt(off1, off, part, ALU.mult))
                    go(tt(off, off1, pad, ALU.add))
                    link(ts(tmp, off1, 0.0, BIG, ALU.is_le, ALU.mult))
                    go(ts(tol, largest, 8 * 2.0 ** -24, None, ALU.mult))
                    link(dve.tensor_tensor_reduce(tmp2, off1, tmp, 1.0, BIG, ALU.add, ALU.min, gap))
                    go(ts(ntop, gap, BIG / 2, None, ALU.is_le))
                    link(ts(top, gap, BIG / 2, None, ALU.is_gt))
                    link(tt(total, total, top, ALU.mult))
                    link(stt(hi, gap, ntop, total, ALU.mult, ALU.add))
                    link(ts(half, hi, 0.5, None, ALU.mult))
                    link(ts(tmp, off, half, None, ALU.subtract))
                    link(dve.reciprocal(tmp2, tmp))
                    link(dve.tensor_tensor_reduce(tmp, tmp2, wts, 1.0, 0.0, ALU.mult, ALU.add, value))
                    link(ts(neg, value, -1.0, None, ALU.is_lt))
                    go(tt(both, neg, top, ALU.mult))
                    link(tt(right, neg, ntop, ALU.mult))
                    go(tt(shift, right, hi, ALU.mult))
                    link(stt(start, right, -2.0, both, ALU.mult, ALU.add))
                    go(stt(mu, start, 1.0, half, ALU.add, ALU.mult))
                    link(ts(origin, off, shift, None, ALU.subtract))
                    link(stt(tmp, origin, 0.0, part, ALU.is_equal, ALU.mult))
                    link(dve.tensor_tensor_reduce(tmp2, wts, tmp, 1.0, 0.0, ALU.mult, ALU.add, own))
                    link(tt(rest, wts, tmp2, ALU.subtract))
                    with ch.loop(NEWTON, 9) as _:
                        link(ts(tmp, origin, mu, None, ALU.subtract))
                        link(dve.reciprocal(tmp2, tmp))
                        link(stt(fac, tmp2, 1.0, rest, ALU.mult, ALU.mult, accum_out=s0))
                        link(stt(tmp, fac, 1.0, tmp2, ALU.mult, ALU.mult, accum_out=s1))
                        link(tt(s1, s1, mu, ALU.mult))
                        go(stt(num, s1, mu, own, ALU.mult, ALU.add))
                        link(stt(den, s0, 1.0, s1, ALU.add, ALU.add))
                        link(dve.reciprocal(den, den))
                        link(tt(mu, num, den, ALU.mult))
                    link(ts(mu, mu, -BIG, BIG, ALU.max, ALU.min))
                    link(ts(tmp, origin, mu, None, ALU.subtract))
                    go(tt(rest, T["not_eye"], off, ALU.mult))
                    link(ts(tmp2, tmp, 0.0, 1e-20, ALU.is_equal, ALU.mult))
                    go(ts(part, part, nd, None, ALU.mult))
                    link(tt(rest, rest, eye, ALU.subtract))
                    link(tt(tmp, tmp, tmp2, ALU.add))
                    go(dve.reciprocal(inv, tmp))
                    go(ts(tmp2, part, -1.0, 1.0, ALU.mult, ALU.add))
                    link(dve.reciprocal(wts, rest))
                    link(tt(fac, wts, tmp, ALU.mult))
                    link(tt(fac, fac, part, ALU.mult))
                    tt(fac, fac, tmp2, ALU.add).then_inc(turn_in, 1)
                    go(ts(keep, nd, -1.0, 1.0, ALU.mult, ALU.add))
                    link(ts(wts, off, gap, None, ALU.is_equal))
                    go(ts(rest, eye, keep, None, ALU.mult))
                    link(dve.tensor_tensor_reduce(off1, wts, z_row, 1.0, 0.0, ALU.mult, ALU.add, z_next))
                    go(tt(close, z_next, z, ALU.mult))
                    link(tt(s0, z_next, z_next, ALU.mult))
                    go(ts(keep, close, 0.0, -2.0, ALU.is_gt, ALU.mult))
                    go(tt(close, close, hi, ALU.mult))
                    link(stt(s0, z, z, s0, ALU.mult, ALU.add))
                    go(tt(keep, keep, ntop, ALU.mult))
                    link(tt(s0, s0, tol, ALU.mult))
                    link(tt(close, close, s0, ALU.is_le))
                    go(tt(keep, keep, nd, ALU.mult))
                    go(ts(sq2, z, 0.0, 2.0, ALU.is_ge, ALU.mult))
                    link(tt(s1, shift, mu, ALU.add))
                    go(ts(sq2, sq2, -1.0, None, ALU.add))
                    go(tt(s1, s1, nd, ALU.mult))
                    link(tt(keep, keep, close, ALU.mult))
                    go(tt(d, d, s1, ALU.add))
                    link(ts(keep, keep, 1.0, None, ALU.add))
                    dve.wait_ge(turn_out, l * 4 + 5)
                    link(dve.tensor_reduce(square, ps[0:N, 0:N], AX, ALU.mult))
                    link(stt(square, square, -1.0, square, ALU.mult, ALU.max))
                    ts(square, square, 1e-30, None, ALU.max).then_inc(sq2_in, 1)
                    link(tt(tmp, ps[0:N, 512:512 + N], part, ALU.mult))
                    dve.wait_ge(sq2_out, l * 2 + 1)
                    link(tt(sq2, sq2, root, ALU.mult))
                    stt(new, tmp, sq2, rest, ALU.mult, ALU.add).then_inc(turn_in, 1)
                    dve.wait_ge(turn_out, l * 4 + 6)
                    link(dve.tensor_copy(vt[:, :], ps[0:N, 1024:1024 + N]))
                    dve.tensor_tensor_reduce(tmp, vt[:, :], vt[:, :], 1.0, 0.0, ALU.mult, ALU.add, square)\
                        .then_inc(sq2_in, 1)
                    dve.wait_ge(sq2_out, l * 2 + 2)
                    link(dve.reciprocal(len2, root))
                    link(ts(vt[:, :], vt[:, :], len2, keep, ALU.mult, ALU.mult))

                dve.tensor_copy(dup[:, 0:N], mat[:, N:2 * N]).then_inc(turn_in, 1)
                dve.wait_ge(turn_out, 4 * LEVELS + 3)
                link(dve.tensor_copy(big[0][:, :], ps[0:N, 0:N]))
                link(dve.tensor_copy(dup[:, N:2 * N], mat[:, N:2 * N]))
                link(dve.tensor_copy(dup[:, P:P + N], big[0][:, :]))
                dve.tensor_copy(dup[:, P + N:2 * P], big[0][:, :]).then_inc(turn_in, 1)
                dve.wait_ge(turn_out, 4 * LEVELS + 4)
                for h in range(2):
                    q = slice(h * N, (h + 1) * N)
                    link(dve.tensor_copy(m.bd_u[q, q], ps[q, 512:512 + N]))
                    link(dve.tensor_copy(m.bd_ut[q, q], ps[q, 1024:1024 + N]))
        sem.clear()


G = 4
GROUPS = 16
TILES = G * GROUPS
ROWS = TILES * P
GR = G * P
EPS = 1e-5


def inverse_root(nc, link, inv, root, square, corr):
    link(nc.vector.reciprocal(inv, root))
    link(nc.vector.tensor_tensor(corr, inv, inv, ALU.mult))
    link(nc.vector.tensor_tensor(corr, corr, square, ALU.mult))
    link(nc.vector.tensor_scalar(corr, corr, -0.5, 1.5, ALU.mult, ALU.add))
    link(nc.vector.tensor_tensor(inv, inv, corr, ALU.mult))


def row_statistics(nc, ch, m, stat, first_tile, tiles):
    ch.eng.sem_inc(ch.entries, 1)
    for t in range(tiles):
        nc.vector.bn_stats(stat[:, t, 0:6], m.X[:, bass.ds(first_tile + t, 1), :]).then_inc(ch.sem, 1)
    ch.n += tiles
    ch.eng.wait_ge(ch.sem, ch.turns + ch.n)
    ch.eng.sem_inc(ch.entries, 1)
    for t in range(tiles):
        nc.vector.bn_aggr(stat[:, t, 6:8], stat[:, t, 0:6]).then_inc(ch.sem, 1)
    ch.n += tiles
    ch.eng.wait_ge(ch.sem, ch.turns + ch.n)
    ch.link(nc.vector.tensor_copy(m.mv[:, bass.ds(first_tile, tiles), :], stat[:, 0:tiles, 6:8]))


def layer_norm(nc, m, tag, out=None):
    with ExitStack() as ctx:
        sb, sem = scope(nc, ctx)
        var, root, inv, corr, shift = (sb(f"{tag}_{k}", [P, TILES]) for k in ("var", "root", "inv", "corr", "shift"))
        step, turns = sem(f"{tag}_step"), sem(f"{tag}_turns")
        var_in, root_out, scales_out = sem(f"{tag}_var_in"), sem(f"{tag}_root_out"), sem(f"{tag}_scales_out")
        even_done, odd_done, stored = sem(f"{tag}_even_done"), sem(f"{tag}_odd_done"), sem(f"{tag}_stored")
        with nc.Block() as block:

            @block.vector
            def _(dve):
                link = Chain(dve, step, turns).link
                nc.vector.tensor_scalar(var[:, :], m.mv[:, :, 1], EPS, None, ALU.add).then_inc(var_in, 1)
                dve.wait_ge(root_out, 1)
                inverse_root(nc, link, inv[:, :], root[:, :], var[:, :], corr[:, :])
                nc.vector.scalar_tensor_tensor(shift[:, :], m.mv[:, :, 0], -1.0, inv[:, :], ALU.mult, ALU.mult)\
                    .then_inc(scales_out, 1)
                with dve.Fori(0, TILES // 2) as i:
                    x = m.X[:, bass.ds(i * 2, 1), :]
                    nc.vector.tensor_scalar(x, x, m.mv[:, bass.ds(i * 2, 1), 0], inv[:, bass.ds(i * 2, 1)],
                                            ALU.subtract, ALU.mult).then_inc(even_done, 1)

            @block.scalar
            def _(act):
                act.wait_ge(var_in, 1)
                nc.scalar.activation(root[:, :], var[:, :], ACT.Sqrt).then_inc(root_out, 1)
                act.wait_ge(scales_out, 1)
                with act.Fori(0, TILES // 2) as i:
                    x = m.X[:, bass.ds(i * 2 + 1, 1), :]
                    nc.scalar.activation(x, x, ACT.Identity, bias=shift[:, bass.ds(i * 2 + 1, 1)],
                                         scale=inv[:, bass.ds(i * 2 + 1, 1)]).then_inc(odd_done, 1)

            if out is not None:
                @block.sync
                def _(sp):
                    view = out.rearrange("(t p) d -> p t d", p=P)
                    with sp.Fori(0, TILES // 8) as i:
                        sp.wait_ge(even_done, i * 4 + 4)
                        sp.wait_ge(odd_done, i * 4 + 4)
                        sp.dma_start(view[:, bass.ds(i * 8, 8), :], m.X[:, bass.ds(i * 8, 8), :]).then_inc(stored, 16)
                    sp.wait_ge(stored, 16 * (TILES // 8))
        sem.clear()


def load_rows(m, io, pool):
    rows = io["x"].rearrange("(t p) d -> p t d", p=P)
    for q in range(4):
        pool.dma_start(m.X[:, q * 16:(q + 1) * 16, :], rows[:, q * 16:(q + 1) * 16, :]).then_inc(m.x_in, 16)


def load_weights(m, io, sp):
    for k, v in m.weights.items():
        sp.dma_start(v, io[k]).then_inc(m.weights_in, 16)


HALVES_TOP = 2.0 ** 14
SPLITS = 3


class WeightSplit:

    WIDTH = 8 * D
    SLICE = SPLITS * 2 * WIDTH // GROUPS

    def __init__(self, nc, m, io, sb, sem):
        self.nc, self.m, self.io = nc, m, io
        self.raw = sb("split_raw", [P, self.WIDTH])
        self.halves = sb("split_halves", [P, 2, self.WIDTH], F16)
        self.extreme = sb("split_extreme", [P, 2, GROUPS])
        self.largest = sb("split_largest", [P, 2])
        self.every = sb("split_every", [P, P])
        self.raw_in, self.raw_used, self.halves_in, self.stored = (
            sem(f"split_{k}") for k in ("raw_in", "raw_used", "halves_in", "stored"))
        self.largest_in, self.bounced, self.every_in, self.scale_in, self.step = (
            sem(f"split_{k}") for k in ("largest_in", "bounced", "every_in", "scale_in", "step"))

    def slot(self, s):
        return self.raw[:, s * self.SLICE:(s + 1) * self.SLICE]

    def loads_and_stores(self, sp):
        weights = self.io["l3_split"]
        for n in range(GROUPS):
            if n:
                sp.wait_ge(self.raw_in, n * 16)
            if n > 1:
                sp.wait_ge(self.raw_used, n - 1)
            sp.dma_start(self.slot(n % 2), weights[:, n * self.SLICE:(n + 1) * self.SLICE]).then_inc(self.raw_in, 16)
        sp.wait_ge(self.largest_in, 1)
        sp.dma_start(self.io["largest"], self.largest[:, 0:1]).then_inc(self.bounced, 16)
        sp.wait_ge(self.bounced, 16)
        sp.dma_start(self.every[:, :], self.io["largest"].rearrange("q a -> (q a)").partition_broadcast(P))\
            .then_inc(self.every_in, 16)
        sp.wait_ge(self.raw_in, GROUPS * 16)
        for n in range(SPLITS * 2):
            sp.wait_ge(self.raw_used, GROUPS + n)
            sp.dma_start(self.raw[:, :], weights[:, n * self.WIDTH:(n + 1) * self.WIDTH]).then_inc(self.raw_in, 16)
            sp.wait_ge(self.halves_in, n + 1)
            sp.dma_start(self.io["split"][n], self.halves[:, :, :]).then_inc(self.stored, 16)
            sp.wait_ge(self.stored, 16 * (n + 1))

    def slice_extremes(self, dve, n, s, carrier):
        dve.wait_ge(self.raw_in, (n + 1) * 16)
        dve.sem_inc(carrier, 1)
        dve.tensor_reduce(self.extreme[:, 0, bass.ds(n, 1)], self.slot(s), AX, ALU.max)
        dve.tensor_reduce(self.extreme[:, 1, bass.ds(n, 1)], self.slot(s), AX, ALU.min).then_inc(self.raw_used, 1)

    def send_largest(self, dve, link):
        dve.wait_ge(self.raw_used, GROUPS)
        link(dve.tensor_reduce(self.largest[:, 0:1], self.extreme[:, 0, :], AX, ALU.max))
        link(dve.tensor_reduce(self.largest[:, 1:2], self.extreme[:, 1, :], AX, ALU.min))
        dve.scalar_tensor_tensor(self.largest[:, 0:1], self.largest[:, 1:2], -1.0, self.largest[:, 0:1], ALU.mult, ALU.max)\
            .then_inc(self.largest_in, 1)

    def find_scale(self, dve, link):
        dve.wait_ge(self.every_in, 16)
        link(dve.tensor_reduce(self.largest[:, 1:2], self.every[:, :], AX, ALU.max))
        link(dve.tensor_scalar(self.largest[:, 1:2], self.largest[:, 1:2], 1e-30, 1.0 / HALVES_TOP, ALU.max, ALU.mult))
        dve.reciprocal(self.m.split_scale[:, :], self.largest[:, 1:2]).then_inc(self.scale_in, 1)

    def split(self, pool):
        pool.wait_ge(self.scale_in, 1)
        for n in range(SPLITS * 2):
            pool.wait_ge(self.raw_in, 16 * (GROUPS + n + 1))
            if n:
                pool.wait_ge(self.stored, 16 * n)
            raw, high, low = self.raw[:, :], self.halves[:, 0, :], self.halves[:, 1, :]
            pool.tensor_scalar(raw, raw, self.m.split_scale[:, 0:1], None, ALU.mult).then_inc(self.step, 1)
            pool.wait_ge(self.step, n * 2 + 1)
            pool.tensor_copy(high, raw).then_inc(self.step, 1)
            pool.wait_ge(self.step, n * 2 + 2)
            pool.tensor_tensor(low, raw, high, ALU.subtract).then_inc(self.halves_in, 1)
            pool.wait_ge(self.halves_in, n + 1)
            pool.sem_inc(self.raw_used, 1)


def two_products(nc, m, tag, first):
    ps, w = m.ps, m.weights
    heads = 1 if first else 2
    mix_a = m.bd_u if first else m.bd_adj
    w1, w2 = (w["l0_w1"], w["l0_w2"]) if first else (w["l3_w0"], w["l3_w1"])
    b2 = w["l0_b2"] if first else w["l3_b1"]
    A_PS, B_PS, C_PS, D_PS = (ps[:, k * 1024:(k + 1) * 1024] for k in range(4))

    def chunked(bank):
        return bank.rearrange("p (c r) -> p c r", c=2)

    with ExitStack() as ctx:
        sb, sem = scope(nc, ctx)
        xs = sb(f"{tag}_xs", [P, G, D])
        agg = sb(f"{tag}_agg", [P, 2, GR])
        pre = sb(f"{tag}_pre", [P, 2, GR])
        hid = sb(f"{tag}_hid", [P, heads, GR])
        mid = sb(f"{tag}_mid", [P, G, D])
        stat = sb(f"{tag}_stat", [P, G, 8])
        sums = sb(f"{tag}_sums", [P, P])
        ones = sb(f"{tag}_ones", [P, P])
        xs_in, a_out, agg_in, b_out, pre_in, hid_in, c_out, mid_in, d_out, d_used = (
            sem(f"{tag}_{k}") for k in ("xs_in", "a_out", "agg_in", "b_out", "pre_in", "hid_in", "c_out", "mid_in",
                                        "d_out", "d_used"))
        ones_in, sums_out, sums_in = sem(f"{tag}_ones_in"), sem(f"{tag}_sums_out"), sem(f"{tag}_sums_in")
        step, turns = sem(f"{tag}_step"), sem(f"{tag}_turns")
        with nc.Block() as block:

            @block.gpsimd
            def _(pool):
                pool.wait_ge(m.x_in, 64)
                pool.tensor_copy(xs[:, :, :], m.X[:, 0:G, :]).then_inc(xs_in, 1)
                with pool.Fori(1, GROUPS) as i:
                    pool.wait_ge(a_out, i)
                    pool.tensor_copy(xs[:, :, :], m.X[:, bass.ds(i * G, G), :]).then_inc(xs_in, 1)

            @block.tensor
            def _(pe):
                pe.wait_ge(m.weights_in, m.weights_total)
                if not first:
                    pe.wait_ge(ones_in, 1)
                    pe.matmul(D_PS[:, 0:P], ones[:, :], m.bd_adj[:, :], start=True, stop=True).then_inc(sums_out, 1)
                    pe.wait_ge(sums_in, 1)

                def mix_in(i):
                    pe.wait_ge(xs_in, i + 1)
                    for c in range(2):
                        for t in range(G):
                            mm = pe.matmul(A_PS[:, c * GR + t * P:c * GR + (t + 1) * P],
                                           xs[:, t, c * P:(c + 1) * P], mix_a[:, :], start=True, stop=True)
                    mm.then_inc(a_out, 1)

                def weights_1(i):
                    pe.wait_ge(agg_in, i + 1)
                    for h in range(heads):
                        for k in range(2):
                            mm = pe.matmul(B_PS[:, h * GR:(h + 1) * GR], w1[:, k, h * P:(h + 1) * P], agg[:, k, :],
                                           start=k == 0, stop=k == 1)
                    mm.then_inc(b_out, 1)

                def weights_2(i):
                    pe.wait_ge(hid_in, i + 1)
                    for t in range(G):
                        for k in range(heads):
                            mm = pe.matmul(C_PS[:, t * D:(t + 1) * D], hid[:, k, t * P:(t + 1) * P], w2[:, k, :],
                                           start=k == 0, stop=k == heads - 1)
                    mm.then_inc(c_out, 1)

                def mix_out(i):
                    pe.wait_ge(mid_in, i + 1)
                    pe.wait_ge(d_used, i + 1)
                    if first:
                        for h in range(2):
                            mm = pe.matmul(D_PS[:, h * GR:(h + 1) * GR], m.bd_ut[:, :], mid[:, 2 * h:2 * h + 2, :],
                                           start=True, stop=True)
                    else:
                        for c in range(2):
                            for t in range(G):
                                mm = pe.matmul(D_PS[:, c * GR + t * P:c * GR + (t + 1) * P],
                                               mid[:, t, c * P:(c + 1) * P], m.bd_adj[:, :], start=True, stop=True)
                    mm.then_inc(d_out, 1)

                mix_in(0)
                weights_1(0)
                with pe.Fori(1, GROUPS) as i:
                    mix_in(i)
                    weights_2(i - 1)
                    weights_1(i)
                    mix_out(i - 1)
                weights_2(GROUPS - 1)
                mix_out(GROUPS - 1)

            @block.scalar
            def _(act):
                act.wait_ge(m.weights_in, m.weights_total)
                if not first:
                    act.sem_inc(d_used, 1)

                def copy_agg(i):
                    act.wait_ge(a_out, i + 1)
                    nc.scalar.copy(agg[:, :, :], chunked(A_PS)).then_inc(agg_in, 1)

                def relu(i):
                    if first:
                        act.wait_ge(b_out, i + 1)
                        nc.scalar.activation(hid[:, 0, :], B_PS[:, 0:GR], ACT.Relu, bias=w["l0_b1"][:, 0:1])\
                            .then_inc(hid_in, 1)
                    else:
                        act.wait_ge(pre_in, i + 1)
                        nc.scalar.activation(hid[:, :, :], pre[:, :, :], ACT.Relu).then_inc(hid_in, 1)

                def result(i):
                    act.wait_ge(d_out, i + 1)
                    nc.scalar.activation(m.T[:, :, bass.ds(i * GR, GR)], chunked(D_PS), ACT.Relu).then_inc(d_used, 1)

                copy_agg(0)
                relu(0)
                with act.Fori(1, GROUPS) as i:
                    copy_agg(i)
                    relu(i)
                    if not first:
                        result(i - 1)
                if not first:
                    result(GROUPS - 1)
                    act.wait_ge(d_used, GROUPS + 1)

            @block.vector
            def _(dve):
                ch = Chain(dve, step, turns)
                if first:
                    dve.sem_inc(d_used, 1)
                else:
                    nc.vector.memset(ones[:, :], 1.0).then_inc(ones_in, 1)
                    dve.wait_ge(sums_out, 1)
                    nc.vector.tensor_copy(sums[:, :], D_PS[:, 0:P]).then_inc(sums_in, 1)
                    dve.wait_ge(sums_in, 1)
                dve.wait_ge(m.weights_in, m.weights_total)

                def bias_1(i):
                    dve.wait_ge(b_out, i + 1)
                    for h in range(2):
                        ins = nc.vector.scalar_tensor_tensor(
                            pre[:, h, :].rearrange("p (t r) -> p t r", t=G), sums[:, None, :].broadcast_to([P, G, P]),
                            w["l3_b0"][:, h:h + 1], B_PS[:, h * GR:(h + 1) * GR].rearrange("p (t r) -> p t r", t=G),
                            ALU.mult, ALU.add)
                    ins.then_inc(pre_in, 1)

                def bias_2(i):
                    dve.wait_ge(c_out, i + 1)
                    nc.vector.tensor_tensor(mid[:, :, :], C_PS.rearrange("p (t d) -> p t d", t=G),
                                            b2[:, None, :].broadcast_to([P, G, D]), ALU.add).then_inc(mid_in, 1)

                def residual(i):
                    dve.wait_ge(d_out, i + 1)
                    x = m.X[:, bass.ds(i * G, G), :]
                    nc.vector.tensor_tensor(x, D_PS.rearrange("p (t d) -> p t d", t=G), x, ALU.add)\
                        .then_inc(d_used, 1)
                    dve.wait_ge(d_used, i + 2)
                    row_statistics(nc, ch, m, stat, i * G, G)

                if not first:
                    bias_1(0)
                with ch.loop(GROUPS - 1, 2 * G + 1 if first else 0, start=1) as i:
                    bias_2(i - 1)
                    if first:
                        residual(i - 1)
                    else:
                        bias_1(i)
                bias_2(GROUPS - 1)
                if first:
                    residual(GROUPS - 1)
        sem.clear()


def batch_normed(nc, m, io):
    ps, w, T = m.ps, m.weights, m.T
    HC = 4
    A_PS, C_PS = ps[:, 0:1024], ps[:, 0:1024]
    B_PS = ps[:, 1024:1024 + HC * GR]
    O_PS = [ps[:, 0:1024], ps[:, 1024:2048]]
    with ExitStack() as ctx:
        sb, sem = scope(nc, ctx)
        xs = sb("l1_xs", [P, G, D])
        hid = sb("l1_hid", [P, HC, GR])
        nrm = [sb(f"l1_nrm{s}", [P, 2, GR]) for s in range(2)]
        hstat = sb("l1_hstat", [P, HC, GROUPS, 6])
        ostat = sb("l1_ostat", [P, 2, GROUPS, 6])
        stat = sb("l1_stat", [P, G, 8])
        moments = sb("l1_moments", [P, HC + 2, 2])
        var, root, inv, corr, scale, mean, shift = (sb(f"l1_{k}", [P, HC + 2]) for k in
                                                    ("var", "root", "inv", "corr", "scale", "mean", "shift"))
        xs_in, a_out, agg_in, b_out, stats_in = (sem(f"l1_{k}") for k in ("xs_in", "a_out", "agg_in", "b_out",
                                                                          "stats_in"))
        b2_out, hid_in, c_out, out_in = (sem(f"l1_{k}") for k in ("b2_out", "hid_in", "c_out", "out_in"))
        nrm_in, turned, added = (sem(f"l1_{k}") for k in ("nrm_in", "turned", "added"))
        var_in, root_out, scales_in, ostat_in = (sem(f"l1_{k}") for k in ("var_in", "root_out", "scales_in",
                                                                          "ostat_in"))
        step, turns = sem("l1_step"), sem("l1_turns")
        split = WeightSplit(nc, m, io, sb, sem)
        with nc.Block() as block:

            @block.gpsimd
            def _(pool):
                pool.tensor_copy(xs[:, :, :], m.X[:, 0:G, :]).then_inc(xs_in, 1)
                with pool.Fori(1, GROUPS) as i:
                    pool.wait_ge(a_out, i)
                    pool.tensor_copy(xs[:, :, :], m.X[:, bass.ds(i * G, G), :]).then_inc(xs_in, 1)
                split.split(pool)

            @block.sync
            def _(sp):
                split.loads_and_stores(sp)

            @block.tensor
            def _(pe):
                def mix(i):
                    pe.wait_ge(xs_in, i + 1)
                    for c in range(2):
                        for t in range(G):
                            mm = pe.matmul(A_PS[:, c * GR + t * P:c * GR + (t + 1) * P],
                                           xs[:, t, c * P:(c + 1) * P], m.bd_hat[:, :], start=True, stop=True)
                    mm.then_inc(a_out, 1)

                def hidden(i, done):
                    for h in range(HC):
                        if done is b_out:
                            pe.wait_ge(stats_in, i * HC + h + 1)
                        for k in range(2):
                            mm = pe.matmul(B_PS[:, h * GR:(h + 1) * GR], w["l1_w1"][:, k, h * P:(h + 1) * P],
                                           T[:, k, bass.ds(i * GR, GR)], start=k == 0, stop=k == 1)
                        mm.then_inc(done, 1)

                mix(0)
                with pe.Fori(1, GROUPS) as i:
                    pe.wait_ge(agg_in, i)
                    mix(i)
                    hidden(i - 1, b_out)
                pe.wait_ge(agg_in, GROUPS)
                hidden(GROUPS - 1, b_out)

                def output(i):
                    for k in range(HC):
                        if k == 0:
                            pe.wait_ge(out_in, i + 1)
                        for h in range(2):
                            pe.wait_ge(hid_in, i * HC + k + 1)
                            mm = pe.matmul(C_PS[:, h * GR:(h + 1) * GR], w["l1_w2"][:, k, h * P:(h + 1) * P],
                                           hid[:, k, :], start=k == 0, stop=k == HC - 1)
                    mm.then_inc(c_out, 1)

                pe.wait_ge(stats_in, GROUPS * HC + HC)
                hidden(0, b2_out)
                with pe.Fori(1, GROUPS) as i:
                    output(i - 1)
                    hidden(i, b2_out)
                output(GROUPS - 1)

                pe.wait_ge(out_in, GROUPS + 1)
                with pe.Fori(0, GROUPS // 2) as i:
                    for s in range(2):
                        pe.wait_ge(nrm_in, i * 2 + s + 1)
                        pe.wait_ge(added, i * 2 + s + 1)
                        for t in range(G):
                            for c in range(2):
                                mm = pe.transpose(O_PS[s][:, t * D + c * P:t * D + (c + 1) * P],
                                                  nrm[s][:, c, t * P:(t + 1) * P], w["eye"])
                        mm.then_inc(turned, 1)

            @block.scalar
            def _(act):
                with act.Fori(0, GROUPS) as i:
                    act.wait_ge(a_out, i + 1)
                    nc.scalar.copy(T[:, :, bass.ds(i * GR, GR)], A_PS.rearrange("p (c r) -> p c r", c=2))\
                        .then_inc(agg_in, 1)
                act.wait_ge(var_in, 1)
                nc.scalar.activation(root[:, 0:HC], var[:, 0:HC], ACT.Sqrt).then_inc(root_out, 1)
                act.wait_ge(scales_in, 1)
                with act.Fori(0, GROUPS) as i:
                    for h in range(HC):
                        act.wait_ge(b2_out, i * HC + h + 1)
                        nc.scalar.activation(hid[:, h, :], B_PS[:, h * GR:(h + 1) * GR], ACT.Relu,
                                             bias=shift[:, h:h + 1], scale=scale[:, h:h + 1]).then_inc(hid_in, 1)
                act.wait_ge(var_in, 2)
                nc.scalar.activation(root[:, HC:], var[:, HC:], ACT.Sqrt).then_inc(root_out, 1)
                act.wait_ge(scales_in, 2)

                def norm_out(i, s):
                    for c in range(2):
                        ins = nc.scalar.activation(nrm[s][:, c, :], T[:, c, bass.ds(i * GR, GR)], ACT.Identity,
                                                   bias=shift[:, HC + c:HC + c + 1], scale=scale[:, HC + c:HC + c + 1])
                    ins.then_inc(nrm_in, 1)

                norm_out(0, 0)
                norm_out(1, 1)
                with act.Fori(1, GROUPS // 2) as i:
                    for s in range(2):
                        act.wait_ge(turned, i * 2 + s - 1)
                        norm_out(i * 2 + s, s)

            @block.vector
            def _(dve):
                ch = Chain(dve, step, turns)
                link = ch.link
                tt, ts, stt = nc.vector.tensor_tensor, nc.vector.tensor_scalar, nc.vector.scalar_tensor_tensor
                dve.wait_ge(m.weights_in, m.weights_total)
                dve.sem_inc(stats_in, HC)
                with dve.Fori(0, GROUPS // 2) as i2:
                    for s in range(2):
                        i = i2 * 2 + s
                        for h in range(HC):
                            dve.wait_ge(b_out, i * HC + h + 1)
                            dve.sem_inc(turns, 1)
                            nc.vector.bn_stats(hstat[:, h, bass.ds(i, 1), :], B_PS[:, h * GR:(h + 1) * GR])\
                                .then_inc(stats_in, 1)
                        split.slice_extremes(dve, i, s, turns)
                dve.wait_ge(stats_in, GROUPS * HC + HC)

                def scales(a, b, stats):
                    for h in range(a, b):
                        link(nc.vector.bn_aggr(moments[:, h, :], stats[:, h - a, :, :]))
                    q = slice(a, b)
                    ts(var[:, q], moments[:, q, 1], EPS, None, ALU.add).then_inc(var_in, 1)
                    dve.wait_ge(root_out, 1 if a == 0 else 2)
                    inverse_root(nc, link, inv[:, q], root[:, q], var[:, q], corr[:, q])
                    link(tt(scale[:, q], inv[:, q], w["l1_g"][:, q], ALU.mult))
                    link(tt(mean[:, q], moments[:, q, 0], w["l1_b"][:, q], ALU.add))
                    link(tt(shift[:, q], w["l1_b"][:, q], mean[:, q], ALU.subtract))
                    link(tt(shift[:, q], shift[:, q], scale[:, q], ALU.mult))
                    tt(shift[:, q], shift[:, q], w["l1_be"][:, q], ALU.add).then_inc(scales_in, 1)

                split.send_largest(dve, link)
                scales(0, HC, hstat)
                split.find_scale(dve, link)
                dve.sem_inc(out_in, 1)
                with dve.Fori(0, GROUPS) as i:
                    dve.wait_ge(c_out, i + 1)
                    dve.sem_inc(turns, 1)
                    for h in range(2):
                        nc.vector.bn_stats(ostat[:, h, bass.ds(i, 1), :], C_PS[:, h * GR:(h + 1) * GR])\
                            .then_inc(ostat_in, 1)
                    nc.vector.tensor_copy(T[:, :, bass.ds(i * GR, GR)], C_PS.rearrange("p (c r) -> p c r", c=2))\
                        .then_inc(out_in, 1)
                dve.wait_ge(ostat_in, GROUPS * 2)
                scales(HC, HC + 2, ostat)
                dve.sem_inc(added, 2)
                with ch.loop(GROUPS // 2, 2 * (2 * G + 1)) as i:
                    for s in range(2):
                        dve.wait_ge(turned, i * 2 + s + 1)
                        x = m.X[:, bass.ds(i * (2 * G) + s * G, G), :]
                        tt(x, O_PS[s].rearrange("p (t d) -> p t d", t=G), x, ALU.add).then_inc(added, 1)
                        dve.wait_ge(added, i * 2 + s + 3)
                        row_statistics(nc, ch, m, stat, i * (2 * G) + s * G, G)
        sem.clear()


HEADS = 4
EDGES = 512
EC = EDGES // P
BLOCKS = 4
BT = TILES // BLOCKS
NODES = 8
CHUNKS = N // NODES


def graph_attention(nc, m, io):
    ps, w = m.ps, m.weights

    def bank(k, n=1):
        return ps[:, k * 512:(k + n) * 512]

    with ExitStack() as ctx:
        sb, sem = scope(nc, ctx)
        ends_i = sb("ends_i", [P, 2, EC], I32)
        rows_i = sb("rows_i", [P, 2, EDGES], I32)
        ends = sb("ends", [P, 2, EC])
        rows = sb("rows", [P, 2, EDGES])
        at_node = sb("at_node", [P, 2, EC, N])
        pairs = sb("pairs", [P, EC, N * N], BF16)
        gather = sb("gather", [P, 2, EDGES], BF16)
        log_a = sb("log_a", [P, N * N])
        ones = sb("l2_ones", [P, P], BF16)
        per_edge = sb("per_edge", [P, EC])
        xs, xt = sb("l2_xs", [P, D]), sb("l2_xt", [P, 2, P])
        xq, xq_rest = sb("l2_xq", [P, 3, D], BF16), sb("l2_xq_rest", [P, D])
        leaky = [sb(f"leaky{j}", [P, EDGES]) for j in range(4)]
        value = sb("value", [P, BT, D])
        attn = sb("attn", [P, BT, HEADS, N])
        score, rest = (leaky[j][:, :].rearrange("p (e r) -> p e r", e=EC) for j in range(2))
        times = attn[:, :, :, :].rearrange("p t h n -> p (t h n)")
        part = [sb(f"part{j}", [P, EC, P], BF16) for j in range(3)]
        soft = [sb("soft0", [P, NODES, N])] + [leaky[j][:, :].rearrange("p (n m) -> p n m", m=N) for j in (2, 3)]
        tops, dens = sb("top", [P, 2, NODES]), sb("den", [P, 2, NODES])
        vs = [leaky[2][:, s * D:(s + 1) * D] for s in range(2)]
        ws = [leaky[s][:, :].rearrange("p (h b n) -> p h b n", h=HEADS, b=2) for s in range(2)]
        yt = [sb(f"yt{s}", [P, 2, P]) for s in range(2)]
        stat = sb("l2_stat", [P, 1, 8])
        of_batch = sb("of_batch", [P, 2])
        edges_in, adj_in, log_in, ones_in, pairs_in, count_out, count_in, adj_eps, made = (
            sem(f"l2_{k}") for k in ("edges_in", "adj_in", "log_in", "ones_in", "pairs_in", "count_out", "count_in", "adj_eps",
                                     "made"))
        xs_in, turned, xt_in, q_out, v_out, xq_in, v_in, ws_in, gather_out, sum_in, leaky_in, score_out = (
            sem(f"l2_{k}") for k in ("xs_in", "turned", "xt_in", "q_out", "v_out", "xq_in", "v_in", "ws_in", "gather_out", "sum_in", "leaky_in",
                                     "score_out"))
        parts_in, dense_out, dense_in, less_max, exp_in, attn_in, turned2, w_in = (
            sem(f"l2_{k}") for k in ("parts_in", "dense_out", "dense_in", "less_max", "exp_in",
                                     "attn_in", "turned2", "w_in"))
        staged, y_out, yt_in, o_out, added = (sem(f"l2_{k}") for k in ("staged", "y_out", "yt_in", "o_out", "added"))
        w_kept = sem("l2_w_kept")
        step, turns, pe_turns, pool_turns = (sem(f"l2_{k}") for k in ("step", "turns", "pe_turns", "pool_turns"))
        with nc.Block() as block:

            @block.sync
            def _(sp):
                sp.dma_start(ends_i[:, :, :], io["edge_ends"]).then_inc(edges_in, 16)
                sp.dma_start(rows_i[:, :, :], io["edge_rows"]).then_inc(edges_in, 16)
                sp.dma_start(log_a[:, :], io["adj_row"].broadcast_to([P, N * N])).then_inc(adj_in, 16)

            @block.gpsimd
            def _(pool):
                with pool.Fori(0, BLOCKS) as q:
                    with pool.Fori(0, BT) as t:
                        pool.wait_ge(turned, q * BT + t + 1)
                        pool.tensor_copy(xs[:, :], m.X[:, bass.ds(q * BT + t, 1), :]).then_inc(xs_in, 1)
                    pool.wait_ge(w_kept, (q + 1) * CHUNKS + 2)
                    pool.sem_inc(pool_turns, 1)
                    with pool.Fori(0, BT // 2) as i:
                        for s in range(2):
                            pool.wait_ge(y_out, q * BT + i * 2 + s + 1)
                            pool.tensor_copy(vs[s], value[:, bass.ds(i * 2 + s, 1), :]).then_inc(staged, 1)

            @block.tensor
            def _(pe):
                pe.sem_inc(turned, 1)
                pe.sem_inc(y_out, 2)
                pe.wait_ge(pairs_in, EC)
                pe.wait_ge(ones_in, 1)
                for k in range(CHUNKS):
                    for e in range(EC):
                        mm = pe.matmul(bank(k), ones[:, :], pairs[:, e, k * 512:(k + 1) * 512],
                                       start=e == 0, stop=e == EC - 1)
                mm.then_inc(count_out, 1)
                pe.wait_ge(made, 1)

                with pe.Fori(0, BLOCKS) as q:
                    def turn(t):
                        u = q * BT + t
                        pe.wait_ge(xs_in, u + 1)
                        pe.wait_ge(v_in, u + 1)
                        for c in range(2):
                            mm = pe.transpose(bank(0)[:, c * P:(c + 1) * P], xs[:, c * P:(c + 1) * P], w["eye"])
                        mm.then_inc(turned, 1)

                    def queries_values(t):
                        pe.wait_ge(xt_in, q * BT + t + 1)
                        for j in range(2):
                            for c in range(2):
                                mm = pe.matmul(bank(1 - j)[:, j * D:(j + 1) * D], xt[:, c, :],
                                               w["l2_wqv"][:, c, j * D:(j + 1) * D], start=c == 0, stop=c == 1)
                            mm.then_inc(v_out if j else q_out, 1)

                    def gathers(t):
                        pe.wait_ge(xq_in, q * BT + t + 1)
                        for b in range(2):
                            for c in range(2):
                                for j in range(3):
                                    mm = pe.matmul(bank(2 + 2 * b + c), xq[:, j, c * P:(c + 1) * P], gather[:, b, :],
                                                   start=j == 0, stop=j == 2)
                                mm.then_inc(gather_out, 1)

                    def scores(t):
                        pe.wait_ge(leaky_in, (q * BT + t + 1) * 4)
                        for b in range(2):
                            for c in range(2):
                                for e in range(EC):
                                    at = t * (2 * HEADS) + e * 2 * P + b * HEADS + c * 2
                                    mm = pe.matmul(bank(6, 2)[:, bass.ds(at, P)], leaky[2 * b + c][:, e * P:(e + 1) * P],
                                                   w["l2_a"][:, c, :], start=True, stop=True)
                        mm.then_inc(score_out, 1)

                    turn(0)
                    pe.wait_ge(added, q * BT + 2)
                    queries_values(0)
                    turn(1)
                    gathers(0)
                    with pe.Fori(1, BT - 1) as t:
                        queries_values(t)
                        scores(t - 1)
                        turn(t + 1)
                        gathers(t)
                    queries_values(BT - 1)
                    scores(BT - 2)
                    gathers(BT - 1)
                    scores(BT - 1)

                    def dense(k):
                        pe.wait_ge(dense_in, q * CHUNKS + k + 1)
                        for j in range(3):
                            for e in range(EC):
                                mm = pe.matmul(bank(k % 2), part[j][:, e, :], pairs[:, e, k * 512:(k + 1) * 512],
                                               start=j + e == 0, stop=j == 2 and e == EC - 1)
                        mm.then_inc(dense_out, 1)

                    def turn_weights(k):
                        v = q * CHUNKS + k
                        pe.wait_ge(w_kept, v + 1)
                        pe.wait_ge(attn_in, v + 1)
                        pe.sem_inc(pe_turns, 1)
                        for n in range(NODES // 2):
                            mm = pe.transpose(bank(2 + k % 2)[:, n * P:(n + 1) * P],
                                              soft[k % 3][:, 2 * n:2 * n + 2, :].rearrange("p n m -> p (n m)"), w["eye"])
                        mm.then_inc(turned2, 1)

                    pe.wait_ge(v_in, (q + 1) * BT + 1)
                    pe.wait_ge(parts_in, q + 1)
                    dense(0)
                    dense(1)
                    for k in range(CHUNKS):
                        if k + 2 < CHUNKS:
                            dense(k + 2)
                        turn_weights(k)

                    def sums(t, s):
                        u = q * BT + t
                        pe.wait_ge(yt_in, u * 2 + 2)
                        pe.wait_ge(ws_in, u * 2 + 2)
                        pe.wait_ge(staged, u + 1)
                        for c in range(2):
                            for h in range(2 * c, 2 * c + 2):
                                mm = pe.matmul(bank(2 * s)[:, h * P:(h + 1) * P], vs[s][:, c * P:(c + 1) * P],
                                               ws[s][:, h, :, :], start=True, stop=True)
                        mm.then_inc(y_out, 1)

                    def output(t, s):
                        u = q * BT + t
                        pe.wait_ge(added, u + 1)
                        pe.wait_ge(yt_in, u * 2 + 6)
                        for c in range(2):
                            mm = pe.matmul(bank(2 * s + 1)[:, 0:D], yt[s][:, c, :], w["l2_wo"][:, c, :],
                                           start=c == 0, stop=c == 1)
                        mm.then_inc(o_out, 1)

                    sums(0, 0)
                    with pe.Fori(0, BT // 2 - 1) as i:
                        sums(i * 2 + 1, 1)
                        output(i * 2, 0)
                        sums(i * 2 + 2, 0)
                        output(i * 2 + 1, 1)
                    sums(BT - 1, 1)
                    output(BT - 2, 0)
                    output(BT - 1, 1)

            @block.scalar
            def _(act):
                act.sem_inc(v_in, 1)
                act.sem_inc(yt_in, 4)
                act.sem_inc(w_kept, 2)
                act.wait_ge(adj_eps, 1)
                nc.scalar.activation(log_a[:, :], log_a[:, :], ACT.Ln)
                act.wait_ge(count_in, 1)
                pair_count = value[:, :, :].rearrange("p t d -> p (t d)")
                nc.scalar.activation(pair_count, pair_count, ACT.Ln).then_inc(log_in, 1)
                with act.Fori(0, BLOCKS) as q:
                    def keep_turned_x(t):
                        act.wait_ge(turned, q * BT + t + 2)
                        nc.scalar.copy(xt[:, :, :], bank(0)[:, 0:D].rearrange("p (c r) -> p c r", c=2)).then_inc(xt_in, 1)

                    def keep_values(t):
                        act.wait_ge(v_out, q * BT + t + 1)
                        nc.scalar.copy(value[:, bass.ds(t, 1), :], bank(0)[:, None, D:2 * D]).then_inc(v_in, 1)

                    def keep_sums(t):
                        for j in range(4):
                            act.wait_ge(gather_out, (q * BT + t) * 4 + j + 1)
                            nc.scalar.copy(leaky[j][:, :], bank(2 + j)).then_inc(sum_in, 1)

                    keep_turned_x(0)
                    with act.Fori(0, BT - 1) as t:
                        keep_values(t)
                        keep_turned_x(t + 1)
                        keep_sums(t)
                    keep_values(BT - 1)
                    keep_sums(BT - 1)

                    def exponential(k):
                        act.wait_ge(less_max, q * CHUNKS + k + 1)
                        nc.scalar.activation(soft[k % 3][:, :, :], soft[k % 3][:, :, :], ACT.Exp).then_inc(exp_in, 1)

                    def keep(k):
                        act.wait_ge(turned2, q * CHUNKS + k + 3)
                        for odd in range(2):
                            src = bank(2 + k % 2)[odd * N:(odd + 1) * N, :]\
                                .rearrange("m (n t b h) -> m b t h n", t=BT, b=2, h=HEADS)
                            for b in range(2):
                                at = slice(k * NODES + odd, (k + 1) * NODES, 2)
                                nc.scalar.copy(attn[b * N:(b + 1) * N, :, :, at], src[:, b]).then_inc(w_in, 1)
                        act.wait_ge(w_in, (q * CHUNKS + k + 1) * 4)
                        act.sem_inc(w_kept, 1)

                    exponential(0)
                    for k in range(CHUNKS):
                        if k + 1 < CHUNKS:
                            exponential(k + 1)
                        keep(k)

                    def stage_weights(t, s):
                        act.wait_ge(y_out, q * BT + t + 1)
                        for b in range(2):
                            nc.scalar.activation(ws[s][:, :, b, :], attn[:, bass.ds(t, 1), :, :], ACT.Copy,
                                                 scale=of_batch[:, b:b + 1]).then_inc(ws_in, 1)

                    def keep_sums_turned(t, s):
                        act.wait_ge(y_out, q * BT + t + 3)
                        for h in range(2):
                            half = slice(h * N, (h + 1) * N)
                            src = bank(2 * s)[half, :].rearrange("p (c h r) -> p c h r", c=2, h=2)
                            nc.scalar.copy(yt[s][half, :, :], src[:, :, h, :]).then_inc(yt_in, 1)

                    stage_weights(0, 0)
                    with act.Fori(0, BT // 2 - 1) as i:
                        stage_weights(i * 2 + 1, 1)
                        keep_sums_turned(i * 2, 0)
                        stage_weights(i * 2 + 2, 0)
                        keep_sums_turned(i * 2 + 1, 1)
                    stage_weights(BT - 1, 1)
                    keep_sums_turned(BT - 2, 0)
                    keep_sums_turned(BT - 1, 1)

            @block.vector
            def _(dve):
                ch = Chain(dve, step, turns)
                link = ch.link
                tt, ts, stt = nc.vector.tensor_tensor, nc.vector.tensor_scalar, nc.vector.scalar_tensor_tensor
                dve.sem_inc(dense_in, 2)
                dve.sem_inc(turned2, 2)
                dve.sem_inc(added, 2)
                nc.vector.memset(ones[:, :], 1.0).then_inc(ones_in, 1)
                dve.wait_ge(edges_in, 32)
                link(nc.vector.tensor_copy(ends[:, :, :], ends_i[:, :, :]))
                link(nc.vector.tensor_copy(rows[:, :, :], rows_i[:, :, :]))
                for s in range(2):
                    for e in range(EC):
                        link(ts(at_node[:, s, e, :], w["l2_nodes"], ends[:, s, e:e + 1], None, ALU.is_equal))
                for e in range(EC):
                    tt(pairs[:, e, :].rearrange("p (n m) -> p n m", m=N),
                       at_node[:, 0, e, :, None].broadcast_to([P, N, N]),
                       at_node[:, 1, e, None, :].broadcast_to([P, N, N]), ALU.mult).then_inc(pairs_in, 1)
                link(ts(of_batch[:, :], w["l2_node"], 0.0, None, ALU.is_ge))
                for b in range(2):
                    node = w["l2_node"][:, b:b + 1]
                    link(ts(leaky[0][:, :], rows[:, 0, :], node, None, ALU.is_equal))
                    link(stt(gather[:, b, :], rows[:, 1, :], node, leaky[0][:, :], ALU.is_equal, ALU.add))
                for e in range(EC):
                    link(ts(leaky[0][:, :], rows[:, 0, :], ends[:, 0, e:e + 1], None, ALU.is_equal))
                    link(stt(leaky[1][:, :], rows[:, 1, :], ends[:, 1, e:e + 1], leaky[0][:, :],
                             ALU.is_equal, ALU.mult))
                    link(nc.vector.tensor_reduce(per_edge[:, e:e + 1], leaky[1][:, :], AX, ALU.add))
                link(nc.vector.reciprocal(per_edge[:, :], per_edge[:, :]))
                dve.wait_ge(adj_in, 16)
                ts(log_a[:, :], log_a[:, :], 1e-8, None, ALU.add).then_inc(adj_eps, 1)
                dve.wait_ge(count_out, 1)
                pair_count = value[:, :, :].rearrange("p t d -> p (t d)")
                link(nc.vector.tensor_copy(times, ps[:, :]))
                ts(pair_count, times, 1.0, None, ALU.max).then_inc(count_in, 1)
                dve.wait_ge(log_in, 1)
                link(tt(log_a[:, :], log_a[:, :], pair_count, ALU.add))
                link(ts(times, times, 0.0, -BIG, ALU.is_equal, ALU.mult))
                tt(log_a[:, :], log_a[:, :], times, ALU.add).then_inc(made, 1)
                dve.wait_ge(made, 1)

                soften, finish, tile_steps = 2, 3, 3
                query_steps = 4
                with ch.loop(BLOCKS, EC + 4 + CHUNKS * (soften + finish) + BT * (tile_steps + query_steps)) as q:
                    with ch.loop(BT, query_steps) as t:
                        dve.wait_ge(q_out, q * BT + t + 1)
                        link(nc.vector.tensor_copy(xq[:, 0, :], bank(1)[:, 0:D]))
                        link(tt(xq_rest[:, :], bank(1)[:, 0:D], xq[:, 0, :], ALU.subtract))
                        link(nc.vector.tensor_copy(xq[:, 1, :], xq_rest[:, :]))
                        link(tt(xq_rest[:, :], xq_rest[:, :], xq[:, 1, :], ALU.subtract))
                        nc.vector.tensor_copy(xq[:, 2, :], xq_rest[:, :]).then_inc(xq_in, 1)
                        for j in range(4):
                            dve.wait_ge(sum_in, (q * BT + t) * 4 + j + 1)
                            stt(leaky[j][:, :], leaky[j][:, :], 0.2, leaky[j][:, :], ALU.mult, ALU.max)\
                                .then_inc(leaky_in, 1)

                    dve.wait_ge(score_out, (q + 1) * BT)
                    dve.sem_inc(turns, 1)
                    for e in range(EC):
                        ts(score[:, e, :], bank(6, 2)[:, e * 2 * P:e * 2 * P + P], per_edge[:, e:e + 1], None, ALU.mult)\
                            .then_inc(step, 1)
                    ch.n += EC
                    dve.wait_ge(step, ch.turns + ch.n)
                    link(nc.vector.tensor_copy(part[0][:, :, :], score[:, :, :]))
                    link(tt(rest[:, :, :], score[:, :, :], part[0][:, :, :], ALU.subtract))
                    link(nc.vector.tensor_copy(part[1][:, :, :], rest[:, :, :]))
                    link(tt(score[:, :, :], rest[:, :, :], part[1][:, :, :], ALU.subtract))
                    nc.vector.tensor_copy(part[2][:, :, :], score[:, :, :]).then_inc(parts_in, 1)

                    def less_maximum(k):
                        v, x = q * CHUNKS + k, soft[k % 3][:, :, :]
                        top = tops[:, k % 2, :]
                        if k > 2:
                            dve.wait_ge(turned2, v)
                        dve.wait_ge(dense_out, v + 1)
                        tt(x, bank(k % 2).rearrange("p (n m) -> p n m", m=N),
                           log_a[:, k * 512:(k + 1) * 512].rearrange("p (n m) -> p n m", m=N), ALU.add)\
                            .then_inc(dense_in, 1)
                        dve.wait_ge(dense_in, v + 3)
                        link(nc.vector.tensor_reduce(top, x, AX, ALU.max))
                        link(ts(top, top, -BIG / 2, None, ALU.max))
                        tt(x, x, top[:, :, None].broadcast_to([P, NODES, N]), ALU.subtract).then_inc(less_max, 1)
                        dve.wait_ge(less_max, v + 1)

                    def normalise(k):
                        v, x = q * CHUNKS + k, soft[k % 3][:, :, :]
                        den = dens[:, k % 2, :]
                        dve.wait_ge(exp_in, v + 1)
                        link(nc.vector.tensor_reduce(den, x, AX, ALU.add))
                        link(ts(den, den, 1e-30, None, ALU.max))
                        link(nc.vector.reciprocal(den, den))
                        tt(x, x, den[:, :, None].broadcast_to([P, NODES, N]), ALU.mult).then_inc(attn_in, 1)

                    less_maximum(0)
                    for k in range(CHUNKS):
                        if k + 1 < CHUNKS:
                            less_maximum(k + 1)
                        normalise(k)

                    with ch.loop(BT // 2, 2 * tile_steps) as i:
                        for s in range(2):
                            u = q * BT + i * 2 + s
                            dve.wait_ge(o_out, u + 1)
                            x = m.X[:, bass.ds(u, 1), :]
                            tt(x, bank(2 * s + 1)[:, None, 0:D], x, ALU.add).then_inc(added, 1)
                            dve.wait_ge(added, u + 3)
                            row_statistics(nc, ch, m, stat, u, 1)
        sem.clear()


SKIPS = 4
GATE_ORDER = (0, 2, 1, 3)


def window_batches(p):
    nb = P
    while nb * (N // p) > 512 or P % nb:
        nb -= 1
    return nb


def skip_lstms(nc, m, io):
    ps, T = m.ps, m.T
    with ExitStack() as ctx:
        sb, sem = scope(nc, ctx)
        wx = [sb(f"wx{s}", [P, 8 * D]) for s in range(2)]
        wh = sb("wh", [P, 8 * D])
        scale = sb("lstm_scale", [P, 2])
        bias2 = sb("lstm_bias2", [P, 2, SKIPS * 8])
        bias = sb("lstm_bias", [P, SKIPS * 8])
        gate = [[sb(f"gate{s}{g}", [P, 512]) for g in range(4)] for s in range(2)]
        cell = sb("cell", [P, 2, 512])
        tanh_c = [gate[c][0] for c in range(2)]
        state = [sb(f"state{s}", [P, 2, 2, 512], F16) for s in range(2)]
        bias_in, bias_sum = sem("lstm_bias_in"), sem("lstm_bias_sum")
        wx_in, wh_in = sem("wx_in"), sem("wh_in")
        gates_out, gates_in, gates_free = sem("lstm_gates_out"), sem("lstm_gates_in"), sem("lstm_gates_free")
        cell_in, tanh_in, state_in, kept = sem("cell_in"), sem("tanh_in"), sem("state_in"), sem("state_kept")
        state_in_primed, pool_turns = sem("state_in_primed"), sem("lstm_pool_turns")
        step, turns = sem("lstm_step"), sem("lstm_turns")

        def split_weights(tile):
            return tile[:, :].bitcast(F16).rearrange("p (s k m) -> p s k m", s=2, k=2)

        def split_rows():
            return T[:, :, :].bitcast(F16).rearrange("p k (b s n) -> p k b s n", s=2, n=N)

        parts = ((0, 0), (0, 1), (1, 0))

        def shape(p):
            nb = window_batches(p)
            nw = N // p
            return nb, nw, nb * nw, P // nb

        units, gates, groups = [0], [0], [0]
        for p in range(1, SKIPS + 1):
            n = shape(p)[3]
            groups.append(groups[-1] + n)
            units.append(units[-1] + n * 2 * p)
            gates.append(gates[-1] + n * (8 * p - 2))

        def alternate(p):
            return 1 + p % 2

        def each_unit(p):
            u = g = 0
            for t in range(p):
                for c in range(2):
                    order = [q for q in GATE_ORDER if t or q != 1]
                    yield t, c, order, u, g
                    u += 1
                    g += len(order)

        with nc.Block() as block:

            @block.sync
            def _(sp):
                sp.dma_start(bias2[:, 0, :], io["l3_bih"]).then_inc(bias_in, 16)
                sp.dma_start(bias2[:, 1, :], io["l3_bhh"]).then_inc(bias_in, 16)
                for p in range(1, SKIPS + 1):
                    if p > 2:
                        sp.wait_ge(gates_out, gates[p - 2])
                    source = io["l3_wx1"] if p == 1 else io["split"][(p - 2) * 2]
                    target = wx[1][:, :].rearrange("p (k m) -> p k m", k=2) if p == 1 else \
                        wx[p % 2][:, :].bitcast(F16).rearrange("p (s m) -> p s m", s=2)
                    sp.dma_start(target, source).then_inc(wx_in, 16)
                    sp.wait_ge(wx_in, 16 * p)
                    if p > 1:
                        if p > 2:
                            sp.wait_ge(gates_out, gates[p - 1])
                        sp.dma_start(wh[:, :].bitcast(F16).rearrange("p (s m) -> p s m", s=2), io["split"][(p - 2) * 2 + 1])\
                            .then_inc(wh_in, 16)

            @block.tensor
            def _(pe):
                for p in range(1, SKIPS + 1):
                    nb, nw, C, n = shape(p)
                    pe.wait_ge(wx_in, 16 * p)
                    if p == 1:
                        rows = T[:, :, :].rearrange("p k (b n) -> p k b n", n=N)
                        w_x = wx[1][:, :].rearrange("p (k m) -> p k m", k=2)
                    else:
                        rows, w_x, w_h = split_rows(), split_weights(wx[p % 2]), split_weights(wh)

                    def gate_bank(c, q):
                        return ps[:, (c * 4 + q) * 512:(c * 4 + q) * 512 + C]

                    def from_rows(i, t, c, order):
                        nodes = slice(t, t + (nw - 1) * p + 1, p)
                        for q in order:
                            bank, col = gate_bank(c, q).rearrange("p (b w) -> p b w", w=nw), q * D + c * P
                            for k in range(2):
                                for a, b in parts if p > 1 else parts[:1]:
                                    x = rows[:, k, bass.ds(i * nb, nb), b, nodes] if p > 1 else \
                                        rows[:, k, bass.ds(i * nb, nb), nodes]
                                    weight = w_x[:, a, k, col:col + P] if p > 1 else w_x[:, k, col:col + P]
                                    mm = pe.matmul(bank, weight, x, start=k == 0 and a + b == 0,
                                                   stop=t == 0 and k == 1 and (p == 1 or a == 1))
                            if t == 0:
                                mm.then_inc(gates_out, 1)

                    def from_state(t, c, order, last):
                        for q in order:
                            col = q * D + c * P
                            for k in range(2):
                                for a, b in parts:
                                    mm = pe.matmul(gate_bank(c, q), w_h[:, a, k, col:col + P],
                                                   state[last][:, b, k, 0:C], start=False, stop=k == 1 and a == 1)
                            mm.then_inc(gates_out, 1)

                    with pe.Fori(0, n // alternate(p)) as turn:
                        for s in range(alternate(p)):
                            i = turn * alternate(p) + s
                            if p > 1:
                                pe.wait_ge(kept, groups[p - 2] + (i + 1) * (nb // window_batches(p - 1)) + 2)
                            for t, c, order, u, g in each_unit(p):
                                pe.wait_ge(gates_free, units[p - 1] + i * (2 * p) + u + 1)
                                from_rows(i, t, c, order)
                                if t and c:
                                    if t == 1:
                                        pe.wait_ge(wh_in, 16 * (p - 1))
                                    pe.wait_ge(state_in, units[p - 1] + i * (2 * p) + 2 * t)
                                    for half in range(2):
                                        from_state(t, half, order, (t - 1 + s) % 2)

            @block.scalar
            def _(act):
                act.sem_inc(gates_free, 2)
                act.wait_ge(bias_sum, 1)
                for p in range(1, SKIPS + 1):
                    nb, nw, C, n = shape(p)
                    with act.Fori(0, n) as i:
                        for t, c, order, u, g in each_unit(p):
                            unit = units[p - 1] + i * (2 * p) + u
                            act.wait_ge(state_in_primed, unit + 1)
                            for j, q in enumerate(order):
                                act.wait_ge(gates_out, gates[p - 1] + i * (8 * p - 2) + g + j + 1)
                                ins = nc.scalar.activation(
                                    gate[c][q][:, 0:C], ps[:, (c * 4 + q) * 512:(c * 4 + q) * 512 + C],
                                    ACT.Tanh if q == 2 else ACT.Sigmoid,
                                    bias=bias[:, (p - 1) * 8 + q * 2 + c:(p - 1) * 8 + q * 2 + c + 1],
                                    scale=scale[:, min(p, 2) - 1:min(p, 2)])
                                ins.then_inc(gates_in, 1)
                            act.wait_ge(gates_in, gates[p - 1] + i * (8 * p - 2) + g + len(order))
                            act.sem_inc(gates_free, 1)
                            act.wait_ge(cell_in, unit + 1)
                            nc.scalar.activation(tanh_c[c][:, 0:C], cell[:, c, 0:C], ACT.Tanh).then_inc(tanh_in, 1)

            @block.vector
            def _(dve):
                tt = nc.vector.tensor_tensor
                dve.wait_ge(bias_in, 32)
                dve.sem_inc(state_in_primed, 2)
                ch = Chain(dve, step, turns)
                ch.link(nc.vector.memset(scale[:, :], 1.0))
                ch.link(nc.vector.tensor_scalar(scale[:, 1:2], m.split_scale[:, :], HALVES_TOP, None, ALU.mult))
                ch.link(nc.vector.reciprocal(scale[:, 1:2], scale[:, 1:2]))
                tt(bias[:, :], bias2[:, 0, :], bias2[:, 1, :], ALU.add).then_inc(bias_sum, 1)
                for p in range(1, SKIPS + 1):
                    nb, nw, C, n = shape(p)
                    with ch.loop(n // alternate(p), (4 * (p - 1) + 4 * p) * alternate(p)) as turn:
                        for s, (t, c, order, u, g) in [(s, x) for s in range(alternate(p)) for x in each_unit(p)]:
                            i = turn * alternate(p) + s
                            gi, gf, gg, go = (gate[c][q][:, 0:C] for q in range(4))
                            unit, at = units[p - 1] + i * (2 * p) + u, gates[p - 1] + i * (8 * p - 2) + g
                            dve.wait_ge(gates_in, at + 2)
                            if t == 0:
                                tt(cell[:, c, 0:C], gi, gg, ALU.mult).then_inc(cell_in, 1)
                            else:
                                tt(gi, gi, gg, ALU.mult).then_inc(step, 1)
                                dve.wait_ge(gates_in, at + 3)
                                tt(gf, gf, cell[:, c, 0:C], ALU.mult).then_inc(step, 1)
                                ch.n += 2
                                dve.wait_ge(step, ch.turns + ch.n)
                                tt(cell[:, c, 0:C], gi, gf, ALU.add).then_inc(cell_in, 1)
                            if t < 2 and c == 0:
                                dve.wait_ge(kept, groups[p - 1] + i + t + 1)
                            dve.wait_ge(tanh_in, unit + 1)
                            h, high, low = tanh_c[c][:, 0:C], *(state[(t + s) % 2][:, a, c, 0:C] for a in range(2))
                            ch.link(nc.vector.scalar_tensor_tensor(h, go, HALVES_TOP, h, ALU.mult, ALU.mult))
                            ch.link(nc.vector.tensor_copy(high, h))
                            tt(low, h, high, ALU.subtract).then_inc(state_in, 1)
                            dve.wait_ge(state_in, unit + 1)
                            dve.sem_inc(state_in_primed, 1)

            @block.gpsimd
            def _(pool):
                pool.sem_inc(kept, 2)
                for p in range(1, SKIPS + 1):
                    nb, nw, C, n = shape(p)
                    def keep(i, slot):
                        pool.wait_ge(state_in, units[p - 1] + (i + 1) * (2 * p))
                        pool.sem_inc(pool_turns, 1)
                        rows = split_rows()
                        for k in range(2):
                            for s in range(2):
                                ins = pool.tensor_copy(
                                    rows[:, k, bass.ds(i * nb, nb), s, p - 1:p - 1 + (nw - 1) * p + 1:p],
                                    state[(p - 1 + slot) % 2][:, s, k, 0:C].rearrange("p (b w) -> p b w", w=nw))
                        ins.then_inc(kept, 1)

                    with pool.Fori(0, n // alternate(p)) as turn:
                        for slot in range(alternate(p)):
                            keep(turn * alternate(p) + slot, slot)
                pool.wait_ge(kept, groups[SKIPS] + 2)
        sem.clear()


def turn_and_add(nc, m):
    ps, T = m.ps, m.T
    O_PS = [ps[:, 0:1024], ps[:, 1024:2048]]
    with ExitStack() as ctx:
        sb, sem = scope(nc, ctx)
        fixed = [sb(f"turn_fixed{s}", [P, 2, GR]) for s in range(2)]
        stat = sb("turn_stat", [P, G, 8])
        fixed_in, turned, added, step, turns, pool_turns = (
            sem(f"turn_{k}") for k in ("fixed_in", "turned", "added", "step", "turns", "pool_turns"))
        with nc.Block() as block:

            @block.gpsimd
            def _(pool):
                batches = GR // N
                halves = T[:, :, :].bitcast(F16).rearrange("p k (b s n) -> p k b s n", s=2, n=N)

                def join(i, s):
                    for k in range(2):
                        q = bass.ds(i * batches, batches)
                        pool.tensor_tensor(fixed[s][:, k, :].rearrange("p (b n) -> p b n", n=N), halves[:, k, q, 0, :],
                                           halves[:, k, q, 1, :], ALU.add).then_inc(fixed_in, 1)

                join(0, 0)
                join(1, 1)
                with pool.Fori(1, GROUPS // 2) as i:
                    for s in range(2):
                        pool.wait_ge(turned, i * 2 + s - 1)
                        pool.sem_inc(pool_turns, 1)
                        join(i * 2 + s, s)

            @block.tensor
            def _(pe):
                with pe.Fori(0, GROUPS // 2) as i:
                    for s in range(2):
                        pe.wait_ge(fixed_in, (i * 2 + s + 1) * 2)
                        pe.wait_ge(added, i * 2 + s + 1)
                        for t in range(G):
                            for c in range(2):
                                mm = pe.transpose(O_PS[s][:, t * D + c * P:t * D + (c + 1) * P],
                                                  fixed[s][:, c, t * P:(t + 1) * P], m.weights["eye"])
                        mm.then_inc(turned, 1)

            @block.vector
            def _(dve):
                ch = Chain(dve, step, turns)
                dve.sem_inc(added, 2)
                with ch.loop(GROUPS // 2, 2 * (2 * G + 1)) as i:
                    for s in range(2):
                        dve.wait_ge(turned, i * 2 + s + 1)
                        x = m.X[:, bass.ds(i * (2 * G) + s * G, G), :]
                        nc.vector.scalar_tensor_tensor(x, O_PS[s].rearrange("p (t d) -> p t d", t=G),
                                                       1.0 / HALVES_TOP, x, ALU.mult, ALU.add)\
                            .then_inc(added, 1)
                        dve.wait_ge(added, i * 2 + s + 3)
                        row_statistics(nc, ch, m, stat, i * (2 * G) + s * G, G)
        sem.clear()


def program(nc, io, out):
    with ExitStack() as ctx:
        m = Mem(nc, ctx)
        m.bd_u, m.bd_ut, m.bd_hat, m.bd_adj = (m.sb(k, [P, P]) for k in ("bd_u", "bd_ut", "bd_hat", "bd_adj"))
        m.root_deg2 = m.sb("root_deg2", [P, 1])
        m.X = m.sb("X", [P, TILES, D])
        m.mv = m.sb("mv", [P, TILES, 2])
        m.split_scale = m.sb("split_scale", [P, 1])
        m.weights = {}
        for k, shape in WEIGHTS.items():
            m.weights[k] = m.sb(k, [P] + shape)[(slice(None),) * (1 + len(shape))]
        m.weights_in, m.x_in = m.sem("weights_in"), m.sem("x_in")
        m.weights_total = 16 * len(m.weights)
        spectral_basis(nc, m, io)
        two_products(nc, m, "l0", True)
        layer_norm(nc, m, "n0")
        with ExitStack() as inner:
            m.T = inner.enter_context(nc.sbuf_tensor("T1", [P, 2, ROWS], F32))
            batch_normed(nc, m, io)
        layer_norm(nc, m, "n1")
        graph_attention(nc, m, io)
        layer_norm(nc, m, "n2")
        with ExitStack() as inner:
            m.T = inner.enter_context(nc.sbuf_tensor("T3", [P, 2, ROWS], F32))
            two_products(nc, m, "l3", False)
            skip_lstms(nc, m, io)
            turn_and_add(nc, m)
        layer_norm(nc, m, "n3", out)


WEIGHTS = dict(l0_w1=[2, P], l0_w2=[1, D], l0_b1=[1], l0_b2=[D], eye=[P],
               l1_w1=[2, 512], l1_w2=[4, D], l1_b=[6], l1_g=[6], l1_be=[6],
               l3_w0=[2, D], l3_w1=[2, D], l3_b0=[2], l3_b1=[D],
               l2_wqv=[2, 2 * D], l2_wo=[2, D], l2_a=[2, P], l2_nodes=[N], l2_node=[2])


def kernel(**inputs):
    import numpy as np
    import concourse.bacc as bacc
    from concourse.bass_utils import run_bass_kernel_spmd

    a = {k: np.asarray(v) for k, v in inputs.items()}

    def chunks(w):
        return w.reshape(-1, P, w.shape[-1]).transpose(1, 0, 2)

    def column(b):
        return b.reshape(-1, P).T

    def everywhere(b):
        return np.broadcast_to(b, (P,) + b.shape)

    head_vectors = np.zeros((P, 2, P), np.float32)
    for h in range(HEADS):
        head_vectors[h % 2 * N:(h % 2 + 1) * N, h // 2, h % 2] = a["L2_gnn_a"][h]

    given = dict(
        adj=a["adj"], adj_t=a["adj"].T, tables=constant_tables(), x=a["x"].reshape(ROWS, D),
        l0_w1=chunks(a["L0_gnn_W1"]), l0_w2=chunks(a["L0_gnn_W2"]), l0_b1=column(a["L0_gnn_b1"]),
        l0_b2=everywhere(a["L0_gnn_b2"]), eye=np.eye(P, dtype=np.float32),
        l1_w1=chunks(a["L1_gnn_W1"].T), l1_w2=chunks(a["L1_gnn_W2"].T),
        l3_w0=chunks(a["L3_gnn_Wg0"]), l3_w1=chunks(a["L3_gnn_Wg1"]), l3_b0=column(a["L3_gnn_bg0"]),
        l3_b1=everywhere(a["L3_gnn_bg1"]), l3_bih=column(a["L3_gnn_bih"]), l3_bhh=column(a["L3_gnn_bhh"]),
        l3_wx1=chunks(a["L3_gnn_Wih"][0].T),
        l3_split=np.concatenate([chunks(a[k][p].T).reshape(P, 8 * D) for p in range(1, 4)
                                 for k in ("L3_gnn_Wih", "L3_gnn_Whh")], 1),
        l2_wqv=np.concatenate([chunks(a["L2_gnn_W_lin"].T), chunks(a["L2_gnn_W_val"].T)], 2),
        l2_wo=chunks(a["L2_gnn_W_out"].T), l2_a=head_vectors, adj_row=a["adj"].reshape(1, N * N),
        l2_nodes=everywhere(np.arange(N, dtype=np.float32)),
        l2_node=np.stack([np.where(np.arange(P) // N == b, np.arange(P) % N, -1) for b in range(2)], 1)
        .astype(np.float32),
        edge_ends=np.stack([a[k].reshape(EC, P).T for k in ("L2_gnn_src", "L2_gnn_dst")], 1),
        edge_rows=everywhere(np.stack([a["L2_gnn_src"], a["L2_gnn_dst"]])),
        l1_b=column(np.concatenate([a["L1_gnn_b1"], a["L1_gnn_b2"]])),
        l1_g=column(np.concatenate([a["L1_gnn_g1"], a["L1_gnn_g2"]])),
        l1_be=column(np.concatenate([a["L1_gnn_be1"], a["L1_gnn_be2"]])),
    )
    nc = bacc.Bacc("TRN2", target_bir_lowering=False, num_devices=1)
    io, arrays = {}, {}
    for name, v in given.items():
        v = np.ascontiguousarray(v)
        arrays[f"in_{name}"] = v
        io[name] = nc.dram_tensor(f"in_{name}", v.shape, mybir.dt.from_np(v.dtype), kind="ExternalInput").ap()
    out = nc.dram_tensor("out", (ROWS, D), F32, kind="ExternalOutput").ap()
    io["split"] = nc.dram_tensor("split", (SPLITS * 2, P, 2, 8 * D), F16, kind="Internal").ap()
    io["largest"] = nc.dram_tensor("largest", (P, 1), F32, kind="Internal").ap()
    program(nc, io, out)
    r = run_bass_kernel_spmd(nc, [arrays], core_ids=[0])
    return r.results[0]["out"].reshape(a["x"].shape)
```
